# Optimizing a Trainium2 kernel written in Bass

```python
import numpy as np
import jax
import jax.numpy as jnp

def _softmax(x, axis=-1):
    return jax.nn.softmax(x, axis=axis)

def _gelu(x):
    return jax.nn.gelu(x, approximate=True)

def _silu(x):
    return jax.nn.silu(x)

def _sigmoid(x):
    return jax.nn.sigmoid(x)

def _layernorm(x, axis=-1, eps=1e-05):
    m = jnp.mean(x, axis=axis, keepdims=True)
    v = jnp.var(x, axis=axis, keepdims=True)
    return (x - m) / jnp.sqrt(v + eps)

def _scatter_add(tgt, idx, src, axis=0):
    return tgt.at[idx].add(src)

def _segment_sum(src, seg, n):
    return jax.ops.segment_sum(src, seg, n)
kernel_name = 'mk_prb_d2_jaxref_r8_e58cc0'

def setup_inputs(seed: int=0):
    np.random.seed(seed)
    _w = jnp.asarray

    def _L0_attn_setup():
        import jax, jax.numpy as jnp
        import numpy as np
        D = 128
        H = 16
        DH = D // H
        B, N = (4, 128)
        key = jax.random.key(seed)
        k0, k1, k2 = jax.random.split(key, 3)
        x = jax.random.normal(k0, (B, N, D), jnp.float32)
        Wkqv = jax.random.normal(k1, (H, D, 2 * D + DH), jnp.float32) * 0.02
        bkqv = jnp.zeros((H, 2 * D + DH), jnp.float32)
        Wp = jax.random.normal(k2, (D, D), jnp.float32) * 0.02
        bp = jnp.zeros((D,), jnp.float32)
        return {'x': x, 'Wkqv': Wkqv, 'bkqv': bkqv, 'Wp': Wp, 'bp': bp}
    _L0_attn_in = _L0_attn_setup()

    def _L0_ffn_setup():
        import jax, jax.numpy as jnp
        import numpy as np
        B, T, D, E, K = (4, 256, 128, 8, 2)
        key = jax.random.key(seed)
        k1, k2, k3 = jax.random.split(key, 3)
        x = jax.random.normal(k1, (B, T, D), dtype=jnp.float32)
        Wg = jax.random.normal(k2, (D, E), dtype=jnp.float32) * (1.0 / np.sqrt(D))
        lim = float(np.sqrt(6.0 / (D + D)))
        We = jax.random.uniform(k3, (E, D, D), dtype=jnp.float32, minval=-lim, maxval=lim)
        return {'x': x, 'Wg': Wg, 'We': We}
    _L0_ffn_in = _L0_ffn_setup()

    def _L1_attn_setup():
        import jax, jax.numpy as jnp
        import numpy as np
        from jax import lax
        B, L, D = (4, 256, 128)
        ED = 2 * D
        N = 16
        K = 15
        R = D // 16
        EPS = 1e-05

        def _silu(u):
            return u * jax.nn.sigmoid(u)

        def _mamba_block(x, gamma, beta, W_in, b_in, conv_w, conv_b, W_x, W_dt, b_dt, A_log, D_param, W_out, b_out):
            mu = jnp.mean(x, axis=-1, keepdims=True)
            var = jnp.var(x, axis=-1, keepdims=True)
            xn = (x - mu) * lax.rsqrt(var + EPS) * gamma + beta
            xz = jnp.einsum('bld,ed->ble', xn, W_in) + b_in
            xin, z = (xz[..., :ED], xz[..., ED:])
            xc = jnp.swapaxes(xin, 1, 2)
            xc = jnp.pad(xc, ((0, 0), (0, 0), (K - 1, 0)))
            xc = lax.conv_general_dilated(xc, conv_w[:, None, :], window_strides=(1,), padding='VALID', dimension_numbers=('NCH', 'OIH', 'NCH'), feature_group_count=ED)
            xc = xc + conv_b[None, :, None]
            xc = _silu(jnp.swapaxes(xc, 1, 2))
            xdbl = jnp.einsum('ble,re->blr', xc, W_x)
            dt_low = xdbl[..., :R]
            Bm = xdbl[..., R:R + N]
            Cm = xdbl[..., R + N:]
            delta = jax.nn.softplus(jnp.einsum('blr,er->ble', dt_low, W_dt) + b_dt)
            A = -jnp.exp(A_log)

            def step(h, inp):
                d_t, B_t, C_t, x_t = inp
                dA = jnp.exp(d_t[..., None] * A)
                dBx = d_t[..., None] * B_t[:, None, :] * x_t[..., None]
                h = h * dA + dBx
                y = jnp.sum(h * C_t[:, None, :], axis=-1)
                return (h, y)
            xs = (jnp.swapaxes(delta, 0, 1), jnp.swapaxes(Bm, 0, 1), jnp.swapaxes(Cm, 0, 1), jnp.swapaxes(xc, 0, 1))
            h0 = jnp.zeros((x.shape[0], ED, N), x.dtype)
            _, ys = lax.scan(step, h0, xs)
            y = jnp.swapaxes(ys, 0, 1) + xc * D_param
            y = y * _silu(z)
            out = jnp.einsum('ble,de->bld', y, W_out) + b_out
            return x + out
        key = jax.random.key(seed)
        ks = jax.random.split(key, 8)
        s = 0.02
        return {'x': jax.random.normal(ks[0], (B, L, D), jnp.float32), 'gamma': jnp.ones((D,), jnp.float32), 'beta': jnp.zeros((D,), jnp.float32), 'W_in': jax.random.normal(ks[1], (2 * ED, D), jnp.float32) * s, 'b_in': jnp.zeros((2 * ED,), jnp.float32), 'conv_w': jax.random.normal(ks[2], (ED, K), jnp.float32) * s, 'conv_b': jnp.zeros((ED,), jnp.float32), 'W_x': jax.random.normal(ks[3], (R + 2 * N, ED), jnp.float32) * s, 'W_dt': jax.random.normal(ks[4], (ED, R), jnp.float32) * s, 'b_dt': jax.random.normal(ks[5], (ED,), jnp.float32) * 0.1, 'A_log': jnp.broadcast_to(jnp.log(jnp.arange(1, N + 1, dtype=jnp.float32)), (ED, N)) + jnp.zeros((ED, N), jnp.float32), 'D_param': jnp.ones((ED,), jnp.float32), 'W_out': jax.random.normal(ks[6], (D, ED), jnp.float32) * s, 'b_out': jnp.zeros((D,), jnp.float32)}
    _L1_attn_in = _L1_attn_setup()

    def _L1_ffn_setup():
        import jax, jax.numpy as jnp
        import numpy as np
        DIM = 128
        DEPTH = 6
        HEADS = 16
        DIM_HEAD = 64
        WINDOW = 32
        INNER = HEADS * DIM_HEAD
        DIM_INNER = int(DIM * 4 * 2 / 3)
        QK_SCALE = 8.0

        def shift_tokens(t):
            a, s = jnp.split(t, 2, -1)
            s = jnp.pad(s, ((0, 0), (1, 0), (0, 0)))[:, :-1]
            return jnp.concatenate([a, s], -1)

        def l2norm(t):
            return t / jnp.maximum(jnp.linalg.norm(t, axis=-1, keepdims=True), 1e-12)

        def rotate_half(x):
            x1, x2 = jnp.split(x, 2, -1)
            return jnp.concatenate([-x2, x1], -1)

        def rotary_tables(n):
            half = jnp.arange(0, DIM_HEAD, 2, dtype=jnp.float32)
            inv_freq = 1.0 / 10000.0 ** (half / DIM_HEAD)
            t = jnp.arange(n, dtype=jnp.float32)
            freqs = t[:, None] * inv_freq[None, :]
            freqs = jnp.concatenate([freqs, freqs], -1)
            base_scale = (half + 0.4 * DIM_HEAD) / (1.4 * DIM_HEAD)
            power = (t - n // 2) / (WINDOW // 2)
            scale = base_scale[None, :] ** power[:, None]
            scale = jnp.concatenate([scale, scale], -1)
            return (freqs, scale)

        def local_attention(q, k, v):
            b, h, n, d = q.shape
            w = WINDOW
            nw = n // w
            bq = q.reshape(b, h, nw, w, d)
            bk = k.reshape(b, h, nw, w, d)
            bv = v.reshape(b, h, nw, w, d)

            def look(t):
                p = jnp.pad(t, ((0, 0), (0, 0), (1, 0), (0, 0), (0, 0)))
                return jnp.concatenate([p[:, :, :nw], p[:, :, 1:]], axis=3)
            bk2, bv2 = (look(bk), look(bv))
            seq = jnp.arange(n).reshape(nw, w)
            seq_p = jnp.pad(seq, ((1, 0), (0, 0)), constant_values=-1)
            jt = jnp.concatenate([seq_p[:nw], seq_p[1:]], axis=1)
            it = seq[:, :, None]
            jb = jt[:, None, :]
            mask = (it < jb) | (it > jb + w) | (jb == -1)
            sim = jnp.einsum('bhwie,bhwje->bhwij', bq, bk2) * QK_SCALE
            sim = jnp.where(mask, -jnp.finfo(sim.dtype).max, sim)
            attn = jax.nn.softmax(sim, -1)
            out = jnp.einsum('bhwij,bhwje->bhwie', attn, bv2)
            return out.reshape(b, h, n, d)

        def attn_layer(x, Wqkv, qs, ksc, Wo):
            b, n, _ = x.shape
            qkv = x @ Wqkv
            q, k, v = jnp.split(qkv, 3, -1)
            sh = lambda t: t.reshape(b, n, HEADS, DIM_HEAD).transpose(0, 2, 1, 3)
            q, k, v = (sh(q), sh(k), sh(v))
            q = l2norm(q) * qs
            k = l2norm(k) * ksc
            freqs, scale = rotary_tables(n)
            cos, sin = (jnp.cos(freqs), jnp.sin(freqs))
            q = q * cos * scale + rotate_half(q) * sin * scale
            inv = 1.0 / scale
            k = k * cos * inv + rotate_half(k) * sin * inv
            out = local_attention(q, k, v)
            out = out.transpose(0, 2, 1, 3).reshape(b, n, INNER)
            return out @ Wo

        def ffn_layer(x, g, bln, W1, b1, W2, b2):
            mu = x.mean(-1, keepdims=True)
            var = ((x - mu) ** 2).mean(-1, keepdims=True)
            xn = (x - mu) / jnp.sqrt(var + 1e-05) * g + bln
            hg = xn @ W1 + b1
            a, gate = jnp.split(hg, 2, -1)
            return a * jax.nn.gelu(gate, approximate=False) @ W2 + b2
        key = jax.random.key(seed)
        ks = jax.random.split(key, 8)
        B, N = (2, 256)
        init = lambda k, shape: jax.random.normal(k, shape, jnp.float32) * 0.02
        return {'x': jax.random.normal(ks[0], (B, N, DIM), jnp.float32), 'Wqkv': init(ks[1], (DEPTH, DIM, 3 * INNER)), 'q_scale': jnp.ones((DEPTH, DIM_HEAD), jnp.float32), 'k_scale': jnp.ones((DEPTH, DIM_HEAD), jnp.float32), 'Wo': init(ks[2], (DEPTH, INNER, DIM)), 'ln_g': jnp.ones((DEPTH, DIM), jnp.float32), 'ln_b': jnp.zeros((DEPTH, DIM), jnp.float32), 'W1': init(ks[3], (DEPTH, DIM, 2 * DIM_INNER)), 'b1': jnp.zeros((DEPTH, 2 * DIM_INNER), jnp.float32), 'W2': init(ks[4], (DEPTH, DIM_INNER, DIM)), 'b2': jnp.zeros((DEPTH, DIM), jnp.float32)}
    _L1_ffn_in = _L1_ffn_setup()
    _d = {'L0_attn_x': _L0_attn_in['x'], 'L0_attn_Wkqv': _L0_attn_in['Wkqv'], 'L0_attn_bkqv': _L0_attn_in['bkqv'], 'L0_attn_Wp': _L0_attn_in['Wp'], 'L0_attn_bp': _L0_attn_in['bp'], 'L0_ffn_Wg': _L0_ffn_in['Wg'], 'L0_ffn_We': _L0_ffn_in['We'], 'L1_attn_gamma': _L1_attn_in['gamma'], 'L1_attn_beta': _L1_attn_in['beta'], 'L1_attn_W_in': _L1_attn_in['W_in'], 'L1_attn_b_in': _L1_attn_in['b_in'], 'L1_attn_conv_w': _L1_attn_in['conv_w'], 'L1_attn_conv_b': _L1_attn_in['conv_b'], 'L1_attn_W_x': _L1_attn_in['W_x'], 'L1_attn_W_dt': _L1_attn_in['W_dt'], 'L1_attn_b_dt': _L1_attn_in['b_dt'], 'L1_attn_A_log': _L1_attn_in['A_log'], 'L1_attn_D_param': _L1_attn_in['D_param'], 'L1_attn_W_out': _L1_attn_in['W_out'], 'L1_attn_b_out': _L1_attn_in['b_out'], 'L1_ffn_Wqkv': _L1_ffn_in['Wqkv'], 'L1_ffn_q_scale': _L1_ffn_in['q_scale'], 'L1_ffn_k_scale': _L1_ffn_in['k_scale'], 'L1_ffn_Wo': _L1_ffn_in['Wo'], 'L1_ffn_ln_g': _L1_ffn_in['ln_g'], 'L1_ffn_ln_b': _L1_ffn_in['ln_b'], 'L1_ffn_W1': _L1_ffn_in['W1'], 'L1_ffn_b1': _L1_ffn_in['b1'], 'L1_ffn_W2': _L1_ffn_in['W2'], 'L1_ffn_b2': _L1_ffn_in['b2']}
    _x0 = _d['L0_attn_x']
    _d['L0_attn_x'] = jax.random.normal(jax.random.fold_in(jax.random.key(seed), 1), (1, 2048, 128), dtype=_x0.dtype)
    del _x0
    return _d

def reference(L0_attn_x, L0_attn_Wkqv, L0_attn_bkqv, L0_attn_Wp, L0_attn_bp, L0_ffn_Wg, L0_ffn_We, L1_attn_gamma, L1_attn_beta, L1_attn_W_in, L1_attn_b_in, L1_attn_conv_w, L1_attn_conv_b, L1_attn_W_x, L1_attn_W_dt, L1_attn_b_dt, L1_attn_A_log, L1_attn_D_param, L1_attn_W_out, L1_attn_b_out, L1_ffn_Wqkv, L1_ffn_q_scale, L1_ffn_k_scale, L1_ffn_Wo, L1_ffn_ln_g, L1_ffn_ln_b, L1_ffn_W1, L1_ffn_b1, L1_ffn_W2, L1_ffn_b2):

    def _L0_attn_ref(x, Wkqv, bkqv, Wp, bp):
        import jax, jax.numpy as jnp
        import numpy as np
        D = 128
        H = 16
        DH = D // H
        B, N = (4, 128)
        Bm, Nm, Dm = x.shape
        y = jnp.einsum('bnd,hde->bhne', x, Wkqv) + bkqv[None, :, None, :]
        k = y[..., :Dm]
        q = y[..., Dm:2 * Dm]
        v = y[..., 2 * Dm:]
        A = jnp.einsum('bhnd,bhmd->bhnm', q, k) / jnp.sqrt(jnp.float32(Dm))
        mask = jnp.tril(jnp.ones((Nm, Nm), dtype=bool))
        A = jnp.where(mask[None, None], A, -jnp.inf)
        A = jax.nn.softmax(A, axis=-1)
        sa = jnp.einsum('bhnm,bhmd->bnhd', A, v).reshape(Bm, Nm, Dm)
        return sa @ Wp + bp

    def _L0_ffn_ref(x, Wg, We):
        import jax, jax.numpy as jnp
        import numpy as np
        B, T, D, E, K = (4, 256, 128, 8, 2)
        logits = jnp.einsum('btd,de->bte', x, Wg)
        gate = jax.nn.softmax(logits, axis=-1)
        top_val, top_idx = jax.lax.top_k(gate, K)
        top_w = top_val / (jnp.sum(top_val, axis=-1, keepdims=True) + 1e-09)
        x_experts = jnp.einsum('btd,edm->btem', x, We)
        x_sel = jnp.take_along_axis(x_experts, top_idx[..., None], axis=2)
        out = jnp.sum(x_sel * top_w[..., None], axis=2)
        return out

    def _L1_attn_ref(x, gamma, beta, W_in, b_in, conv_w, conv_b, W_x, W_dt, b_dt, A_log, D_param, W_out, b_out):
        import jax, jax.numpy as jnp
        import numpy as np
        from jax import lax
        B, L, D = (4, 256, 128)
        ED = 2 * D
        N = 16
        K = 15
        R = D // 16
        EPS = 1e-05

        def _silu(u):
            return u * jax.nn.sigmoid(u)

        def _mamba_block(x, gamma, beta, W_in, b_in, conv_w, conv_b, W_x, W_dt, b_dt, A_log, D_param, W_out, b_out):
            mu = jnp.mean(x, axis=-1, keepdims=True)
            var = jnp.var(x, axis=-1, keepdims=True)
            xn = (x - mu) * lax.rsqrt(var + EPS) * gamma + beta
            xz = jnp.einsum('bld,ed->ble', xn, W_in) + b_in
            xin, z = (xz[..., :ED], xz[..., ED:])
            xc = jnp.swapaxes(xin, 1, 2)
            xc = jnp.pad(xc, ((0, 0), (0, 0), (K - 1, 0)))
            xc = lax.conv_general_dilated(xc, conv_w[:, None, :], window_strides=(1,), padding='VALID', dimension_numbers=('NCH', 'OIH', 'NCH'), feature_group_count=ED)
            xc = xc + conv_b[None, :, None]
            xc = _silu(jnp.swapaxes(xc, 1, 2))
            xdbl = jnp.einsum('ble,re->blr', xc, W_x)
            dt_low = xdbl[..., :R]
            Bm = xdbl[..., R:R + N]
            Cm = xdbl[..., R + N:]
            delta = jax.nn.softplus(jnp.einsum('blr,er->ble', dt_low, W_dt) + b_dt)
            A = -jnp.exp(A_log)

            def step(h, inp):
                d_t, B_t, C_t, x_t = inp
                dA = jnp.exp(d_t[..., None] * A)
                dBx = d_t[..., None] * B_t[:, None, :] * x_t[..., None]
                h = h * dA + dBx
                y = jnp.sum(h * C_t[:, None, :], axis=-1)
                return (h, y)
            xs = (jnp.swapaxes(delta, 0, 1), jnp.swapaxes(Bm, 0, 1), jnp.swapaxes(Cm, 0, 1), jnp.swapaxes(xc, 0, 1))
            h0 = jnp.zeros((x.shape[0], ED, N), x.dtype)
            _, ys = lax.scan(step, h0, xs)
            y = jnp.swapaxes(ys, 0, 1) + xc * D_param
            y = y * _silu(z)
            out = jnp.einsum('ble,de->bld', y, W_out) + b_out
            return x + out
        return _mamba_block(x, gamma, beta, W_in, b_in, conv_w, conv_b, W_x, W_dt, b_dt, A_log, D_param, W_out, b_out)

    def _L1_ffn_ref(x, Wqkv, q_scale, k_scale, Wo, ln_g, ln_b, W1, b1, W2, b2):
        import jax, jax.numpy as jnp
        import numpy as np
        DIM = 128
        DEPTH = 6
        HEADS = 16
        DIM_HEAD = 64
        WINDOW = 32
        INNER = HEADS * DIM_HEAD
        DIM_INNER = int(DIM * 4 * 2 / 3)
        QK_SCALE = 8.0

        def shift_tokens(t):
            a, s = jnp.split(t, 2, -1)
            s = jnp.pad(s, ((0, 0), (1, 0), (0, 0)))[:, :-1]
            return jnp.concatenate([a, s], -1)

        def l2norm(t):
            return t / jnp.maximum(jnp.linalg.norm(t, axis=-1, keepdims=True), 1e-12)

        def rotate_half(x):
            x1, x2 = jnp.split(x, 2, -1)
            return jnp.concatenate([-x2, x1], -1)

        def rotary_tables(n):
            half = jnp.arange(0, DIM_HEAD, 2, dtype=jnp.float32)
            inv_freq = 1.0 / 10000.0 ** (half / DIM_HEAD)
            t = jnp.arange(n, dtype=jnp.float32)
            freqs = t[:, None] * inv_freq[None, :]
            freqs = jnp.concatenate([freqs, freqs], -1)
            base_scale = (half + 0.4 * DIM_HEAD) / (1.4 * DIM_HEAD)
            power = (t - n // 2) / (WINDOW // 2)
            scale = base_scale[None, :] ** power[:, None]
            scale = jnp.concatenate([scale, scale], -1)
            return (freqs, scale)

        def local_attention(q, k, v):
            b, h, n, d = q.shape
            w = WINDOW
            nw = n // w
            bq = q.reshape(b, h, nw, w, d)
            bk = k.reshape(b, h, nw, w, d)
            bv = v.reshape(b, h, nw, w, d)

            def look(t):
                p = jnp.pad(t, ((0, 0), (0, 0), (1, 0), (0, 0), (0, 0)))
                return jnp.concatenate([p[:, :, :nw], p[:, :, 1:]], axis=3)
            bk2, bv2 = (look(bk), look(bv))
            seq = jnp.arange(n).reshape(nw, w)
            seq_p = jnp.pad(seq, ((1, 0), (0, 0)), constant_values=-1)
            jt = jnp.concatenate([seq_p[:nw], seq_p[1:]], axis=1)
            it = seq[:, :, None]
            jb = jt[:, None, :]
            mask = (it < jb) | (it > jb + w) | (jb == -1)
            sim = jnp.einsum('bhwie,bhwje->bhwij', bq, bk2) * QK_SCALE
            sim = jnp.where(mask, -jnp.finfo(sim.dtype).max, sim)
            attn = jax.nn.softmax(sim, -1)
            out = jnp.einsum('bhwij,bhwje->bhwie', attn, bv2)
            return out.reshape(b, h, n, d)

        def attn_layer(x, Wqkv, qs, ksc, Wo):
            b, n, _ = x.shape
            qkv = x @ Wqkv
            q, k, v = jnp.split(qkv, 3, -1)
            sh = lambda t: t.reshape(b, n, HEADS, DIM_HEAD).transpose(0, 2, 1, 3)
            q, k, v = (sh(q), sh(k), sh(v))
            q = l2norm(q) * qs
            k = l2norm(k) * ksc
            freqs, scale = rotary_tables(n)
            cos, sin = (jnp.cos(freqs), jnp.sin(freqs))
            q = q * cos * scale + rotate_half(q) * sin * scale
            inv = 1.0 / scale
            k = k * cos * inv + rotate_half(k) * sin * inv
            out = local_attention(q, k, v)
            out = out.transpose(0, 2, 1, 3).reshape(b, n, INNER)
            return out @ Wo

        def ffn_layer(x, g, bln, W1, b1, W2, b2):
            mu = x.mean(-1, keepdims=True)
            var = ((x - mu) ** 2).mean(-1, keepdims=True)
            xn = (x - mu) / jnp.sqrt(var + 1e-05) * g + bln
            hg = xn @ W1 + b1
            a, gate = jnp.split(hg, 2, -1)
            return a * jax.nn.gelu(gate, approximate=False) @ W2 + b2
        for i in range(DEPTH):
            x = attn_layer(shift_tokens(x), Wqkv[i], q_scale[i], k_scale[i], Wo[i]) + x
            x = ffn_layer(shift_tokens(x), ln_g[i], ln_b[i], W1[i], b1[i], W2[i], b2[i]) + x
        return x
    x = L0_attn_x
    xn = _layernorm(x, axis=-1)
    x = x + _L0_attn_ref(xn, L0_attn_Wkqv, L0_attn_bkqv, L0_attn_Wp, L0_attn_bp) + _L0_ffn_ref(xn, L0_ffn_Wg, L0_ffn_We)
    xn = _layernorm(x, axis=-1)
    x = x + _L1_attn_ref(xn, L1_attn_gamma, L1_attn_beta, L1_attn_W_in, L1_attn_b_in, L1_attn_conv_w, L1_attn_conv_b, L1_attn_W_x, L1_attn_W_dt, L1_attn_b_dt, L1_attn_A_log, L1_attn_D_param, L1_attn_W_out, L1_attn_b_out) + _L1_ffn_ref(xn, L1_ffn_Wqkv, L1_ffn_q_scale, L1_ffn_k_scale, L1_ffn_Wo, L1_ffn_ln_g, L1_ffn_ln_b, L1_ffn_W1, L1_ffn_b1, L1_ffn_W2, L1_ffn_b2)
    return x

_drawn_inputs = setup_inputs


def setup_inputs(seed=0):
    import zlib

    import numpy as np

    out = dict(_drawn_inputs(seed))
    spreads = {'L0_attn_bkqv': (0.0, 0.435),
     'L0_attn_bp': (0.0, 0.1),
     'L1_attn_gamma': (1.0, 0.6),
     'L1_attn_beta': (0.0, 0.8),
     'L1_attn_b_in': (0.0, 0.8),
     'L1_attn_conv_b': (0.0, 0.8),
     'L1_attn_D_param': (1.0, 0.6),
     'L1_attn_b_out': (0.0, 0.27),
     'L1_ffn_q_scale': (1.0, 0.6),
     'L1_ffn_k_scale': (1.0, 0.6),
     'L1_ffn_ln_g': (1.0, 0.6),
     'L1_ffn_ln_b': (0.0, 0.8),
     'L1_ffn_b1': (0.0, 0.8),
     'L1_ffn_b2': (0.0, 0.1)}
    factors = {'L0_attn_Wkqv': 8.0,
     'L0_attn_Wp': 3.09,
     'L1_attn_W_in': 8.0,
     'L1_attn_conv_w': 8.0,
     'L1_attn_W_x': 8.0,
     'L1_attn_W_dt': 8.0,
     'L1_attn_b_dt': 8.0,
     'L1_attn_A_log': 8.0,
     'L1_attn_W_out': 8.0,
     'L1_ffn_W1': 5.897,
     'L1_ffn_W2': 5.785}
    for name, (base, spread) in spreads.items():
        noise = np.random.default_rng([zlib.crc32(name.encode()), seed]).standard_normal(out[name].shape)
        drawn = base * np.exp(spread * noise) if base else spread * noise
        out[name] = jnp.asarray(drawn.astype(out[name].dtype))
    for name, factor in factors.items():
        out[name] = (out[name] * factor).astype(out[name].dtype)
    return out
```

```python
from contextlib import ExitStack, contextmanager

import numpy as np

import concourse.bass as bass
from concourse import mybir

F32 = mybir.dt.float32
BF16 = mybir.dt.bfloat16
ALU = mybir.AluOpType
ACT = mybir.ActivationFunctionType
X_AXIS = mybir.AxisListType.X
ds = bass.ds

STOP = 99

P = 128
T = 2048
NT = T // P
EPS = 1e-5
H0 = 16
DV0 = 8
VW = DV0 + 1
KB = 1024
NE = 8
ED = 256
ET = ED // P
NS = 16
KC = 15
R = 8
RX = R + 2 * NS
L = 6
H = 16
DH = 64
INNER = H * DH
WIN = 32
FI = 341
FCH = [(0, 128), (128, 128), (256, FI - 256)]
TB = 4
KW = WIN + P
PERM = [0, 2, 1, 3]


class Counter:

    def __init__(self, nc, eng, name, step=1):
        self.eng, self.name, self.step = eng, name, step
        self.sem = nc.alloc_semaphore("s_" + name)
        self.base, self.k, self.seen, self.alone, self.spare = 0, 0, {}, False, None

    def tick(self, ins):
        ins.then_inc(self.sem, self.step)
        self.k += self.step
        return self.now()

    def now(self):
        return (self, self.base + self.k, self.k)

    def wait(self, *events):
        new = [ev for ev in events if ev and self.seen.get(ev[0].name, -1) < ev[2]]
        for ev in new:
            if ev is None:
                continue
            c, value, k = ev
            if self.seen.get(c.name, -1) < k:
                self.eng.wait_ge(c.sem, value)
                self.seen[c.name] = k
                if self.alone and not isinstance(value, int):
                    self.settle()

    def settle(self):
        self.eng.sem_inc(self.spare, 1)


class Program:
    def __init__(self, nc):
        self.nc = nc
        self.pe = Counter(nc, nc.tensor, "pe")
        self.dve = Counter(nc, nc.vector, "dve")
        self.act = Counter(nc, nc.scalar, "act")
        self.pool = Counter(nc, nc.gpsimd, "pool")
        self.sp = Counter(nc, nc.sync, "sp")
        self.engines = [self.pe, self.dve, self.act, self.pool, self.sp]
        self.counters = list(self.engines)
        self.sp.alone = self.pool.alone = True
        for e in self.engines:
            e.spare = nc.alloc_semaphore("spare_" + e.name)

    def dma(self, name):
        c = Counter(self.nc, self.nc.sync, name, 16)
        self.counters.append(c)
        return c

    @contextmanager
    def loop(self, n, **per):
        kept = [(c.base, c.k) for c in self.counters]
        for e in self.engines:
            if not isinstance(e.base, int):
                e.settle()
        with self.nc.Fori(0, n) as i:
            for c in self.counters:
                c.base = c.base + c.k + i * (per.get(c.name, 0) * c.step) if per.get(c.name, 0) else c.base + c.k
                c.k = 0
                c.seen = {}
            self.meet()
            yield i
            gained = {c.name: c.k // c.step for c in self.counters if c.k}
            assert gained == {a: b for a, b in per.items() if b}, f"the loop's counts are {gained}"
            for c in self.counters:
                c.seen = {}
        for c, (base, k) in zip(self.counters, kept):
            c.base, c.k = base, k + n * per.get(c.name, 0) * c.step
            c.seen = {}

    def meet(self):
        for e in self.engines:
            for c in self.engines:
                positive = c.k > 0 or not isinstance(c.base, int) or c.base > 0
                if positive:
                    e.seen[c.name] = -1
                    e.wait(c.now())


def bcast(ap, at, n):
    shape = list(ap.shape)
    return ap.unsqueeze(at).broadcast_to(shape[:at] + [n] + shape[at:])


def layer_norm(p, src, dst, st, after, scratch):
    dve, act = p.dve, p.act
    V, A = p.nc.vector, p.nc.scalar
    dve.wait(*after)
    e = dve.tick(V.tensor_reduce(st[:, 0, :], src, X_AXIS, ALU.add))
    dve.wait(e)
    e = dve.tick(V.tensor_scalar(st[:, 1, :], st[:, 0, :], -1.0 / P, None, ALU.mult))
    dve.wait(e)
    e = dve.tick(V.tensor_tensor(dst, src, bcast(st[:, 1, :], 2, P), ALU.add))
    act.wait(e)
    e = act.tick(A.activation(scratch, dst, ACT.Square))
    dve.wait(e)
    e = dve.tick(V.tensor_reduce(st[:, 2, :], scratch, X_AXIS, ALU.add))
    dve.wait(e)
    e = dve.tick(V.tensor_scalar(st[:, 3, :], st[:, 2, :], 1.0 / P, EPS, ALU.mult, ALU.add))
    act.wait(e)
    e = act.tick(A.activation(st[:, 0, :], st[:, 3, :], ACT.Sqrt))
    dve.wait(e)
    e = dve.tick(V.reciprocal(st[:, 1, :], st[:, 0, :]))
    dve.wait(e)
    return dve.tick(V.tensor_tensor(dst, dst, bcast(st[:, 1, :], 2, P), ALU.mult))


def build(nc, d, out):
    p = Program(nc)
    pe, dve, act, pool, sp = p.engines
    TE, V, A, G, S = nc.tensor, nc.vector, nc.scalar, nc.gpsimd, nc.sync
    ctx = ExitStack()
    with ctx:
        def sb(name, shape, dt=F32, c=ctx):
            return c.enter_context(nc.sbuf_tensor(name, shape, dt))

        ps = ctx.enter_context(nc.psum_tensor("ps", [P, 8, 512], F32))

        def load(dst, src, name, after=()):
            c = p.dma(name)
            sp.wait(*after)
            return c.tick(S.dma_start(dst, src))

        ident = sb("ident", [P, P])
        identb = sb("identb", [P, P], BF16)
        acc = sb("acc", [P, NT, P])
        xn = sb("xn", [P, NT, P])
        xs = sb("xs", [P, NT + 1, P])
        st = sb("st", [P, 4, NT])

        x0 = xs[:, 1:, :]
        x_in = load(x0, d["x"].rearrange("(t p) d -> p t d", p=P), "x")
        id_in = load(ident[:], d["ident"], "ident")
        dve.wait(id_in)
        idb_in = dve.tick(V.tensor_copy(identb[:], ident[:]))
        pool.tick(G.memset(xs[:, 0, :], 0.0))
        outs = p.dma("out")

        def transpose_tiles(src, dst, after, scale=None, bias=None, banks=(0, 1)):
            free, last = [None, None], None
            for q in range(NT // 4):
                bank = ps[:, banks[q % 2], :]
                pe.wait(id_in, *after, free[q % 2])
                for c in range(4):
                    mm = TE.transpose(bank[:, c * P:(c + 1) * P], src[:, 4 * q + c, :], ident[:])
                done = pe.tick(mm)
                to = dst[:, q * 512:(q + 1) * 512]
                if scale is None and q % 2:
                    dve.wait(done)
                    free[1] = dve.tick(V.tensor_copy(to, bank))
                else:
                    act.wait(done)
                    if scale is None:
                        ins = A.activation(to, bank, ACT.Copy)
                    else:
                        ins = A.activation(to, bank, ACT.Identity, bias=bias, scale=scale)
                    free[q % 2] = act.tick(ins)
            return free

        with ExitStack() as c0:
            xnT = sb("xnT", [P, T], c=c0)
            valL = sb("values", [P, NT, H0, VW], c=c0)
            wv = sb("wv", [P, P], c=c0)
            bv = sb("bv", [P, P], c=c0)
            wp = sb("wp", [P, P], c=c0)
            bp = sb("bp", [P, P], c=c0)
            causal = sb("causal", [P, P], BF16, c=c0)
            nmaxL = sb("nmaxL", [P, H0, 24], c=c0)
            oL = sb("oL", [P, H0, 24, VW], c=c0)
            wv_in = load(wv[:], d["wv"], "wv")
            bv_in = load(bv[:], d["bv"].partition_broadcast(P), "bv")
            causal32 = sb("causal32", [P, P], c=c0)
            e = load(causal32[:], d["causal"], "causal")
            dve.wait(e)
            causal_in = dve.tick(V.tensor_copy(causal[:], causal32[:]))
            wp_in = load(wp[:], d["wp"], "wp")
            bp_in = load(bp[:], d["bp"].partition_broadcast(P), "bp")
            with ExitStack() as cm:
                wg = sb("wg", [P, NE], c=cm)
                we = sb("we", [P, NE * P], c=cm)
                lower = sb("lower", [P, NE, NE], c=cm)
                wg_in = load(wg[:], d["wg"], "wg")
                we_in = load(we[:].rearrange("p (e m) -> p e m", e=NE), d["we"].rearrange("e d m -> d e m"), "we")
                lower_in = load(lower[:], d["lower"].partition_broadcast(P), "lower")
                gate = sb("gate", [P, NT, NE], c=cm)
                g1 = sb("g1", [P, NT], c=cm)
                g2 = sb("g2", [P, NT, NE], c=cm)
                cmp1 = sb("cmp1", [P, NT, NE, NE], c=cm)
                cmp2 = sb("cmp2", [P, NT, NE, NE], c=cm)
                xe = sb("xe", [P, 2, NE, P], c=cm)

                e = layer_norm(p, x0, xn[:], st[:], [x_in], acc[:])
                xnT_ready = transpose_tiles(xn, xnT, [e])
                ones_set = pool.tick(G.memset(valL[:, :, :, DV0], 1.0))

                free = [None, None]
                for q in range(4):
                    bank = ps[:, 2 + q % 2, :]
                    pe.wait(wv_in, *xnT_ready, free[q % 2])
                    for c in range(4):
                        t = 4 * q + c
                        mm = TE.matmul(bank[:, c * P:(c + 1) * P], xnT[:, t * P:(t + 1) * P], wv[:], start=True, stop=True)
                    done = pe.tick(mm)
                    dve.wait(done, bv_in)
                    for c in range(4):
                        t = 4 * q + c
                        ins = V.tensor_tensor(valL[:, t, :, 0:DV0], bank[:, c * P:(c + 1) * P].rearrange("p (h v) -> p h v", h=H0),
                                              bv[:].rearrange("p (h v) -> p h v", h=H0), ALU.add)
                    free[q % 2] = dve.tick(ins)

                glog = ps[:, 4, 0:NT * NE].rearrange("p (t e) -> p t e", e=NE)
                pe.wait(wg_in)
                for t in range(NT):
                    mm = TE.matmul(glog[:, t, :], xnT[:, t * P:(t + 1) * P], wg[:], start=True, stop=True)
                done = pe.tick(mm)
                dve.wait(done)
                e = dve.tick(V.tensor_reduce(g1[:], glog, X_AXIS, ALU.max))
                dve.wait(e)
                e = dve.tick(V.tensor_tensor(g2[:], glog, bcast(g1[:], 2, NE), ALU.subtract))
                act.wait(e)
                e = act.tick(A.activation(g2[:], g2[:], ACT.Exp))
                dve.wait(e)
                e = dve.tick(V.tensor_reduce(g1[:], g2[:], X_AXIS, ALU.add))
                dve.wait(e)
                e = dve.tick(V.reciprocal(g1[:], g1[:]))
                dve.wait(e)
                e = dve.tick(V.tensor_tensor(gate[:], g2[:], bcast(g1[:], 2, NE), ALU.mult))
                mine, other = bcast(gate[:], 3, NE), bcast(gate[:], 2, NE)
                dve.wait(e, lower_in)
                V.tensor_tensor(cmp1[:], other, mine, ALU.is_gt)
                e = dve.tick(V.tensor_tensor(cmp2[:], other, mine, ALU.is_equal))
                dve.wait(e)
                e = dve.tick(V.tensor_tensor(cmp2[:], cmp2[:], bcast(lower[:], 1, NT), ALU.mult))
                dve.wait(e)
                e = dve.tick(V.tensor_tensor(cmp1[:], cmp1[:], cmp2[:], ALU.add))
                dve.wait(e)
                e = dve.tick(V.tensor_reduce(g2[:], cmp1[:], X_AXIS, ALU.add))
                dve.wait(e)
                e = dve.tick(V.tensor_scalar(g2[:], g2[:], 1.5, None, ALU.is_lt))
                dve.wait(e)
                e = dve.tick(V.tensor_tensor(gate[:], gate[:], g2[:], ALU.mult))
                dve.wait(e)
                e = dve.tick(V.tensor_reduce(g1[:], gate[:], X_AXIS, ALU.add))
                dve.wait(e)
                e = dve.tick(V.tensor_scalar(g1[:], g1[:], 1e-9, None, ALU.add))
                dve.wait(e)
                e = dve.tick(V.reciprocal(g1[:], g1[:]))
                dve.wait(e)
                gate_ready = dve.tick(V.tensor_tensor(gate[:], gate[:], bcast(g1[:], 2, NE), ALU.mult))
                free, pend = [None, None], [None, None]
                for t in range(NT):
                    b = t % 2
                    bank = ps[:, 2 * b:2 * b + 2, :]
                    pe.wait(we_in, free[b], dve.now())
                    for g in range(2):
                        mm = TE.matmul(bank[:, g, :], xnT[:, t * P:(t + 1) * P], we[:, g * 512:(g + 1) * 512], start=True, stop=True)
                    done = pe.tick(mm)
                    dve.wait(done, gate_ready, pend[b])
                    for g in range(2):
                        ins = V.tensor_tensor(xe[:, b, 4 * g:4 * g + 4, :], bank[:, g, :].rearrange("p (e m) -> p e m", e=4),
                                              bcast(gate[:, t, 4 * g:4 * g + 4], 2, P), ALU.mult)
                    free[b] = dve.tick(ins)
                    dve.wait(free[b])
                    e = dve.tick(V.tensor_reduce(acc[:, t, :], xe[:, b, :, :].rearrange("p e m -> p m e"), X_AXIS, ALU.add))
                    pool.wait(e)
                    pend[b] = pool.tick(G.tensor_tensor(acc[:, t, :], acc[:, t, :], x0[:, t, :], ALU.add))
                p.meet()

            with ExitStack() as ca:
                wh = sb("wh", [P, 2, 2 * P], c=ca)
                bh = sb("bh", [P, 2, 2], c=ca)
                bqs = sb("bqs", [P, 2], c=ca)
                kq = sb("kq", [P, 2, 2, T], c=ca)
                prob = sb("prob", [P, 2, KB], c=ca)
                probT = sb("probT", [P, 2, 512], c=ca)
                nmx = sb("nmx", [P, 2, 24], c=ca)
                w_in = [p.dma(f"wh{b}") for b in range(2)]
                units = [(g, 0, (g + 1) * P) for g in range(NT // 2)]
                for g in range(NT // 2, NT):
                    units += [(g, 0, KB), (g, KB, (g + 1) * P - KB)]
                o_banks = ps[:, 7, :]

                with p.loop(H0 // 2, pe=224, act=104, dve=94, wh0=2, wh1=2) as i:
                    def fetch(b):
                        w_in[b].tick(S.dma_start(wh[:, b, :], d["wkq"][ds(2 * i + b, 1), :, :].rearrange("a d e -> d (a e)")))
                        w_in[b].tick(S.dma_start(bh[:, b, :], d["bkq"][ds(2 * i + b, 1), :, :].rearrange("a d e -> d (a e)")))

                    fetch(0)
                    fetch(1)
                    free_s, free_pt, free_prob, free_probT = [None] * 2, [None] * 2, [None] * 2, [None] * 2
                    free_pr, npt, n_s = None, 0, 0
                    last_act = None
                    for b in range(2):
                        ready = {}
                        dve.wait(w_in[b].now())
                        bqs_ready = dve.tick(V.tensor_scalar(bqs[:, b:b + 1], bh[:, b, 1:2], P ** -0.5, None, ALU.mult))
                        for n in range(8):
                            w, ch = n % 2, n // 2
                            pe.wait(w_in[b].now(), free_pr)
                            done = pe.tick(TE.matmul(ps[:, 6, :], wh[:, b, w * P:(w + 1) * P], xnT[:, ch * 512:(ch + 1) * 512], start=True, stop=True))
                            act.wait(done, bqs_ready)
                            free_pr = act.tick(A.activation(kq[:, b, w, ch * 512:(ch + 1) * 512], ps[:, 6, :], ACT.Identity,
                                                            bias=(bh[:, b, 0:1], bqs[:, b:b + 1])[w], scale=(1.0, P ** -0.5)[w]))
                            ready[w, ch] = free_pr

                        def scores(u):
                            nonlocal n_s
                            g, k0, nk = units[u]
                            s = n_s % 2
                            n_s += 1
                            pe.wait(free_s[s], ready[1, g // 4], ready[0, (k0 + nk - 1) // 512])
                            diag = k0 + nk == (g + 1) * P
                            for c0_ in range(0, nk, 512):
                                w = min(512, nk - c0_)
                                last = c0_ + w == nk
                                mm = TE.matmul(ps[:, 2 * s + c0_ // 512, 0:w], kq[:, b, 1, g * P:(g + 1) * P], kq[:, b, 0, k0 + c0_:k0 + c0_ + w],
                                               start=True, stop=not (last and diag), skip_group_check=True)
                            if diag:
                                c0_ = (nk - P) // 512
                                o = (nk - P) % 512
                                pe.wait(causal_in, idb_in)
                                mm = TE.matmul(ps[:, 2 * s + c0_, o:o + P], identb[:], causal[:], start=False, stop=True, skip_group_check=True)
                            done = pe.tick(mm)
                            sc = ps[:, 2 * s:2 * s + 2, :].rearrange("p a b -> p (a b)")[:, 0:nk]
                            dve.wait(done)
                            e = dve.tick(V.tensor_reduce(nmx[:, b, u:u + 1], sc, X_AXIS, ALU.max, negate=True))
                            act.wait(e, free_prob[s])
                            free_s[s] = act.tick(A.activation(prob[:, s, 0:nk], sc, ACT.Exp, bias=nmx[:, b, u:u + 1]))
                            return s, free_s[s]

                        def values(u, s, prob_ready):
                            nonlocal npt
                            g, k0, nk = units[u]
                            n = nk // P
                            for g0 in range(0, n, 4):
                                m = min(4, n - g0)
                                r = npt % 2
                                npt += 1
                                pe.wait(prob_ready, free_pt[r])
                                for c in range(m):
                                    mm = TE.transpose(ps[:, 4 + r, c * P:(c + 1) * P], prob[:, s, (g0 + c) * P:(g0 + c + 1) * P], ident[:])
                                done = pe.tick(mm)
                                eng = (dve, act)[r]
                                eng.wait(done, free_probT[r])
                                if r:
                                    ins = A.activation(probT[:, r, 0:m * P], ps[:, 4 + r, 0:m * P], ACT.Copy)
                                else:
                                    ins = V.tensor_copy(probT[:, r, 0:m * P], ps[:, 4 + r, 0:m * P])
                                free_pt[r] = eng.tick(ins)
                                pe.wait(free_pt[r])
                                for c in range(m):
                                    j = k0 // P + g0 + c
                                    mm = TE.matmul(o_banks[:, 256 * b + u * VW:256 * b + (u + 1) * VW], probT[:, r, c * P:(c + 1) * P],
                                                   valL[:, j, ds(2 * i + b, 1), :], start=(g0 + c == 0), stop=(g0 + c == n - 1), skip_group_check=True)
                                free_probT[r] = pe.tick(mm)
                            free_prob[s] = done

                        held = None
                        for u in range(len(units)):
                            nxt = (u,) + scores(u)
                            if held:
                                values(*held)
                            held = nxt
                        values(*held)
                        dve.wait(pe.now())
                        dve.tick(V.tensor_copy(oL[:, ds(2 * i + b, 1), :, :], o_banks[:, 256 * b:256 * b + 24 * VW]))
                        dve.tick(V.tensor_copy(nmaxL[:, ds(2 * i + b, 1), :], nmx[:, b, :]))
                p.meet()

            with ExitStack() as cj:
                sa = sb("sa", [P, NT, H0, DV0], c=cj)
                saT = sb("saT", [P, T], c=cj)
                HN = NT // 2
                wgt = sb("wgt", [P, 2, H0, HN], c=cj)
                mn = sb("mn", [P, H0, HN], c=cj)
                o2 = sb("o2", [P, 2, H0, HN, VW], c=cj)
                rec = sb("rec", [P, H0, HN], c=cj)
                nm = [nmaxL[:, :, HN + j::2] for j in range(2)]
                ov = [oL[:, :, HN + j::2, :] for j in range(2)]
                e = dve.tick(V.tensor_tensor(mn[:], nm[0], nm[1], ALU.min))
                dve.wait(e)
                for j in range(2):
                    e = dve.tick(V.tensor_tensor(wgt[:, j], mn[:], nm[j], ALU.subtract))
                act.wait(e)
                e = act.tick(A.activation(wgt[:], wgt[:], ACT.Exp))
                dve.wait(e)
                for j in range(2):
                    e = dve.tick(V.tensor_tensor(o2[:, j], ov[j], bcast(wgt[:, j], 3, VW), ALU.mult))
                dve.wait(e)
                e = dve.tick(V.tensor_tensor(o2[:, 0], o2[:, 0], o2[:, 1], ALU.add))
                dve.wait(e)
                for half, o in ((0, oL[:, :, 0:HN, :]), (1, o2[:, 0])):
                    e = dve.tick(V.reciprocal(rec[:], o[:, :, :, DV0]))
                    dve.wait(e)
                    e = dve.tick(V.tensor_tensor(sa[:, half * HN:(half + 1) * HN, :, :].rearrange("p g h v -> p h g v"), o[:, :, :, 0:DV0],
                                                 bcast(rec[:], 3, DV0), ALU.mult))
                    dve.wait(e)
                saT_ready = transpose_tiles(sa[:].rearrange("p t h v -> p t (h v)"), saT, [e])
                pe.wait(*saT_ready, wp_in)
                for t in range(NT):
                    mm = TE.matmul(ps[:, 2 + t // 4, (t % 4) * P:(t % 4 + 1) * P], saT[:, t * P:(t + 1) * P], wp[:], start=True, stop=True, skip_group_check=True)
                done = pe.tick(mm)
                dve.wait(done, bp_in, pool.now())
                e = dve.tick(V.tensor_tensor(acc[:].rearrange("p (q c) d -> p q (c d)", q=4), acc[:].rearrange("p (q c) d -> p q (c d)", q=4), ps[:, 2:6, :], ALU.add))
                dve.wait(e)
                e = dve.tick(V.tensor_tensor(acc[:], acc[:], bcast(bp[:], 1, NT), ALU.add))
                e = layer_norm(p, acc[:], xn[:], st[:], [e], saT[:].rearrange("p (t d) -> p t d", d=P))
                p.meet()

        if STOP >= 2:
            mamba(p, d, sb, ps, load, acc, xn, st, ident, transpose_tiles)
        if STOP >= 3:
            transformer(p, d, sb, ps, load, acc, xn, xs, ident, identb)

        res = acc if STOP >= 2 else (acc if STOP == 1 else xn)
        S.dma_start(out.rearrange("(t p) d -> p t d", p=P), res[:]).then_inc(outs.sem, 16)
        S.wait_ge(outs.sem, 16)


def mamba(p, d, sb, ps, load, acc, xn, st, ident, transpose_tiles):
    pe, dve, act, pool, sp = p.engines
    TE, V, A, G, S = p.nc.tensor, p.nc.vector, p.nc.scalar, p.nc.gpsimd, p.nc.sync
    PAD = KC - 1
    with ExitStack() as c:
        u = sb("mu", [P, ET, T], c=c)
        z = sb("mz", [P, ET, T], c=c)
        y = sb("my", [P, ET, T], c=c)
        xd = sb("xd", [RX, T], c=c)
        win = sb("win", [P, 4 * P], c=c)
        wx = sb("wx", [P, ET, RX], c=c)
        wdt = sb("wdt", [R, ET * P], c=c)
        wout = sb("wout", [P, ET, P], c=c)
        taps = sb("taps", [P, ET, KC], c=c)
        alog = sb("alog", [P, ET, NS], c=c)
        cols = sb("cols", [P, 12], c=c)
        bout = sb("bout", [P, P], c=c)
        gam, bet, bin_, cb, bdt, dpar = (cols[:, a:b] for a, b in ((0, 1), (1, 2), (2, 6), (6, 8), (8, 10), (10, 12)))
        win_in = load(win[:], d["win"], "win")
        cols_in = load(cols[:], d["cols"], "cols")
        taps_in = load(taps[:], d["taps"].rearrange("(a p) k -> p a k", p=P), "taps")
        wx_in = load(wx[:], d["wx"].rearrange("(a p) r -> p a r", p=P), "wx")
        wdt_in = load(wdt[:], d["wdt"], "wdt")
        alog_in = load(alog[:], d["alog"].rearrange("(a p) n -> p a n", p=P), "alog")
        wout_in = load(wout[:], d["wout"].rearrange("(a p) n -> p a n", p=P), "wout")
        bout_in = load(bout[:], d["bout"].partition_broadcast(P), "bout")
        act.wait(alog_in)
        a_exp = act.tick(A.activation(alog[:], alog[:], ACT.Exp))
        pool.wait(a_exp)
        neg_a = pool.tick(G.tensor_scalar(alog[:], alog[:], -1.0, None, ALU.mult))
        with ExitStack() as cx:
            xT = sb("mxT", [P, T], c=cx)
            xp = sb("mxp", [P, ET, PAD + T], c=cx)
            hat = y[:, 0, :].rearrange("p (t d) -> p t d", d=P)
            e = layer_norm(p, xn[:], hat, st[:], [], y[:, 1, :].rearrange("p (t d) -> p t d", d=P))
            act.wait(cols_in)
            xT_ready = transpose_tiles(hat, xT, [e], scale=gam, bias=bet)
            padded = dve.tick(V.memset(xp[:, :, 0:PAD], 0.0))
            free = [None] * 4
            pe.wait(win_in, *xT_ready)
            n = 0
            for m in (2, 3, 0, 1):
                for q in range(4):
                    bank = ps[:, 2 + n % 4, :]
                    pe.wait(free[n % 4])
                    done = pe.tick(TE.matmul(bank, win[:, m * P:(m + 1) * P], xT[:, q * 512:(q + 1) * 512], start=True, stop=True))
                    act.wait(done)
                    if m >= 2:
                        ins = A.activation(z[:, m - 2, q * 512:(q + 1) * 512], bank, ACT.Silu, bias=bin_[:, m:m + 1])
                    else:
                        ins = A.activation(xp[:, m, PAD + q * 512:PAD + (q + 1) * 512], bank, ACT.Identity, bias=bin_[:, m:m + 1])
                    free[n % 4] = act.tick(ins)
                    n += 1
            dve.wait(act.now(), padded, taps_in)
            e0 = [None] * ET
            for k in range(KC):
                for a in range(ET):
                    if k == 0:
                        e = dve.tick(V.tensor_scalar(u[:, a, :], xp[:, a, 0:T], taps[:, a, 0:1], cb[:, a:a + 1], ALU.mult, ALU.add))
                    else:
                        dve.wait(e0[a])
                        e = dve.tick(V.scalar_tensor_tensor(u[:, a, :], xp[:, a, k:k + T], taps[:, a, k:k + 1], u[:, a, :], ALU.mult, ALU.add))
                    e0[a] = e
            act.wait(dve.now())
            for a in range(ET):
                u_ready = act.tick(A.activation(u[:, a, :], u[:, a, :], ACT.Silu))
            p.meet()
        pe.wait(wx_in, u_ready)
        for q in range(4):
            for a in range(ET):
                mm = TE.matmul(ps[0:RX, q, :], wx[:, a, :], u[:, a, q * 512:(q + 1) * 512], start=a == 0, stop=a == ET - 1)
        done = pe.tick(mm)
        dve.wait(done)
        xd_ready = dve.tick(V.tensor_copy(xd[:].rearrange("p (q n) -> p q n", q=4), ps[0:RX, 0:4, :]))
        bc = p.nc.dram_tensor("bc_scratch", [2 * NS, T], F32).ap()
        bc_saved = load(bc, xd[R:RX, :], "bc_save", [xd_ready])
        delta = sb("delta", [P, ET, T], c=c)
        du = sb("du", [P, ET, T], c=c)
        tmp = y
        pe.wait(wdt_in, xd_ready)
        for a in range(ET):
            for q in range(4):
                mm = TE.matmul(ps[:, 4 * a + q, :], wdt[:, a * P:(a + 1) * P], xd[0:R, q * 512:(q + 1) * 512], start=True, stop=True)
        done = pe.tick(mm)
        act.wait(done)
        for a in range(ET):
            e = act.tick(A.activation(delta[:, a, :], ps[:, 4 * a:4 * a + 4, :].rearrange("p a b -> p (a b)"), ACT.Identity, bias=bdt[:, a:a + 1]))
        act.wait(e)
        e = act.tick(A.activation(tmp[:], delta[:], ACT.Abs))
        act.wait(e)
        e = act.tick(A.activation(tmp[:], tmp[:], ACT.Exp, scale=-1.0))
        act.wait(e)
        e = act.tick(A.activation(tmp[:], tmp[:], ACT.Ln, bias=1.0))
        dve.wait(e)
        e = dve.tick(V.scalar_tensor_tensor(delta[:], delta[:], 0.0, tmp[:], ALU.max, ALU.add))
        dve.wait(e)
        e = dve.tick(V.tensor_tensor(du[:], delta[:], u[:], ALU.mult))
        y_zero = dve.tick(V.memset(y[:], 0.0))
        with ExitStack() as cs:
            rows = sb("rows", [1, 2, T], c=cs)
            ones = sb("ones", [1, P], c=cs)
            dec = sb("dec", [P, ET, T], c=cs)
            inp = sb("inp", [P, ET, T], c=cs)
            ones_set = pool.tick(G.memset(ones[:], 1.0))
            ac = sb("ac", [P, ET], c=cs)
            bc_in = p.dma("bc")
            sp.wait(bc_saved)
            p.meet()
            with p.loop(NS, pe=2, act=2, dve=7, pool=2, bc=2) as n:
                sp.wait(dve.now())
                bc_in.tick(S.dma_start(rows[:, 0, :], bc[ds(n, 1), :]))
                got = bc_in.tick(S.dma_start(rows[:, 1, :], bc[ds(NS + n, 1), :]))
                pe.wait(got)
                for w in range(2):
                    for q in range(4):
                        mm = TE.matmul(ps[:, 4 * w + q, :], ones[:], rows[:, w, q * 512:(q + 1) * 512], start=True, stop=True)
                    rows_out = pe.tick(mm)
                    if w == 0:
                        b_out = rows_out
                e = dve.tick(V.tensor_copy(ac[:], alog[:, :, ds(n, 1)]))
                act.wait(e)
                for a in range(ET):
                    e = act.tick(A.activation(dec[:, a, :], delta[:, a, :], ACT.Exp, scale=ac[:, a:a + 1]))
                    if a == 0:
                        dec_ready = [e]
                dec_ready.append(e)
                dve.wait(b_out)
                for a in range(ET):
                    inp_ready = dve.tick(V.tensor_tensor(inp[:, a, :], du[:, a, :], ps[:, 0:4, :].rearrange("p a b -> p (a b)"), ALU.mult))
                dve.wait(inp_ready)
                for a in range(ET):
                    dve.wait(dec_ready[a])
                    e = dve.tick(V.tensor_tensor_scan(inp[:, a, :], dec[:, a, :], inp[:, a, :], 0.0, ALU.mult, ALU.add))
                    if a == 0:
                        h_ready = [e]
                h_ready.append(e)
                dve.wait(rows_out)
                for a in range(ET):
                    dve.wait(h_ready[a])
                    e = dve.tick(V.tensor_tensor(dec[:, a, :], inp[:, a, :], ps[:, 4:8, :].rearrange("p a b -> p (a b)"), ALU.mult))
                    pool.wait(e)
                    pool.tick(G.tensor_tensor(y[:, a, :], y[:, a, :], dec[:, a, :], ALU.add))
            p.meet()
        for a in range(ET):
            e = dve.tick(V.scalar_tensor_tensor(y[:, a, :], u[:, a, :], dpar[:, a:a + 1], y[:, a, :], ALU.mult, ALU.add))
            dve.wait(e)
            e = dve.tick(V.tensor_tensor(y[:, a, :], y[:, a, :], z[:, a, :], ALU.mult))
        pe.wait(e, wout_in)
        for t in range(NT):
            for a in range(ET):
                mm = TE.matmul(ps[:, t // 4, (t % 4) * P:(t % 4 + 1) * P], y[:, a, t * P:(t + 1) * P], wout[:, a, :],
                               start=a == 0, stop=a == ET - 1, skip_group_check=True)
        done = pe.tick(mm)
        flat = acc[:].rearrange("p (q c) d -> p q (c d)", q=4)
        dve.wait(done, bout_in)
        e = dve.tick(V.tensor_tensor(flat, flat, ps[:, 0:4, :], ALU.add))
        dve.wait(e)
        e = dve.tick(V.tensor_tensor(acc[:], acc[:], bcast(bout[:], 1, NT), ALU.add))
        dve.wait(e)
        dve.tick(V.tensor_tensor(acc[:], acc[:], xn[:], ALU.add))
        p.meet()


def transformer(p, d, sb, ps, load, acc, xn, xs, ident, identb):
    pe, dve, act, pool, sp = p.engines
    TE, V, A, G, S = p.nc.tensor, p.nc.vector, p.nc.scalar, p.nc.gpsimd, p.nc.sync
    NB = NT // TB
    c = ExitStack()
    with c:
        ys = sb("ys", [P, NT + 1, P], c=c)
        wqkv = sb("wqkv", [P, 3 * INNER], c=c)
        wo = sb("wo", [P, INNER // P, P], c=c)
        w1 = sb("w1", [P, 2 * FI], c=c)
        w2 = sb("w2", [P, 3, P], c=c)
        colA = sb("colA", [P, 2 + 6], c=c)
        b2 = sb("b2", [P, P], c=c)
        qks = sb("qks", [P, 4, DH], c=c)
        rotary = sb("rotary", [P, 4, DH], c=c)
        tab = sb("tab", [P, 4, DH], c=c)
        turn = sb("turn", [P, P], c=c)
        band = sb("band", [P, NB, 2 * KW], BF16, c=c)
        band32 = sb("band32", [P, NB, 2 * KW], c=c)
        xc = sb("xc", [P, TB, P], c=c)
        xcT = sb("xcT", [P, TB * P], c=c)
        half = sb("half", [P, 1], c=c)
        uc = sb("uc", [P, 2, 512], c=c)
        sq = sb("sq", [P, 2, 512], c=c)
        ra = sb("ra", [P, 2, 4, 512], c=c)
        rb = sb("rb", [P, 2, 512], c=c)
        ss = sb("ss", [P, 2, 4, 8], c=c)
        rn = sb("rn", [P, 2, 4, 8], c=c)
        qT = sb("qT", [P, 2, 8, P], c=c)
        kT = sb("kT", [P, 2, 8, KW], c=c)
        vs = sb("vs", [P, 2, H, DH + 1], c=c)
        vh = sb("vh", [WIN, 2, H, DH + 1], c=c)
        pr = sb("pr", [P, 2, 4, KW], c=c)
        prT = sb("prT", [P, 2, 512], c=c)
        phT = sb("phT", [WIN, 2, P], c=c)
        nmx = sb("nmxl", [P, 2, 4], c=c)
        rec = sb("recl", [P, 2, 4], c=c)
        on = sb("on", [P, 2, INNER], c=c)
        oT = sb("oT", [P, INNER], c=c)
        hv = sb("hv", [P, 3, 512], c=c)
        bnst = sb("bnst", [P, TB, 6], c=c)
        mv = sb("mv", [P, TB, 2], c=c)
        rs = sb("rs", [P, TB], c=c)

        turn_in = load(turn[:], d["turn"], "turn")
        rotary_in = load(rotary[:], d["rotary"], "rotary")
        band_in = load(band32[:], d["band"], "band")
        dve.wait(band_in)
        dve.tick(V.tensor_copy(band[:], band32[:]))
        pool.tick(G.memset(ys[:, 0, :], 0.0))
        pool.tick(G.memset(half[:], -0.5))
        pool.tick(G.memset(vh[:], 0.0))
        pool.tick(G.memset(vs[:], 1.0))
        pool.tick(G.memset(kT[:], 0.0))
        pool.tick(G.memset(xc[:], 0.0))
        dve.tick(V.tensor_copy(xs[:, 1:, :], xn[:]))
        pe.wait(turn_in, band_in)
        dve.wait(rotary_in)
        p.meet()

        wA = p.dma("wA")
        wB = p.dma("wB")
        xc_in = p.dma("xc")
        vh_in = [p.dma("vh0"), p.dma("vh1")]

        def tiles(src, q):
            xc_in.tick(S.dma_start(xc[:, :, 0:DH], src[:, ds(q * TB + 1, TB), 0:DH]))
            xc_in.tick(S.dma_start(xc[1:P, :, DH:P], src[0:P - 1, ds(q * TB + 1, TB), DH:P]))
            return xc_in.tick(S.dma_start(xc[0:1, :, DH:P], src[P - 1:P, ds(q * TB, TB), DH:P]))

        with p.loop(L, **LAYER) as l:
            def row(name):
                return d[name][ds(l, 1)]

            wA.tick(S.dma_start(wqkv[:], row("lwqkv").rearrange("a p n -> p (a n)")))
            wA.tick(S.dma_start(wo[:], row("lwo").rearrange("a (c p) n -> p (a c) n", p=P)))
            wA_in = wA.tick(S.dma_start(qks[:].rearrange("p a b -> p (a b)"), row("qks").rearrange("a n -> (a n)").partition_broadcast(P)))
            wB.tick(S.dma_start(w1[:], row("lw1").rearrange("a p n -> p (a n)")))
            for j, (o, w) in enumerate(FCH):
                wB.tick(S.dma_start(w2[0:w, j, :], d["lw2"][ds(l, 1), o:o + w, :].rearrange("a p n -> p (a n)")))
            wB.tick(S.dma_start(colA[:], row("cols1").rearrange("a p n -> p (a n)")))
            wB_in = wB.tick(S.dma_start(b2[:], row("lb2").rearrange("a n -> (a n)").partition_broadcast(P)))
            dve.wait(wA_in)
            dve.tick(V.tensor_tensor(tab[:], rotary[:], qks[:], ALU.mult))
            pe.wait(wA_in, wB_in)
            act.wait(wB_in)
            dve.wait(wB_in)

            with p.loop(NB, **ATTN) as q:
                got = tiles(xs, q)
                pe.wait(got)
                for t in range(TB):
                    mm = TE.transpose(ps[:, 0, t * P:(t + 1) * P], xc[:, t, :], ident[:])
                e = pe.tick(mm)
                act.wait(e)
                xcT_ready = act.tick(A.activation(xcT[:], ps[:, 0, :], ACT.Copy))
                pe.wait(xcT_ready)

                free_s, free_qkv, free_o, free_t = [None, None], None, None, [None, None]
                free_uc = [[], []]
                free_sq, free_rb, free_pr, free_prT = [None, None], [None, None], [None, None], [None, None]
                free_phT, free_ra, free_qT, free_on, free_oT = [None, None], {}, None, [None, None], None
                n_t, rows, v_ready, vh_ready, kT_ready, on_ready, v_used, vh_used, qT_ready = 0, {}, {}, {}, {}, {}, {}, {}, {}
                free_k = {}

                def t_bank():
                    nonlocal n_t
                    n_t += 1
                    r = n_t % 2
                    pe.wait(free_t[r])
                    return r, ps[:, 6 + r, :]

                def project(t, w):
                    nonlocal free_qkv
                    b = t % 2
                    pe.wait(free_qkv)
                    bank = ps[:, 4, :]
                    done = pe.tick(TE.matmul(bank, xcT[:, t * P:(t + 1) * P], wqkv[:, w * 512:(w + 1) * 512], start=True, stop=True))
                    heads = bank.rearrange("p (h d) -> p h d", d=DH)
                    if w >= 4:
                        act.wait(done, v_used.get(b), vh_ready.get(t - 1))
                        v_ready[t] = act.tick(A.activation(vs[:, b, (w - 4) * 8:(w - 3) * 8, 0:DH], heads, ACT.Copy))
                        free_qkv = v_ready[t]
                        return
                    r = w % 2
                    act.wait(done, *free_uc[r])
                    out = free_qkv = act.tick(A.activation(uc[:, r, :], bank, ACT.Copy))
                    act.wait(out, free_sq[r])
                    squared = act.tick(A.activation(sq[:, r, :], uc[:, r, :], ACT.Square))
                    heads = uc[:, r, :].rearrange("p (h d) -> p h d", d=DH)
                    cos, sin = tab[:, w // 2 * 2, :], tab[:, w // 2 * 2 + 1, :]
                    out_a = ra[:, b, w, :].rearrange("p (h d) -> p h d", d=DH)
                    out_b = rb[:, r, :].rearrange("p (h d) -> p h d", d=DH)
                    dve.wait(out, free_ra.get((b, w)), free_rb[r])
                    V.tensor_tensor(out_a, heads, bcast(cos, 1, 8), ALU.mult)
                    V.tensor_tensor(out_b[:, :, 0:32], heads[:, :, 32:64], bcast(sin[:, 0:32], 1, 8), ALU.mult)
                    turned = dve.tick(V.tensor_tensor(out_b[:, :, 32:64], heads[:, :, 0:32], bcast(sin[:, 32:64], 1, 8), ALU.mult))
                    free_uc[r] = [turned, squared]
                    dve.wait(squared)
                    free_sq[r] = dve.tick(V.tensor_reduce(ss[:, b, w, :], sq[:, r, :].rearrange("p (h d) -> p h d", d=DH), X_AXIS, ALU.add))
                    pool.wait(turned)
                    e = free_rb[r] = pool.tick(G.tensor_tensor(ra[:, b, w, :], ra[:, b, w, :], rb[:, r, :], ALU.add))
                    pool.wait(free_sq[r])
                    e = pool.tick(G.tensor_scalar(rn[:, b, w, :], ss[:, b, w, :], 1e-24, None, ALU.max))
                    pool.wait(e)
                    e = pool.tick(G.tensor_tensor(rn[:, b, w, :], rn[:, b, w, :], half[:].broadcast_to([P, 8]), ALU.pow))
                    pool.wait(e)
                    rows[t, w] = pool.tick(G.tensor_tensor(out_a, out_a, bcast(rn[:, b, w, :], 2, DH), ALU.mult))

                def turn_rows(t):
                    nonlocal free_qT
                    b = t % 2
                    for w in range(4):
                        r, bank = t_bank()
                        pe.wait(rows[t, w])
                        for j in range(4):
                            mm = TE.transpose(bank[:, j * P:(j + 1) * P], ra[:, b, w, j * P:(j + 1) * P], ident[:])
                        done = free_ra[b, w] = pe.tick(mm)
                        act.wait(done, free_k.get(b), free_k.get(1 - b))
                        if w < 2:
                            to = qT[:, b, 4 * w:4 * w + 4, :]
                        else:
                            to = kT[:, b, 4 * w - 8:4 * w - 4, WIN:KW]
                        qT_ready[t] = free_t[r] = act.tick(A.activation(to, bank.rearrange("p (j n) -> p j n", n=P), ACT.Copy))
                    r, bank = t_bank()
                    pe.wait(kT_ready.get(t - 1))
                    done = pe.tick(TE.matmul(bank[:, 0:8 * WIN], turn[:], kT[:, 1 - b, :, P:KW], start=True, stop=True))
                    free_k[1 - b] = done
                    dve.wait(done)
                    kT_ready[t] = free_t[r] = dve.tick(V.tensor_copy(kT[:, b, :, 0:WIN], bank[:, 0:8 * WIN].rearrange("p (j n) -> p j n", n=WIN)))

                def fetch_before(t):
                    b = t % 2
                    sp.wait(v_ready.get(t - 1), vh_used.get(b))
                    vh_ready[t] = vh_in[b].tick(S.dma_start(vh[:, b, :, :], vs[P - WIN:P, 1 - b, :, :]))

                def scores(t, g):
                    b, r = t % 2, g % 2
                    pe.wait(free_s[r], qT_ready[t], kT_ready[t])
                    m = band[:, ds(q, 1), :] if t == 0 else band[:, NB - 1, :]
                    for o in range(2):
                        TE.matmul(ps[:, 2 * r + o, 0:2 * KW], identb[:], m.rearrange("p a n -> p (a n)") if t == 0 else m,
                                  start=True, stop=False, skip_group_check=True)
                    for pair in range(2):
                        for o in range(2):
                            j = 2 * g + pair
                            mm = TE.matmul(ps[:, 2 * r + o, pair * KW:(pair + 1) * KW], qT[o * DH:(o + 1) * DH, b, j, :], kT[o * DH:(o + 1) * DH, b, j, :],
                                           start=False, stop=pair == 1, skip_group_check=True)
                    done = pe.tick(mm)
                    dve.wait(done)
                    sc = ps[:, 2 * r:2 * r + 2, 0:2 * KW].rearrange("p o (a n) -> p o a n", a=2)
                    e = dve.tick(V.tensor_reduce(nmx[:, r, :].rearrange("p (o a) -> p o a", o=2), sc, X_AXIS, ALU.max, negate=True))
                    act.wait(e, free_pr[r])
                    for j in range(4):
                        ins = A.activation(pr[:, r, j, :], sc[:, j // 2, j % 2, :], ACT.Exp, bias=nmx[:, r, j:j + 1])
                    free_s[r] = act.tick(ins)
                    return free_s[r]

                def weigh(t, g, prob_ready):
                    nonlocal free_o
                    b, r = t % 2, g % 2
                    s, bank = t_bank()
                    pe.wait(prob_ready)
                    for j in range(4):
                        mm = TE.transpose(bank[:, j * P:(j + 1) * P], pr[:, r, j, WIN:KW], ident[:])
                    done = pe.tick(mm)
                    dve.wait(done, free_prT[r])
                    own = free_t[s] = dve.tick(V.tensor_copy(prT[:, r, :], bank))
                    s, bank = t_bank()
                    pe.settle()
                    for j in range(4):
                        mm = TE.transpose(bank[0:WIN, j * WIN:(j + 1) * WIN], pr[0:WIN, r, j, 0:WIN], ident[0:WIN, 0:WIN])
                    done = free_pr[r] = pe.tick(mm)
                    dve.wait(done)
                    before = free_t[s] = dve.tick(V.tensor_copy(phT[:, r, :], bank[0:WIN, 0:P]))
                    pe.wait(own, before, v_ready[t], vh_ready[t], free_o)
                    o_bank = ps[:, 5, 0:4 * (DH + 1)]
                    for j in range(4):
                        TE.matmul(o_bank[:, j * (DH + 1):(j + 1) * (DH + 1)], prT[:, r, j * P:(j + 1) * P], vs[:, b, 4 * g + PERM[j], :],
                                  start=j == 0, stop=False, skip_group_check=True)
                    for j in range(4):
                        mm = TE.matmul(o_bank[0:WIN, j * (DH + 1):(j + 1) * (DH + 1)], phT[:, r, j * WIN:(j + 1) * WIN], vh[:, b, 4 * g + PERM[j], :],
                                       start=False, stop=j == 3, skip_group_check=True)
                    done = free_prT[r] = v_used[b] = vh_used[b] = pe.tick(mm)
                    o4 = o_bank.rearrange("p (j d) -> p j d", j=4)
                    dve.wait(done, free_on[b])
                    e = dve.tick(V.reciprocal(rec[:, r, :], o4[:, :, DH]))
                    dve.wait(e)
                    to = on[:, b, 4 * g * DH:4 * (g + 1) * DH].rearrange("p (a o d) -> p o a d", a=2, o=2)
                    free_o = on_ready[t] = dve.tick(V.tensor_tensor(to, o4[:, :, 0:DH].rearrange("p (o a) d -> p o a d", o=2),
                                                                    bcast(rec[:, r, :].rearrange("p (o a) -> p o a", o=2), 3, DH), ALU.mult))

                def finish(t):
                    nonlocal free_oT
                    b = t % 2
                    for w in range(2):
                        r, bank = t_bank()
                        pe.wait(on_ready[t])
                        for j in range(4):
                            mm = TE.transpose(bank[:, j * P:(j + 1) * P], on[:, b, (4 * w + j) * P:(4 * w + j + 1) * P], ident[:])
                        done = free_on[b] = pe.tick(mm)
                        act.wait(done, free_oT)
                        e = free_t[r] = act.tick(A.activation(oT[:, w * 512:(w + 1) * 512], bank, ACT.Copy))
                    r, bank = t_bank()
                    pe.wait(e)
                    for j in range(8):
                        mm = TE.matmul(bank[:, 0:P], oT[:, j * P:(j + 1) * P], wo[:, j, :], start=j == 0, stop=j == 7)
                    done = free_oT = pe.tick(mm)
                    dve.wait(done)
                    free_t[r] = dve.tick(V.tensor_tensor(ys[:, ds(q * TB + 1 + t, 1), :], xs[:, ds(q * TB + 1 + t, 1), :], bank[:, 0:P].unsqueeze(1), ALU.add))

                fetch_before(0)
                for w in range(6):
                    project(0, w)
                for t in range(TB):
                    turn_rows(t)
                    if t:
                        finish(t - 1)
                    if t + 1 < TB:
                        fetch_before(t + 1)
                    ahead = list(range(6)) if t + 1 < TB else []
                    held = None
                    for g in range(4):
                        nxt = (t, g, scores(t, g))
                        for w in ahead[:(2, 2, 1, 1)[g]]:
                            project(t + 1, w)
                        ahead = ahead[(2, 2, 1, 1)[g]:]
                        if held:
                            weigh(*held)
                        held = nxt
                    weigh(*held)
                finish(TB - 1)

            with p.loop(NB, **FFN) as q:
                got = tiles(ys, q)
                dve.wait(got)
                for t in range(TB):
                    e = dve.tick(V.bn_stats(bnst[:, t, :], xc[:, t, :]))
                dve.wait(e)
                dve.settle()
                for t in range(TB):
                    e = dve.tick(V.bn_aggr(mv[:, t, :], bnst[:, t, :]))
                pool.wait(e)
                e = pool.tick(G.tensor_scalar(rs[:], mv[:, :, 1], EPS, None, ALU.add))
                pool.wait(e)
                rs_ready = pool.tick(G.tensor_tensor(rs[:], rs[:], half[:].broadcast_to([P, TB]), ALU.pow))
                dve.wait(rs_ready)
                for t in range(TB):
                    e = dve.tick(V.tensor_scalar(xc[:, t, :], xc[:, t, :], mv[:, t, 0:1], rs[:, t:t + 1], ALU.subtract, ALU.mult))
                pe.wait(e)
                for t in range(TB):
                    mm = TE.transpose(ps[:, 0, t * P:(t + 1) * P], xc[:, t, :], ident[:])
                e = pe.tick(mm)
                act.wait(e)
                e = act.tick(A.activation(xcT[:], ps[:, 0, :], ACT.Identity, bias=colA[:, 1:2], scale=colA[:, 0:1]))
                pe.wait(e)
                for j, (o, w) in enumerate(FCH):
                    gate, val = ps[0:w, 1 + 2 * j, :], ps[0:w, 2 + 2 * j, :]
                    TE.matmul(gate, w1[:, FI + o:FI + o + w], xcT[:], start=True, stop=True)
                    e = pe.tick(TE.matmul(val, w1[:, o:o + w], xcT[:], start=True, stop=True))
                    act.wait(e)
                    e = act.tick(A.activation(hv[0:w, j, :], gate, ACT.Gelu, bias=colA[0:w, 2 + j:3 + j]))
                    dve.wait(e)
                    e = dve.tick(V.scalar_tensor_tensor(hv[0:w, j, :], val, colA[0:w, 5 + j:6 + j], hv[0:w, j, :], ALU.add, ALU.mult))
                pe.wait(e)
                for t in range(TB):
                    for j, (o, w) in enumerate(FCH):
                        mm = TE.matmul(ps[:, 7, t * P:(t + 1) * P], hv[0:w, j, t * P:(t + 1) * P], w2[0:w, j, :], start=j == 0, stop=j == 2,
                                       skip_group_check=True)
                e = pe.tick(mm)
                to = xs[:, ds(q * TB + 1, TB), :]
                dve.wait(e)
                e = dve.tick(V.tensor_tensor(to, ys[:, ds(q * TB + 1, TB), :], ps[:, 7, :].rearrange("p (t d) -> p t d", d=P), ALU.add))
                dve.wait(e)
                dve.tick(V.tensor_tensor(to, to, bcast(b2[:], 1, TB), ALU.add))
        p.meet()
        dve.tick(V.tensor_tensor(acc[:], acc[:], xs[:, 1:, :], ALU.add))
        p.meet()


ATTN = dict(pe=121, dve=120, act=81, pool=64, xc=3, vh0=2, vh1=2)
FFN = dict(pe=5, dve=17, act=4, pool=2, xc=3)
LAYER = dict(pe=504, dve=549, act=340, pool=264, wA=3, wB=6, xc=24, vh0=8, vh1=8)


def constants():
    c = {"ident": np.eye(P, dtype=np.float32), }
    q, k = np.arange(P)[:, None], np.arange(P)[None, :]
    c["causal"] = np.where(k > q, -1e30, 0.0).astype(np.float32)
    c["lower"] = (np.arange(NE)[None, :] < np.arange(NE)[:, None]).astype(np.float32)
    half = np.arange(0, DH, 2, dtype=np.float64)
    freq = np.tile(1.0 / 10000.0 ** (half / DH), 2)
    base = np.tile((half + 0.4 * DH) / (1.4 * DH), 2)
    pos = np.arange(P, dtype=np.float64)[:, None] - P // 2
    scale = base[None, :] ** (pos / (WIN // 2))
    sign = np.where(np.arange(DH) < DH // 2, -1.0, 1.0)
    cos, sin = np.cos(pos * freq), np.sin(pos * freq) * sign
    c["rotary"] = np.stack([8 * cos * scale, 8 * sin * scale, cos / scale, sin / scale], 1).astype(np.float32)
    phi = -P * freq
    turn = np.zeros((2 * DH, 2 * DH))
    fac = base ** (P / (WIN // 2))
    for h in range(2):
        for f in range(DH):
            o = h * DH
            turn[o + f, o + f] = np.cos(phi[f]) * fac[f]
            turn[o + (f + DH // 2) % DH, o + f] = sign[f] * np.sin(phi[f]) * fac[f]
    c["turn"] = turn.astype(np.float32)
    j = np.arange(KW)[None, :] - WIN
    keep = (j <= q) & (j >= q - WIN)
    rows = [np.where(keep & (j >= 0), 0.0, -1e30), np.where(keep, 0.0, -1e30)]
    c["band"] = np.stack([np.tile(r, (1, 2)) for r in [rows[0]] + [rows[1]] * (NT // TB - 1)], 1).astype(np.float32)
    return c


def kernel(**inputs):
    import concourse.bacc as bacc
    from concourse.bass_utils import run_bass_kernel_spmd

    a = {k: np.asarray(v) for k, v in inputs.items()}
    wkqv, bkqv = a["L0_attn_Wkqv"], a["L0_attn_bkqv"]
    host = constants()
    host.update({
        "x": a["L0_attn_x"][0],
        "wkq": wkqv[:, :, :2 * P], "bkq": bkqv[:, :2 * P].reshape(H0, 2, P).transpose(0, 2, 1),
        "wv": wkqv[:, :, 2 * P:].transpose(1, 0, 2).reshape(P, P), "bv": bkqv[:, 2 * P:].reshape(P),
        "wp": a["L0_attn_Wp"], "bp": a["L0_attn_bp"], "wg": a["L0_ffn_Wg"], "we": a["L0_ffn_We"],
    })
    col = lambda n: a["L1_attn_" + n].reshape(-1, P).T
    host.update({
        "win": a["L1_attn_W_in"].T, "wx": a["L1_attn_W_x"].T, "wdt": a["L1_attn_W_dt"].T, "wout": a["L1_attn_W_out"].T,
        "taps": a["L1_attn_conv_w"], "alog": a["L1_attn_A_log"], "bout": a["L1_attn_b_out"],
        "cols": np.concatenate([col(n) for n in ("gamma", "beta", "b_in", "conv_b", "b_dt", "D_param")], 1),
    })
    qs, ks = a["L1_ffn_q_scale"], a["L1_ffn_k_scale"]
    turned = lambda v: np.concatenate([v[:, DH // 2:], v[:, :DH // 2]], 1)
    b1 = np.zeros((L, P, 6), np.float32)
    for j, (o, w) in enumerate(FCH):
        b1[:, :w, j] = a["L1_ffn_b1"][:, FI + o:FI + o + w]
        b1[:, :w, 3 + j] = a["L1_ffn_b1"][:, o:o + w]
    host.update({
        "lwqkv": a["L1_ffn_Wqkv"], "lwo": a["L1_ffn_Wo"], "lw1": a["L1_ffn_W1"], "lw2": a["L1_ffn_W2"], "lb2": a["L1_ffn_b2"],
        "qks": np.concatenate([qs, turned(qs), ks, turned(ks)], 1),
        "cols1": np.concatenate([a["L1_ffn_ln_g"][:, :, None], a["L1_ffn_ln_b"][:, :, None], b1], 2),
    })
    nc = bacc.Bacc("TRN2", target_bir_lowering=False, num_devices=1)
    arrays, aps = {}, {}
    for name, v in host.items():
        v = np.ascontiguousarray(v)
        arrays[name + "_dram"] = v
        aps[name] = nc.dram_tensor(name + "_dram", v.shape, mybir.dt.from_np(v.dtype), kind="ExternalInput").ap()
    out = nc.dram_tensor("out_dram", (1, T, P), F32, kind="ExternalOutput").ap()
    build(nc, aps, out[0])
    return run_bass_kernel_spmd(nc, [arrays], core_ids=[0]).results[0]["out_dram"]
```

```python
from contextlib import ExitStack, contextmanager

import numpy as np

import concourse.bass as bass
from concourse import mybir

F32 = mybir.dt.float32
BF16 = mybir.dt.bfloat16
ALU = mybir.AluOpType
ACT = mybir.ActivationFunctionType
X_AXIS = mybir.AxisListType.X
ds = bass.ds

STOP = 99

P = 128
T = 2048
NT = T // P
EPS = 1e-5
H0 = 16
DV0 = 8
VW = DV0 + 1
KB = 1024
NE = 8
ED = 256
ET = ED // P
NS = 16
KC = 15
R = 8
RX = R + 2 * NS
L = 6
H = 16
DH = 64
INNER = H * DH
WIN = 32
FI = 341
FCH = [(0, 128), (128, 128), (256, FI - 256)]
TB = 4
KW = WIN + P
PERM = [0, 2, 1, 3]


class Counter:

    def __init__(self, nc, eng, name, step=1):
        self.eng, self.name, self.step = eng, name, step
        self.sem = nc.alloc_semaphore("s_" + name)
        self.base, self.k, self.seen, self.alone, self.spare = 0, 0, {}, False, None

    def tick(self, ins):
        ins.then_inc(self.sem, self.step)
        self.k += self.step
        return self.now()

    def now(self):
        return (self, self.k)

    def wait(self, *events):
        for ev in events:
            if ev is None:
                continue
            c, k = ev
            if k > self.seen.get(c.name, -1 << 40):
                self.eng.wait_ge(c.sem, c.base + k)
                self.seen[c.name] = k
                if self.alone and not isinstance(c.base, int):
                    self.settle()

    def settle(self):
        self.eng.sem_inc(self.spare, 1)


class Program:
    def __init__(self, nc):
        self.nc = nc
        self.pe = Counter(nc, nc.tensor, "pe")
        self.dve = Counter(nc, nc.vector, "dve")
        self.act = Counter(nc, nc.scalar, "act")
        self.pool = Counter(nc, nc.gpsimd, "pool")
        self.sp = Counter(nc, nc.sync, "sp")
        self.engines = [self.pe, self.dve, self.act, self.pool, self.sp]
        self.counters = list(self.engines)
        self.sp.alone = self.pool.alone = True
        for e in self.engines:
            e.spare = nc.alloc_semaphore("spare_" + e.name)

    def dma(self, name):
        c = Counter(self.nc, self.nc.sync, name, 16)
        self.counters.append(c)
        return c

    def forget(self):
        for c in self.counters:
            c.seen = {}

    @contextmanager
    def loop(self, n, **per):
        kept = [(c.base, c.k) for c in self.counters]
        for e in self.engines:
            if not isinstance(e.base, int):
                e.settle()
        with self.nc.Fori(0, n) as i:
            for c in self.counters:
                gain = per.get(c.name, 0) * c.step
                c.base = c.base + c.k + i * gain if gain else c.base + c.k
                c.k = 0
            self.forget()
            self.meet()
            yield i
            gained = {c.name: c.k // c.step for c in self.counters if c.k}
            assert gained == {a: b for a, b in per.items() if b}, f"the loop's counts are {gained}"
        for c, (base, k) in zip(self.counters, kept):
            c.base, c.k = base, k + n * per.get(c.name, 0) * c.step
        self.forget()

    def pipeline(self, n, body, state):
        def moved(by):
            return {a: e and (e[0], e[1] + by[e[0].name]) for a, e in state.items()}

        start = {c.name: c.k for c in self.counters}
        body(0, state, True)
        ends = {c.name: c.k for c in self.counters}
        gain = {a: ends[a] - start.get(a, 0) for a in ends}
        first = moved({a: -v for a, v in ends.items()})
        state.update(first)
        kept = [(c.base, c.k) for c in self.counters]
        for e in self.engines:
            if not isinstance(e.base, int):
                e.settle()
        with self.nc.Fori(1, n - 1) as i:
            for c in self.counters:
                g = gain[c.name]
                c.base = c.base + (c.k - g) + i * g if g else c.base + c.k
                c.k = 0
            self.forget()
            body(i, state, True)
            assert {c.name: c.k for c in self.counters} == gain
            state.update(moved({a: -v for a, v in gain.items()}))
            assert state == first, "the turns differ"
        for c, (base, k) in zip(self.counters, kept):
            c.base, c.k = base, k + (n - 2) * gain[c.name]
        state.update(moved({c.name: c.k for c in self.counters}))
        self.forget()
        body(n - 1, state, False)

    def meet(self):
        for e in self.engines:
            e.seen = {}
            for c in self.engines:
                if c.k > 0 or not isinstance(c.base, int) or c.base > 0:
                    e.wait(c.now())


def bcast(ap, at, n):
    shape = list(ap.shape)
    return ap.unsqueeze(at).broadcast_to(shape[:at] + [n] + shape[at:])


def layer_norm(p, src, dst, st, after, scratch):
    dve, act = p.dve, p.act
    V, A = p.nc.vector, p.nc.scalar
    dve.wait(*after)
    e = dve.tick(V.tensor_reduce(st[:, 0, :], src, X_AXIS, ALU.add))
    dve.wait(e)
    e = dve.tick(V.tensor_scalar(st[:, 1, :], st[:, 0, :], -1.0 / P, None, ALU.mult))
    dve.wait(e)
    e = dve.tick(V.tensor_tensor(dst, src, bcast(st[:, 1, :], 2, P), ALU.add))
    act.wait(e)
    e = act.tick(A.activation(scratch, dst, ACT.Square))
    dve.wait(e)
    e = dve.tick(V.tensor_reduce(st[:, 2, :], scratch, X_AXIS, ALU.add))
    dve.wait(e)
    e = dve.tick(V.tensor_scalar(st[:, 3, :], st[:, 2, :], 1.0 / P, EPS, ALU.mult, ALU.add))
    act.wait(e)
    e = act.tick(A.activation(st[:, 0, :], st[:, 3, :], ACT.Sqrt))
    dve.wait(e)
    e = dve.tick(V.reciprocal(st[:, 1, :], st[:, 0, :]))
    dve.wait(e)
    return dve.tick(V.tensor_tensor(dst, dst, bcast(st[:, 1, :], 2, P), ALU.mult))


def build(nc, d, out):
    p = Program(nc)
    pe, dve, act, pool, sp = p.engines
    TE, V, A, G, S = nc.tensor, nc.vector, nc.scalar, nc.gpsimd, nc.sync
    ctx = ExitStack()
    with ctx:
        def sb(name, shape, dt=F32, c=ctx):
            return c.enter_context(nc.sbuf_tensor(name, shape, dt))

        ps = ctx.enter_context(nc.psum_tensor("ps", [P, 8, 512], F32))

        def load(dst, src, name, after=()):
            c = p.dma(name)
            sp.wait(*after)
            return c.tick(S.dma_start(dst, src))

        ident = sb("ident", [P, P])
        identb = sb("identb", [P, P], BF16)
        acc = sb("acc", [P, NT, P])
        xn = sb("xn", [P, NT, P])
        xs = sb("xs", [P, NT + 2, P])
        st = sb("st", [P, 4, NT])

        x0 = xs[:, 1:NT + 1, :]
        x_in = load(x0, d["x"].rearrange("(t p) d -> p t d", p=P), "x")
        id_in = load(ident[:], d["ident"], "ident")
        dve.wait(id_in)
        idb_in = dve.tick(V.tensor_copy(identb[:], ident[:]))
        pool.tick(G.memset(xs[:, 0, :], 0.0))
        pool.tick(G.memset(xs[:, NT + 1, :], 0.0))
        outs = p.dma("out")

        def transpose_tiles(src, dst, after, scale=None, bias=None, banks=(0, 1)):
            free, last = [None, None], None
            for q in range(NT // 4):
                bank = ps[:, banks[q % 2], :]
                pe.wait(id_in, *after, free[q % 2])
                for c in range(4):
                    mm = TE.transpose(bank[:, c * P:(c + 1) * P], src[:, 4 * q + c, :], ident[:])
                done = pe.tick(mm)
                to = dst[:, q * 512:(q + 1) * 512]
                if scale is None and q % 2:
                    dve.wait(done)
                    free[1] = dve.tick(V.tensor_copy(to, bank))
                else:
                    act.wait(done)
                    if scale is None:
                        ins = A.activation(to, bank, ACT.Copy)
                    else:
                        ins = A.activation(to, bank, ACT.Identity, bias=bias, scale=scale)
                    free[q % 2] = act.tick(ins)
            return free

        with ExitStack() as c0:
            xnT = sb("xnT", [P, T], c=c0)
            valL = sb("values", [P, NT, H0, VW], c=c0)
            wv = sb("wv", [P, P], c=c0)
            bv = sb("bv", [P, P], c=c0)
            wp = sb("wp", [P, P], c=c0)
            bp = sb("bp", [P, P], c=c0)
            causal = sb("causal", [P, P], BF16, c=c0)
            nmaxL = sb("nmaxL", [P, H0, 24], c=c0)
            oL = sb("oL", [P, H0, 24, VW], c=c0)
            wv_in = load(wv[:], d["wv"], "wv")
            bv_in = load(bv[:], d["bv"].partition_broadcast(P), "bv")
            causal32 = sb("causal32", [P, P], c=c0)
            e = load(causal32[:], d["causal"], "causal")
            dve.wait(e)
            causal_in = dve.tick(V.tensor_copy(causal[:], causal32[:]))
            wp_in = load(wp[:], d["wp"], "wp")
            bp_in = load(bp[:], d["bp"].partition_broadcast(P), "bp")
            with ExitStack() as cm:
                wg = sb("wg", [P, NE], c=cm)
                we = sb("we", [P, NE * P], c=cm)
                lower = sb("lower", [P, NE, NE], c=cm)
                wg_in = load(wg[:], d["wg"], "wg")
                we_in = load(we[:].rearrange("p (e m) -> p e m", e=NE), d["we"].rearrange("e d m -> d e m"), "we")
                lower_in = load(lower[:], d["lower"].partition_broadcast(P), "lower")
                gate = sb("gate", [P, NT, NE], c=cm)
                g1 = sb("g1", [P, NT], c=cm)
                g2 = sb("g2", [P, NT, NE], c=cm)
                cmp1 = sb("cmp1", [P, NT, NE, NE], c=cm)
                cmp2 = sb("cmp2", [P, NT, NE, NE], c=cm)
                xe = sb("xe", [P, 2, NE, P], c=cm)

                e = layer_norm(p, x0, xn[:], st[:], [x_in], acc[:])
                xnT_ready = transpose_tiles(xn, xnT, [e])
                ones_set = pool.tick(G.memset(valL[:, :, :, DV0], 1.0))

                free = [None, None]
                for q in range(4):
                    bank = ps[:, 2 + q % 2, :]
                    pe.wait(wv_in, *xnT_ready, free[q % 2])
                    for c in range(4):
                        t = 4 * q + c
                        mm = TE.matmul(bank[:, c * P:(c + 1) * P], xnT[:, t * P:(t + 1) * P], wv[:], start=True, stop=True)
                    done = pe.tick(mm)
                    dve.wait(done, bv_in)
                    for c in range(4):
                        t = 4 * q + c
                        ins = V.tensor_tensor(valL[:, t, :, 0:DV0], bank[:, c * P:(c + 1) * P].rearrange("p (h v) -> p h v", h=H0),
                                              bv[:].rearrange("p (h v) -> p h v", h=H0), ALU.add)
                    free[q % 2] = dve.tick(ins)

                glog = ps[:, 4, 0:NT * NE].rearrange("p (t e) -> p t e", e=NE)
                pe.wait(wg_in)
                for t in range(NT):
                    mm = TE.matmul(glog[:, t, :], xnT[:, t * P:(t + 1) * P], wg[:], start=True, stop=True)
                done = pe.tick(mm)
                dve.wait(done)
                e = dve.tick(V.tensor_reduce(g1[:], glog, X_AXIS, ALU.max))
                dve.wait(e)
                e = dve.tick(V.tensor_tensor(g2[:], glog, bcast(g1[:], 2, NE), ALU.subtract))
                act.wait(e)
                e = act.tick(A.activation(g2[:], g2[:], ACT.Exp))
                dve.wait(e)
                e = dve.tick(V.tensor_reduce(g1[:], g2[:], X_AXIS, ALU.add))
                dve.wait(e)
                e = dve.tick(V.reciprocal(g1[:], g1[:]))
                dve.wait(e)
                e = dve.tick(V.tensor_tensor(gate[:], g2[:], bcast(g1[:], 2, NE), ALU.mult))
                mine, other = bcast(gate[:], 3, NE), bcast(gate[:], 2, NE)
                dve.wait(e, lower_in)
                V.tensor_tensor(cmp1[:], other, mine, ALU.is_gt)
                e = dve.tick(V.tensor_tensor(cmp2[:], other, mine, ALU.is_equal))
                dve.wait(e)
                e = dve.tick(V.tensor_tensor(cmp2[:], cmp2[:], bcast(lower[:], 1, NT), ALU.mult))
                dve.wait(e)
                e = dve.tick(V.tensor_tensor(cmp1[:], cmp1[:], cmp2[:], ALU.add))
                dve.wait(e)
                e = dve.tick(V.tensor_reduce(g2[:], cmp1[:], X_AXIS, ALU.add))
                dve.wait(e)
                e = dve.tick(V.tensor_scalar(g2[:], g2[:], 1.5, None, ALU.is_lt))
                dve.wait(e)
                e = dve.tick(V.tensor_tensor(gate[:], gate[:], g2[:], ALU.mult))
                dve.wait(e)
                e = dve.tick(V.tensor_reduce(g1[:], gate[:], X_AXIS, ALU.add))
                dve.wait(e)
                e = dve.tick(V.tensor_scalar(g1[:], g1[:], 1e-9, None, ALU.add))
                dve.wait(e)
                e = dve.tick(V.reciprocal(g1[:], g1[:]))
                dve.wait(e)
                gate_ready = dve.tick(V.tensor_tensor(gate[:], gate[:], bcast(g1[:], 2, NE), ALU.mult))
                free, pend = [None, None], [None, None]
                for t in range(NT):
                    b = t % 2
                    bank = ps[:, 2 * b:2 * b + 2, :]
                    pe.wait(we_in, free[b], dve.now())
                    for g in range(2):
                        mm = TE.matmul(bank[:, g, :], xnT[:, t * P:(t + 1) * P], we[:, g * 512:(g + 1) * 512], start=True, stop=True)
                    done = pe.tick(mm)
                    dve.wait(done, gate_ready, pend[b])
                    for g in range(2):
                        ins = V.tensor_tensor(xe[:, b, 4 * g:4 * g + 4, :], bank[:, g, :].rearrange("p (e m) -> p e m", e=4),
                                              bcast(gate[:, t, 4 * g:4 * g + 4], 2, P), ALU.mult)
                    free[b] = dve.tick(ins)
                    dve.wait(free[b])
                    e = dve.tick(V.tensor_reduce(acc[:, t, :], xe[:, b, :, :].rearrange("p e m -> p m e"), X_AXIS, ALU.add))
                    pool.wait(e)
                    pend[b] = pool.tick(G.tensor_tensor(acc[:, t, :], acc[:, t, :], x0[:, t, :], ALU.add))
                p.meet()

            with ExitStack() as ca:
                wh = sb("wh", [P, 2, 2 * P], c=ca)
                bh = sb("bh", [P, 2, 2], c=ca)
                bqs = sb("bqs", [P, 2], c=ca)
                kq = sb("kq", [P, 2, 2, T], c=ca)
                prob = sb("prob", [P, 2, KB], c=ca)
                probT = sb("probT", [P, 2, 512], c=ca)
                nmx = sb("nmx", [P, 2, 24], c=ca)
                w_in = [p.dma(f"wh{b}") for b in range(2)]
                units = [(g, 0, (g + 1) * P) for g in range(NT // 2)]
                for g in range(NT // 2, NT):
                    units += [(g, 0, KB), (g, KB, (g + 1) * P - KB)]
                o_banks = ps[:, 7, :]

                NU = len(units)
                st0 = dict.fromkeys(["proj", "out"] + [n + str(b) for n in ("s", "prob", "probT", "pt", "kept", "w", "bias", "kq", "e") for b in range(2)])

                def fetch(ev, b, head):
                    sp.wait(ev["kq%d" % b], ev["bias%d" % b])
                    w_in[b].tick(S.dma_start(wh[:, b, :], d["wkq"][head, :, :].rearrange("a d e -> d (a e)")))
                    ev["w%d" % b] = w_in[b].tick(S.dma_start(bh[:, b, :], d["bkq"][head, :, :].rearrange("a d e -> d (a e)")))

                def project(ev, b, n):
                    w, ch = n % 2, n // 2
                    if n == 0:
                        dve.wait(ev["w%d" % b])
                        ev["bias%d" % b] = dve.tick(V.tensor_scalar(bqs[:, b:b + 1], bh[:, b, 1:2], P ** -0.5, None, ALU.mult))
                    pe.wait(ev["w%d" % b], ev["proj"])
                    done = pe.tick(TE.matmul(ps[:, 6, :], wh[:, b, w * P:(w + 1) * P], xnT[:, ch * 512:(ch + 1) * 512], start=True, stop=True))
                    to = kq[:, b, w, ch * 512:(ch + 1) * 512]
                    act.wait(done, ev["bias%d" % b])
                    ev["proj"] = ev["kq%d" % b] = act.tick(A.activation(to, ps[:, 6, :], ACT.Identity, bias=(bh[:, b, 0:1], bqs[:, b:b + 1])[w],
                                                                        scale=(1.0, P ** -0.5)[w]))

                def scores(ev, b, u):
                    g, k0, nk = units[u]
                    s = u % 2
                    pe.wait(ev["s%d" % s], ev["kq%d" % b])
                    diag = k0 + nk == (g + 1) * P
                    for o in range(0, nk, 512):
                        w = min(512, nk - o)
                        mm = TE.matmul(ps[:, 2 * s + o // 512, 0:w], kq[:, b, 1, g * P:(g + 1) * P], kq[:, b, 0, k0 + o:k0 + o + w],
                                       start=True, stop=not (o + w == nk and diag), skip_group_check=True)
                    if diag:
                        j, o = (nk - P) // 512, (nk - P) % 512
                        mm = TE.matmul(ps[:, 2 * s + j, o:o + P], identb[:], causal[:], start=False, stop=True, skip_group_check=True)
                    done = pe.tick(mm)
                    sc = ps[:, 2 * s:2 * s + 2, :].rearrange("p a b -> p (a b)")[:, 0:nk]
                    dve.wait(done, ev["kept%d" % b])
                    e = dve.tick(V.tensor_reduce(nmx[:, b, u:u + 1], sc, X_AXIS, ALU.max, negate=True))
                    act.wait(e, ev["prob%d" % s])
                    ev["s%d" % s] = ev["e%d" % s] = act.tick(A.activation(prob[:, s, 0:nk], sc, ACT.Exp, bias=nmx[:, b, u:u + 1]))

                def turn_probs(ev, b, u, r):
                    g, k0, nk = units[u]
                    s, m = u % 2, min(4, nk // P - 4 * r)
                    pe.wait(ev["e%d" % s], ev["pt%d" % r])
                    for c in range(m):
                        mm = TE.transpose(ps[:, 4 + r, c * P:(c + 1) * P], prob[:, s, (4 * r + c) * P:(4 * r + c + 1) * P], ident[:])
                    done = ev["prob%d" % s] = pe.tick(mm)
                    eng = (act, dve)[r]
                    eng.wait(done, ev["probT%d" % r])
                    if r:
                        ins = V.tensor_copy(probT[:, r, 0:m * P], ps[:, 4 + r, 0:m * P])
                    else:
                        ins = A.activation(probT[:, r, 0:m * P], ps[:, 4 + r, 0:m * P], ACT.Copy)
                    ev["pt%d" % r] = eng.tick(ins)

                def values(ev, b, head, u, r):
                    g, k0, nk = units[u]
                    n = nk // P
                    m = min(4, n - 4 * r)
                    pe.wait(ev["pt%d" % r], ev["out"])
                    for c in range(m):
                        j = 4 * r + c
                        mm = TE.matmul(o_banks[:, 256 * b + u * VW:256 * b + (u + 1) * VW], probT[:, r, c * P:(c + 1) * P],
                                       valL[:, k0 // P + j, head, :], start=j == 0, stop=j == n - 1, skip_group_check=True)
                    ev["probT%d" % r] = pe.tick(mm)

                def two_heads(i, ev, more):
                    for b in range(2):
                        head = ds(2 * i + b, 1)
                        ahead = more or b == 0
                        if ahead:
                            fetch(ev, 1 - b, ds(2 * i + b + 1, 1))
                        for u in range(NU):
                            groups = range(-(-units[u][2] // 512))
                            for r in groups:
                                turn_probs(ev, b, u, r)
                            if ahead and u >= 6 and u % 2 == 0 and (u - 6) // 2 < 8:
                                project(ev, 1 - b, (u - 6) // 2)
                            if u + 2 < NU:
                                scores(ev, b, u + 2)
                            elif ahead:
                                scores(ev, 1 - b, u + 2 - NU)
                            for r in groups:
                                values(ev, b, head, u, r)
                        dve.wait(pe.now())
                        ev["out"] = dve.tick(V.tensor_copy(oL[:, head, :, :], o_banks[:, 256 * b:256 * b + NU * VW]))
                        ev["kept%d" % b] = dve.tick(V.tensor_copy(nmaxL[:, head, :], nmx[:, b, :]))

                fetch(st0, 0, ds(0, 1))
                for n in range(8):
                    project(st0, 0, n)
                for u in range(2):
                    scores(st0, 0, u)
                p.pipeline(H0 // 2, two_heads, st0)
                p.meet()

            with ExitStack() as cj:
                sa = sb("sa", [P, NT, H0, DV0], c=cj)
                saT = sb("saT", [P, T], c=cj)
                HN = NT // 2
                wgt = sb("wgt", [P, 2, H0, HN], c=cj)
                mn = sb("mn", [P, H0, HN], c=cj)
                o2 = sb("o2", [P, 2, H0, HN, VW], c=cj)
                rec = sb("rec", [P, H0, HN], c=cj)
                nm = [nmaxL[:, :, HN + j::2] for j in range(2)]
                ov = [oL[:, :, HN + j::2, :] for j in range(2)]
                e = dve.tick(V.tensor_tensor(mn[:], nm[0], nm[1], ALU.min))
                dve.wait(e)
                for j in range(2):
                    e = dve.tick(V.tensor_tensor(wgt[:, j], mn[:], nm[j], ALU.subtract))
                act.wait(e)
                e = act.tick(A.activation(wgt[:], wgt[:], ACT.Exp))
                dve.wait(e)
                for j in range(2):
                    e = dve.tick(V.tensor_tensor(o2[:, j], ov[j], bcast(wgt[:, j], 3, VW), ALU.mult))
                dve.wait(e)
                e = dve.tick(V.tensor_tensor(o2[:, 0], o2[:, 0], o2[:, 1], ALU.add))
                dve.wait(e)
                for half, o in ((0, oL[:, :, 0:HN, :]), (1, o2[:, 0])):
                    e = dve.tick(V.reciprocal(rec[:], o[:, :, :, DV0]))
                    dve.wait(e)
                    e = dve.tick(V.tensor_tensor(sa[:, half * HN:(half + 1) * HN, :, :].rearrange("p g h v -> p h g v"), o[:, :, :, 0:DV0],
                                                 bcast(rec[:], 3, DV0), ALU.mult))
                    dve.wait(e)
                saT_ready = transpose_tiles(sa[:].rearrange("p t h v -> p t (h v)"), saT, [e])
                pe.wait(*saT_ready, wp_in)
                for t in range(NT):
                    mm = TE.matmul(ps[:, 2 + t // 4, (t % 4) * P:(t % 4 + 1) * P], saT[:, t * P:(t + 1) * P], wp[:], start=True, stop=True, skip_group_check=True)
                done = pe.tick(mm)
                dve.wait(done, bp_in, pool.now())
                e = dve.tick(V.tensor_tensor(acc[:].rearrange("p (q c) d -> p q (c d)", q=4), acc[:].rearrange("p (q c) d -> p q (c d)", q=4), ps[:, 2:6, :], ALU.add))
                dve.wait(e)
                e = dve.tick(V.tensor_tensor(acc[:], acc[:], bcast(bp[:], 1, NT), ALU.add))
                e = layer_norm(p, acc[:], xn[:], st[:], [e], saT[:].rearrange("p (t d) -> p t d", d=P))
                p.meet()

        if STOP >= 2:
            mamba(p, d, sb, ps, load, acc, xn, st, ident, transpose_tiles)
        if STOP >= 3:
            transformer(p, d, sb, ps, load, acc, xn, xs, ident, identb)

        res = acc if STOP >= 2 else (acc if STOP == 1 else xn)
        S.dma_start(out.rearrange("(t p) d -> p t d", p=P), res[:]).then_inc(outs.sem, 16)
        S.wait_ge(outs.sem, 16)


def mamba(p, d, sb, ps, load, acc, xn, st, ident, transpose_tiles):
    pe, dve, act, pool, sp = p.engines
    TE, V, A, G, S = p.nc.tensor, p.nc.vector, p.nc.scalar, p.nc.gpsimd, p.nc.sync
    PAD = KC - 1
    with ExitStack() as c:
        u = sb("mu", [P, ET, T], c=c)
        z = sb("mz", [P, ET, T], c=c)
        y = sb("my", [P, ET, T], c=c)
        xd = sb("xd", [RX, T], c=c)
        win = sb("win", [P, 4 * P], c=c)
        wx = sb("wx", [P, ET, RX], c=c)
        wdt = sb("wdt", [R, ET * P], c=c)
        wout = sb("wout", [P, ET, P], c=c)
        taps = sb("taps", [P, ET, KC], c=c)
        alog = sb("alog", [P, ET, NS], c=c)
        cols = sb("cols", [P, 12], c=c)
        bout = sb("bout", [P, P], c=c)
        gam, bet, bin_, cb, bdt, dpar = (cols[:, a:b] for a, b in ((0, 1), (1, 2), (2, 6), (6, 8), (8, 10), (10, 12)))
        win_in = load(win[:], d["win"], "win")
        cols_in = load(cols[:], d["cols"], "cols")
        taps_in = load(taps[:], d["taps"].rearrange("(a p) k -> p a k", p=P), "taps")
        wx_in = load(wx[:], d["wx"].rearrange("(a p) r -> p a r", p=P), "wx")
        wdt_in = load(wdt[:], d["wdt"], "wdt")
        alog_in = load(alog[:], d["alog"].rearrange("(a p) n -> p a n", p=P), "alog")
        wout_in = load(wout[:], d["wout"].rearrange("(a p) n -> p a n", p=P), "wout")
        bout_in = load(bout[:], d["bout"].partition_broadcast(P), "bout")
        act.wait(alog_in)
        a_exp = act.tick(A.activation(alog[:], alog[:], ACT.Exp))
        pool.wait(a_exp)
        neg_a = pool.tick(G.tensor_scalar(alog[:], alog[:], -1.0, None, ALU.mult))
        with ExitStack() as cx:
            xT = sb("mxT", [P, T], c=cx)
            xp = sb("mxp", [P, ET, PAD + T], c=cx)
            hat = y[:, 0, :].rearrange("p (t d) -> p t d", d=P)
            e = layer_norm(p, xn[:], hat, st[:], [], y[:, 1, :].rearrange("p (t d) -> p t d", d=P))
            act.wait(cols_in)
            xT_ready = transpose_tiles(hat, xT, [e], scale=gam, bias=bet)
            padded = dve.tick(V.memset(xp[:, :, 0:PAD], 0.0))
            free = [None] * 4
            pe.wait(win_in, *xT_ready)
            n = 0
            for m in (2, 3, 0, 1):
                for q in range(4):
                    bank = ps[:, 2 + n % 4, :]
                    pe.wait(free[n % 4])
                    done = pe.tick(TE.matmul(bank, win[:, m * P:(m + 1) * P], xT[:, q * 512:(q + 1) * 512], start=True, stop=True))
                    act.wait(done)
                    if m >= 2:
                        ins = A.activation(z[:, m - 2, q * 512:(q + 1) * 512], bank, ACT.Silu, bias=bin_[:, m:m + 1])
                    else:
                        ins = A.activation(xp[:, m, PAD + q * 512:PAD + (q + 1) * 512], bank, ACT.Identity, bias=bin_[:, m:m + 1])
                    free[n % 4] = act.tick(ins)
                    n += 1
            dve.wait(act.now(), padded, taps_in)
            e0 = [None] * ET
            for k in range(KC):
                for a in range(ET):
                    if k == 0:
                        e = dve.tick(V.tensor_scalar(u[:, a, :], xp[:, a, 0:T], taps[:, a, 0:1], cb[:, a:a + 1], ALU.mult, ALU.add))
                    else:
                        dve.wait(e0[a])
                        e = dve.tick(V.scalar_tensor_tensor(u[:, a, :], xp[:, a, k:k + T], taps[:, a, k:k + 1], u[:, a, :], ALU.mult, ALU.add))
                    e0[a] = e
            act.wait(dve.now())
            for a in range(ET):
                u_ready = act.tick(A.activation(u[:, a, :], u[:, a, :], ACT.Silu))
            p.meet()
        pe.wait(wx_in, u_ready)
        for q in range(4):
            for a in range(ET):
                mm = TE.matmul(ps[0:RX, q, :], wx[:, a, :], u[:, a, q * 512:(q + 1) * 512], start=a == 0, stop=a == ET - 1)
        done = pe.tick(mm)
        dve.wait(done)
        xd_ready = dve.tick(V.tensor_copy(xd[:].rearrange("p (q n) -> p q n", q=4), ps[0:RX, 0:4, :]))
        bc = p.nc.dram_tensor("bc_scratch", [2 * NS, T], F32).ap()
        bc_saved = load(bc, xd[R:RX, :], "bc_save", [xd_ready])
        delta = sb("delta", [P, ET, T], c=c)
        du = sb("du", [P, ET, T], c=c)
        tmp = y
        pe.wait(wdt_in, xd_ready)
        for a in range(ET):
            for q in range(4):
                mm = TE.matmul(ps[:, 4 * a + q, :], wdt[:, a * P:(a + 1) * P], xd[0:R, q * 512:(q + 1) * 512], start=True, stop=True)
        done = pe.tick(mm)
        act.wait(done)
        for a in range(ET):
            e = act.tick(A.activation(delta[:, a, :], ps[:, 4 * a:4 * a + 4, :].rearrange("p a b -> p (a b)"), ACT.Identity, bias=bdt[:, a:a + 1]))
        act.wait(e)
        e = act.tick(A.activation(tmp[:], delta[:], ACT.Abs))
        act.wait(e)
        e = act.tick(A.activation(tmp[:], tmp[:], ACT.Exp, scale=-1.0))
        act.wait(e)
        e = act.tick(A.activation(tmp[:], tmp[:], ACT.Ln, bias=1.0))
        dve.wait(e)
        e = dve.tick(V.scalar_tensor_tensor(delta[:], delta[:], 0.0, tmp[:], ALU.max, ALU.add))
        dve.wait(e)
        e = dve.tick(V.tensor_tensor(du[:], delta[:], u[:], ALU.mult))
        y_zero = dve.tick(V.memset(y[:], 0.0))
        with ExitStack() as cs:
            rows = sb("rows", [1, 2, T], c=cs)
            ones = sb("ones", [1, P], c=cs)
            dec = sb("dec", [P, ET, T], c=cs)
            inp = sb("inp", [P, ET, T], c=cs)
            ones_set = pool.tick(G.memset(ones[:], 1.0))
            ac = sb("ac", [P, ET], c=cs)
            bc_in = p.dma("bc")
            sp.wait(bc_saved)
            p.meet()
            with p.loop(NS, pe=2, act=2, dve=7, pool=2, bc=2) as n:
                sp.wait(dve.now())
                bc_in.tick(S.dma_start(rows[:, 0, :], bc[ds(n, 1), :]))
                got = bc_in.tick(S.dma_start(rows[:, 1, :], bc[ds(NS + n, 1), :]))
                pe.wait(got)
                for w in range(2):
                    for q in range(4):
                        mm = TE.matmul(ps[:, 4 * w + q, :], ones[:], rows[:, w, q * 512:(q + 1) * 512], start=True, stop=True)
                    rows_out = pe.tick(mm)
                    if w == 0:
                        b_out = rows_out
                e = dve.tick(V.tensor_copy(ac[:], alog[:, :, ds(n, 1)]))
                act.wait(e)
                for a in range(ET):
                    e = act.tick(A.activation(dec[:, a, :], delta[:, a, :], ACT.Exp, scale=ac[:, a:a + 1]))
                    if a == 0:
                        dec_ready = [e]
                dec_ready.append(e)
                dve.wait(b_out)
                for a in range(ET):
                    inp_ready = dve.tick(V.tensor_tensor(inp[:, a, :], du[:, a, :], ps[:, 0:4, :].rearrange("p a b -> p (a b)"), ALU.mult))
                dve.wait(inp_ready)
                for a in range(ET):
                    dve.wait(dec_ready[a])
                    e = dve.tick(V.tensor_tensor_scan(inp[:, a, :], dec[:, a, :], inp[:, a, :], 0.0, ALU.mult, ALU.add))
                    if a == 0:
                        h_ready = [e]
                h_ready.append(e)
                dve.wait(rows_out)
                for a in range(ET):
                    dve.wait(h_ready[a])
                    e = dve.tick(V.tensor_tensor(dec[:, a, :], inp[:, a, :], ps[:, 4:8, :].rearrange("p a b -> p (a b)"), ALU.mult))
                    pool.wait(e)
                    pool.tick(G.tensor_tensor(y[:, a, :], y[:, a, :], dec[:, a, :], ALU.add))
            p.meet()
        for a in range(ET):
            e = dve.tick(V.scalar_tensor_tensor(y[:, a, :], u[:, a, :], dpar[:, a:a + 1], y[:, a, :], ALU.mult, ALU.add))
            dve.wait(e)
            e = dve.tick(V.tensor_tensor(y[:, a, :], y[:, a, :], z[:, a, :], ALU.mult))
        pe.wait(e, wout_in)
        for t in range(NT):
            for a in range(ET):
                mm = TE.matmul(ps[:, t // 4, (t % 4) * P:(t % 4 + 1) * P], y[:, a, t * P:(t + 1) * P], wout[:, a, :],
                               start=a == 0, stop=a == ET - 1, skip_group_check=True)
        done = pe.tick(mm)
        flat = acc[:].rearrange("p (q c) d -> p q (c d)", q=4)
        dve.wait(done, bout_in)
        e = dve.tick(V.tensor_tensor(flat, flat, ps[:, 0:4, :], ALU.add))
        dve.wait(e)
        e = dve.tick(V.tensor_tensor(acc[:], acc[:], bcast(bout[:], 1, NT), ALU.add))
        dve.wait(e)
        dve.tick(V.tensor_tensor(acc[:], acc[:], xn[:], ALU.add))
        p.meet()


def transformer(p, d, sb, ps, load, acc, xn, xs, ident, identb):
    pe, dve, act, pool, sp = p.engines
    TE, V, A, G, S = p.nc.tensor, p.nc.vector, p.nc.scalar, p.nc.gpsimd, p.nc.sync
    NB = NT // TB
    c = ExitStack()
    with c:
        ys = sb("ys", [P, NT + 1, P], c=c)
        wqkv = sb("wqkv", [P, 3 * INNER], c=c)
        wo = sb("wo", [P, INNER // P, P], c=c)
        w1 = sb("w1", [P, 2 * FI], c=c)
        w2 = sb("w2", [P, 3, P], c=c)
        colA = sb("colA", [P, 2 + 6], c=c)
        b2 = sb("b2", [P, P], c=c)
        qks = sb("qks", [P, 4, DH], c=c)
        rotary = sb("rotary", [P, 4, DH], c=c)
        tab = sb("tab", [P, 4, DH], c=c)
        turn = sb("turn", [P, P], c=c)
        band = sb("band", [P, 2, 2 * KW], BF16, c=c)
        band32 = sb("band32", [P, 2, 2 * KW], c=c)
        xc = sb("xc", [P, 2, P], c=c)
        xcT = sb("xcT", [P, 2, P], c=c)
        xf = sb("xf", [P, 2, TB, P], c=c)
        xfT = sb("xfT", [P, 2, TB * P], c=c)
        half = sb("half", [P, 1], c=c)
        uc = sb("uc", [P, 2, 512], c=c)
        sq = sb("sq", [P, 2, 512], c=c)
        ra = sb("ra", [P, 2, 4, 512], c=c)
        rb = sb("rb", [P, 2, 512], c=c)
        ss = sb("ss", [P, 2, 4, 8], c=c)
        rn = sb("rn", [P, 2, 4, 8], c=c)
        qT = sb("qT", [P, 2, 8, P], c=c)
        kT = sb("kT", [P, 2, 8, KW], c=c)
        vs = sb("vs", [P, 2, H, DH + 1], c=c)
        vh = sb("vh", [WIN, 2, H, DH + 1], c=c)
        pr = sb("pr", [P, 2, 4, KW], c=c)
        prT = sb("prT", [P, 2, 512], c=c)
        phT = sb("phT", [WIN, 2, P], c=c)
        nmx = sb("nmxl", [P, 2, 4], c=c)
        rec = sb("recl", [P, 2, 4], c=c)
        on = sb("on", [P, 2, INNER], c=c)
        oT = sb("oT", [P, INNER], c=c)
        hv = sb("hv", [P, 2, 3, 512], c=c)
        bnst = sb("bnst", [P, 2, TB, 6], c=c)
        mv = sb("mv", [P, 2, TB, 2], c=c)
        rs = sb("rs", [P, 2, TB], c=c)

        turn_in = load(turn[:], d["turn"], "turn")
        rotary_in = load(rotary[:], d["rotary"], "rotary")
        band_in = load(band32[:], d["band"], "band")
        dve.wait(band_in)
        dve.tick(V.tensor_copy(band[:], band32[:]))
        pool.tick(G.memset(ys[:, 0, :], 0.0))
        pool.tick(G.memset(half[:], -0.5))
        pool.tick(G.memset(vh[:], 0.0))
        pool.tick(G.memset(vs[:], 1.0))
        pool.tick(G.memset(kT[:], 0.0))
        pool.tick(G.memset(xc[:], 0.0))
        pool.tick(G.memset(xf[:], 0.0))
        dve.tick(V.tensor_copy(xs[:, 1:NT + 1, :], xn[:]))
        pe.wait(turn_in, band_in)
        dve.wait(rotary_in)
        p.meet()

        wA = p.dma("wA")
        wB = p.dma("wB")
        xc_in = [p.dma("xc0"), p.dma("xc1")]
        xf_in = [p.dma("xf0"), p.dma("xf1")]
        vh_in = [p.dma("vh0"), p.dma("vh1")]

        def shifted(c, to, src, t0, n):
            c.tick(S.dma_start(to[:, :, 0:DH], src[:, ds(t0 + 1, n), 0:DH]))
            c.tick(S.dma_start(to[1:P, :, DH:P], src[0:P - 1, ds(t0 + 1, n), DH:P]))
            return c.tick(S.dma_start(to[0:1, :, DH:P], src[P - 1:P, ds(t0, n), DH:P]))

        with p.loop(L, **LAYER) as l:
            def row(name):
                return d[name][ds(l, 1)]

            wA.tick(S.dma_start(wqkv[:], row("lwqkv").rearrange("a p n -> p (a n)")))
            wA.tick(S.dma_start(wo[:], row("lwo").rearrange("a (c p) n -> p (a c) n", p=P)))
            wA_in = wA.tick(S.dma_start(qks[:].rearrange("p a b -> p (a b)"), row("qks").rearrange("a n -> (a n)").partition_broadcast(P)))
            wB.tick(S.dma_start(w1[:], row("lw1").rearrange("a p n -> p (a n)")))
            for j, (o, w) in enumerate(FCH):
                wB.tick(S.dma_start(w2[0:w, j, :], d["lw2"][ds(l, 1), o:o + w, :].rearrange("a p n -> p (a n)")))
            wB.tick(S.dma_start(colA[:], row("cols1").rearrange("a p n -> p (a n)")))
            wB_in = wB.tick(S.dma_start(b2[:], row("lb2").rearrange("a n -> (a n)").partition_broadcast(P)))
            dve.wait(wA_in)
            dve.wait(dve.tick(V.tensor_tensor(tab[:], rotary[:], qks[:], ALU.mult)))
            pe.wait(wA_in, wB_in)
            act.wait(wB_in)
            dve.wait(wB_in)

            ev = dict.fromkeys(["bank4", "bank5", "bank6", "bank7", "halo"] + [n + str(r) for n in (
                "s", "exp", "xc", "xcT", "xc_used", "xcT_used", "uc", "uc_sq", "sq", "rb", "ss", "q_rows", "k_rows", "ra_used",
                "qT", "kT", "kT_used", "v", "v_used", "vh", "vh_used", "prob_used", "prT", "prT_used", "phT", "on", "on_used", "oT_used") for r in range(2)])
            turn_of_t = [0]

            def t_bank(ev):
                turn_of_t[0] += 1
                r = turn_of_t[0] % 2
                pe.wait(ev[f"bank{6 + r}"])
                return f"bank{6 + r}", ps[:, 6 + r, :]

            def fetch_tile(ev, b, t):
                sp.wait(ev[f"xc_used{b}"])
                ev[f"xc{b}"] = shifted(xc_in[b], xc[:, b:b + 1, :], xs, t, 1)

            def prepare(ev, b):
                k, bank = t_bank(ev)
                pe.wait(ev[f"xc{b}"])
                done = ev[f"xc_used{b}"] = pe.tick(TE.transpose(bank[:, 0:P], xc[:, b, :], ident[:]))
                act.wait(done, ev[f"xcT_used{b}"])
                ev[k] = ev[f"xcT{b}"] = act.tick(A.activation(xcT[:, b, :], bank[:, 0:P], ACT.Copy))

            def project_v(ev, b, w):
                bank = ps[:, 4, :]
                pe.wait(ev["bank4"])
                done = ev[f"xcT_used{b}"] = pe.tick(TE.matmul(bank, xcT[:, b, :], wqkv[:, (4 + w) * 512:(5 + w) * 512], start=True, stop=True))
                act.wait(done, ev[f"v_used{b}"], ev[f"vh{1 - b}"])
                ev["bank4"] = ev[f"v{b}"] = act.tick(A.activation(vs[:, b, w * 8:(w + 1) * 8, 0:DH], bank.rearrange("p (h d) -> p h d", d=DH), ACT.Copy))

            def project_qk(ev, b, w):
                r, bank = w % 2, ps[:, 4, :]
                pe.wait(ev["bank4"], ev[f"xcT{b}"])
                done = pe.tick(TE.matmul(bank, xcT[:, b, :], wqkv[:, w * 512:(w + 1) * 512], start=True, stop=True))
                act.wait(done, ev[f"uc{r}"], ev[f"uc_sq{r}"])
                out = ev["bank4"] = act.tick(A.activation(uc[:, r, :], bank, ACT.Copy))
                act.wait(out, ev[f"sq{r}"])
                squared = ev[f"uc_sq{r}"] = act.tick(A.activation(sq[:, r, :], uc[:, r, :], ACT.Square))
                heads, out_a, out_b = (x.rearrange("p (h d) -> p h d", d=DH) for x in (uc[:, r, :], ra[:, b, w, :], rb[:, r, :]))
                cos, sin = tab[:, w // 2 * 2, :], tab[:, w // 2 * 2 + 1, :]
                dve.wait(out, ev[f"ra_used{b}"], ev[f"rb{r}"])
                V.tensor_tensor(out_a, heads, bcast(cos, 1, 8), ALU.mult)
                V.tensor_tensor(out_b[:, :, 0:32], heads[:, :, 32:64], bcast(sin[:, 0:32], 1, 8), ALU.mult)
                turned = ev[f"uc{r}"] = dve.tick(V.tensor_tensor(out_b[:, :, 32:64], heads[:, :, 0:32], bcast(sin[:, 32:64], 1, 8), ALU.mult))
                dve.wait(squared)
                summed = ev[f"sq{r}"] = dve.tick(V.tensor_reduce(ss[:, b, w, :], sq[:, r, :].rearrange("p (h d) -> p h d", d=DH), X_AXIS, ALU.add))
                pool.wait(turned)
                ev[f"rb{r}"] = pool.tick(G.tensor_tensor(ra[:, b, w, :], ra[:, b, w, :], rb[:, r, :], ALU.add))
                pool.wait(summed)
                e = pool.tick(G.tensor_scalar(rn[:, b, w, :], ss[:, b, w, :], 1e-24, None, ALU.max))
                pool.wait(e)
                e = pool.tick(G.tensor_tensor(rn[:, b, w, :], rn[:, b, w, :], half[:].broadcast_to([P, 8]), ALU.pow))
                pool.wait(e, ev[f"rb{r}"])
                ev[("q_rows", "k_rows")[w // 2] + str(b)] = pool.tick(G.tensor_tensor(out_a, out_a, bcast(rn[:, b, w, :], 2, DH), ALU.mult))

            def turn_rows(ev, b, w):
                k, bank = t_bank(ev)
                pe.wait(ev[("q_rows", "k_rows")[w // 2] + str(b)])
                for j in range(4):
                    mm = TE.transpose(bank[:, j * P:(j + 1) * P], ra[:, b, w, j * P:(j + 1) * P], ident[:])
                done = ev[f"ra_used{b}"] = pe.tick(mm)
                to = qT[:, b, 4 * w:4 * w + 4, :] if w < 2 else kT[:, b, 4 * w - 8:4 * w - 4, WIN:KW]
                act.wait(done)
                ev[k] = ev[("qT", "kT")[w // 2] + str(b)] = act.tick(A.activation(to, bank.rearrange("p (j n) -> p j n", n=P), ACT.Copy))

            def keys_before(ev, b):
                k, bank = t_bank(ev)
                pe.wait(ev[f"kT{1 - b}"])
                done = pe.tick(TE.matmul(bank[:, 0:8 * WIN], turn[:], kT[:, 1 - b, :, P:KW], start=True, stop=True))
                dve.wait(done)
                ev[k] = ev["halo"] = dve.tick(V.tensor_copy(kT[:, b, :, 0:WIN], bank[:, 0:8 * WIN].rearrange("p (j n) -> p j n", n=WIN)))

            def values_before(ev, b):
                sp.wait(ev[f"v{1 - b}"], ev[f"vh_used{b}"])
                ev[f"vh{b}"] = vh_in[b].tick(S.dma_start(vh[:, b, :, :], vs[P - WIN:P, 1 - b, :, :]))

            def scores(ev, b, g, first):
                r = g % 2
                pe.wait(ev[f"s{r}"], ev[f"qT{b}"], ev[f"kT{b}"], ev["halo"])
                for o in range(2):
                    TE.matmul(ps[:, 2 * r + o, 0:2 * KW], identb[:], band[:, 0 if first else 1, :], start=True, stop=False, skip_group_check=True)
                for pair in range(2):
                    for o in range(2):
                        j = 2 * g + pair
                        mm = TE.matmul(ps[:, 2 * r + o, pair * KW:(pair + 1) * KW], qT[o * DH:(o + 1) * DH, b, j, :], kT[o * DH:(o + 1) * DH, b, j, :],
                                       start=False, stop=pair == 1, skip_group_check=True)
                done = pe.tick(mm)
                sc = ps[:, 2 * r:2 * r + 2, 0:2 * KW].rearrange("p o (a n) -> p o a n", a=2)
                dve.wait(done, ev[f"exp{r}"])
                e = dve.tick(V.tensor_reduce(nmx[:, r, :].rearrange("p (o a) -> p o a", o=2), sc, X_AXIS, ALU.max, negate=True))
                act.wait(e, ev[f"prob_used{r}"], ev[f"phT{r}"])
                for j in range(4):
                    ins = A.activation(pr[:, r, j, :], sc[:, j // 2, j % 2, :], ACT.Exp, bias=nmx[:, r, j:j + 1])
                ev[f"s{r}"] = ev[f"exp{r}"] = act.tick(ins)

            def turn_probs(ev, b, g):
                r = g % 2
                k, bank = t_bank(ev)
                pe.wait(ev[f"exp{r}"])
                for j in range(4):
                    mm = TE.transpose(bank[:, j * P:(j + 1) * P], pr[:, r, j, WIN:KW], ident[:])
                done = ev[f"prob_used{r}"] = pe.tick(mm)
                dve.wait(done, ev[f"prT_used{r}"])
                ev[k] = ev[f"prT{r}"] = dve.tick(V.tensor_copy(prT[:, r, :], bank))
                ev[f"phT{r}"] = dve.tick(V.transpose(phT[:, r, :].rearrange("p (j n) -> p j n", j=4), pr[0:WIN, r, :, 0:WIN]))

            def values(ev, b, g):
                r = g % 2
                pe.wait(ev[f"prT{r}"], ev[f"phT{r}"], ev[f"v{b}"], ev[f"vh{b}"], ev["bank5"])
                o_bank = ps[:, 5, 0:4 * (DH + 1)]
                for j in range(4):
                    TE.matmul(o_bank[:, j * (DH + 1):(j + 1) * (DH + 1)], prT[:, r, j * P:(j + 1) * P], vs[:, b, 4 * g + PERM[j], :],
                              start=j == 0, stop=False, skip_group_check=True)
                for j in range(4):
                    mm = TE.matmul(o_bank[0:WIN, j * (DH + 1):(j + 1) * (DH + 1)], phT[:, r, j * WIN:(j + 1) * WIN], vh[:, b, 4 * g + PERM[j], :],
                                   start=False, stop=j == 3, skip_group_check=True)
                done = ev[f"prT_used{r}"] = ev[f"v_used{b}"] = ev[f"vh_used{b}"] = pe.tick(mm)
                o4 = o_bank.rearrange("p (j d) -> p j d", j=4)
                dve.wait(done, ev[f"on_used{b}"])
                e = dve.tick(V.reciprocal(rec[:, r, :], o4[:, :, DH]))
                dve.wait(e)
                to = on[:, b, 4 * g * DH:4 * (g + 1) * DH].rearrange("p (a o d) -> p o a d", a=2, o=2)
                ev["bank5"] = ev[f"on{b}"] = dve.tick(V.tensor_tensor(to, o4[:, :, 0:DH].rearrange("p (o a) d -> p o a d", o=2),
                                                                      bcast(rec[:, r, :].rearrange("p (o a) -> p o a", o=2), 3, DH), ALU.mult))

            def turn_out(ev, b, w):
                k, bank = t_bank(ev)
                pe.wait(ev[f"on{b}"])
                for j in range(4):
                    mm = TE.transpose(bank[:, j * P:(j + 1) * P], on[:, b, (4 * w + j) * P:(4 * w + j + 1) * P], ident[:])
                done = ev[f"on_used{b}"] = pe.tick(mm)
                act.wait(done, ev["oT_used0"])
                ev[k] = ev["oT_used1"] = act.tick(A.activation(oT[:, w * 512:(w + 1) * 512], bank, ACT.Copy))

            def finish(ev, t):
                k, bank = t_bank(ev)
                pe.wait(ev["oT_used1"])
                for j in range(8):
                    mm = TE.matmul(bank[:, 0:P], oT[:, j * P:(j + 1) * P], wo[:, j, :], start=j == 0, stop=j == 7)
                done = ev["oT_used0"] = pe.tick(mm)
                dve.wait(done)
                ev[k] = dve.tick(V.tensor_tensor(ys[:, ds(t + 1, 1), :], xs[:, ds(t + 1, 1), :], bank[:, 0:P].unsqueeze(1), ALU.add))

            def two_tiles(i, ev, more):
                for b in range(2):
                    last = not more and b == 1
                    for g in range(4):
                        turn_probs(ev, b, g)
                        if g == 0 and more:
                            prepare(ev, b)
                            fetch_tile(ev, 1 - b, 2 * i + b + 3)
                        if g == 0 and not last:
                            values_before(ev, 1 - b)
                        if g < 2 and not last:
                            project_v(ev, 1 - b, g)
                        if more:
                            project_qk(ev, b, g)
                        if not last and g < 2:
                            turn_rows(ev, 1 - b, g)
                            turn_rows(ev, 1 - b, 2 + g)
                        if not last and g == 1:
                            keys_before(ev, 1 - b)
                        if g < 2:
                            scores(ev, b, g + 2, isinstance(i, int) and i + b == 0)
                        elif not last:
                            scores(ev, 1 - b, g - 2, False)
                        values(ev, b, g)
                    for w in range(2):
                        turn_out(ev, b, w)
                    finish(ev, 2 * i + b)

            for b in range(2):
                fetch_tile(ev, b, b)
            for b in range(2):
                prepare(ev, b)
            fetch_tile(ev, 0, 2)
            values_before(ev, 0)
            for w in range(4):
                project_qk(ev, 0, w)
            for w in range(2):
                project_v(ev, 0, w)
            for w in range(4):
                project_qk(ev, 1, w)
            for w in range(4):
                turn_rows(ev, 0, w)
            keys_before(ev, 0)
            for g in range(2):
                scores(ev, 0, g, True)
            p.pipeline(NT // 2, two_tiles, ev)

            last_y = dve.now()
            pe_free = [pe.now(), act.now(), dve.now()]
            fe = {}

            def normalise(q):
                b = q % 2
                sp.wait(last_y, fe.get(("xf_used", b)))
                got = shifted(xf_in[b], xf[:, b, :, :], ys, q * TB, TB)
                dve.wait(got)
                for t in range(TB):
                    e = dve.tick(V.bn_stats(bnst[:, b, t, :], xf[:, b, t, :]))
                dve.wait(e)
                dve.settle()
                for t in range(TB):
                    e = dve.tick(V.bn_aggr(mv[:, b, t, :], bnst[:, b, t, :]))
                pool.wait(e)
                e = pool.tick(G.tensor_scalar(rs[:, b, :], mv[:, b, :, 1], EPS, None, ALU.add))
                pool.wait(e)
                e = pool.tick(G.tensor_tensor(rs[:, b, :], rs[:, b, :], half[:].broadcast_to([P, TB]), ALU.pow))
                dve.wait(e)
                for t in range(TB):
                    e = dve.tick(V.tensor_scalar(xf[:, b, t, :], xf[:, b, t, :], mv[:, b, t, 0:1], rs[:, b, t:t + 1], ALU.subtract, ALU.mult))
                pe.wait(e, *pe_free, fe.get(("t", b)))
                for t in range(TB):
                    mm = TE.transpose(ps[:, b, t * P:(t + 1) * P], xf[:, b, t, :], ident[:])
                fe["xf_used", b] = e = pe.tick(mm)
                act.wait(e, fe.get(("xfT_used", b)))
                fe["t", b] = fe["xfT", b] = act.tick(A.activation(xfT[:, b, :], ps[:, b, :], ACT.Identity, bias=colA[:, 1:2], scale=colA[:, 0:1]))

            def feed_forward(q):
                b = q % 2
                for j, (o, w) in enumerate(FCH):
                    r = (3 * q + j) % 2
                    gate, val = ps[0:w, 2 + 2 * r, :], ps[0:w, 3 + 2 * r, :]
                    pe.wait(fe["xfT", b], fe.get(("gv", r)))
                    TE.matmul(gate, w1[:, FI + o:FI + o + w], xfT[:, b, :], start=True, stop=True)
                    e = pe.tick(TE.matmul(val, w1[:, o:o + w], xfT[:, b, :], start=True, stop=True))
                    act.wait(e, fe.get(("hv_used", b)))
                    e = act.tick(A.activation(hv[0:w, b, j, :], gate, ACT.Gelu, bias=colA[0:w, 2 + j:3 + j]))
                    dve.wait(e)
                    fe["gv", r] = fe["h", j] = dve.tick(V.scalar_tensor_tensor(hv[0:w, b, j, :], val, colA[0:w, 5 + j:6 + j], hv[0:w, b, j, :], ALU.add, ALU.mult))
                fe["xfT_used", b] = pe.now()

            def down(q):
                b = q % 2
                pe.wait(fe["h", 0], fe["h", 1], fe["h", 2], fe.get(("o", b)))
                for t in range(TB):
                    for j, (o, w) in enumerate(FCH):
                        mm = TE.matmul(ps[:, 6 + b, t * P:(t + 1) * P], hv[0:w, b, j, t * P:(t + 1) * P], w2[0:w, j, :], start=j == 0, stop=j == 2,
                                       skip_group_check=True)
                fe["hv_used", b] = e = pe.tick(mm)
                to = xs[:, q * TB + 1:(q + 1) * TB + 1, :]
                dve.wait(e)
                e = fe["o", b] = dve.tick(V.tensor_tensor(to, ys[:, q * TB + 1:(q + 1) * TB + 1, :], ps[:, 6 + b, :].rearrange("p (t d) -> p t d", d=P), ALU.add))
                dve.wait(e)
                dve.tick(V.tensor_tensor(to, to, bcast(b2[:], 1, TB), ALU.add))

            normalise(0)
            for q in range(NB):
                if q + 1 < NB:
                    normalise(q + 1)
                feed_forward(q)
                down(q)
        sp.wait(xc_in[0].now(), xc_in[1].now())
        p.meet()
        dve.tick(V.tensor_tensor(acc[:], acc[:], xs[:, 1:NT + 1, :], ALU.add))
        p.meet()


LAYER = dict(pe=452, dve=549, act=352, pool=264, wA=3, wB=6, xc0=27, xc1=24, xf0=6, xf1=6, vh0=8, vh1=8)


def constants():
    c = {"ident": np.eye(P, dtype=np.float32), }
    q, k = np.arange(P)[:, None], np.arange(P)[None, :]
    c["causal"] = np.where(k > q, -1e30, 0.0).astype(np.float32)
    c["lower"] = (np.arange(NE)[None, :] < np.arange(NE)[:, None]).astype(np.float32)
    half = np.arange(0, DH, 2, dtype=np.float64)
    freq = np.tile(1.0 / 10000.0 ** (half / DH), 2)
    base = np.tile((half + 0.4 * DH) / (1.4 * DH), 2)
    pos = np.arange(P, dtype=np.float64)[:, None] - P // 2
    scale = base[None, :] ** (pos / (WIN // 2))
    sign = np.where(np.arange(DH) < DH // 2, -1.0, 1.0)
    cos, sin = np.cos(pos * freq), np.sin(pos * freq) * sign
    c["rotary"] = np.stack([8 * cos * scale, 8 * sin * scale, cos / scale, sin / scale], 1).astype(np.float32)
    phi = -P * freq
    turn = np.zeros((2 * DH, 2 * DH))
    fac = base ** (P / (WIN // 2))
    for h in range(2):
        for f in range(DH):
            o = h * DH
            turn[o + f, o + f] = np.cos(phi[f]) * fac[f]
            turn[o + (f + DH // 2) % DH, o + f] = sign[f] * np.sin(phi[f]) * fac[f]
    c["turn"] = turn.astype(np.float32)
    j = np.arange(KW)[None, :] - WIN
    keep = (j <= q) & (j >= q - WIN)
    rows = [np.where(keep & (j >= 0), 0.0, -1e30), np.where(keep, 0.0, -1e30)]
    c["band"] = np.stack([np.tile(r, (1, 2)) for r in rows], 1).astype(np.float32)
    return c


def kernel(**inputs):
    import concourse.bacc as bacc
    from concourse.bass_utils import run_bass_kernel_spmd

    a = {k: np.asarray(v) for k, v in inputs.items()}
    wkqv, bkqv = a["L0_attn_Wkqv"], a["L0_attn_bkqv"]
    host = constants()
    host.update({
        "x": a["L0_attn_x"][0],
        "wkq": wkqv[:, :, :2 * P], "bkq": bkqv[:, :2 * P].reshape(H0, 2, P).transpose(0, 2, 1),
        "wv": wkqv[:, :, 2 * P:].transpose(1, 0, 2).reshape(P, P), "bv": bkqv[:, 2 * P:].reshape(P),
        "wp": a["L0_attn_Wp"], "bp": a["L0_attn_bp"], "wg": a["L0_ffn_Wg"], "we": a["L0_ffn_We"],
    })
    col = lambda n: a["L1_attn_" + n].reshape(-1, P).T
    host.update({
        "win": a["L1_attn_W_in"].T, "wx": a["L1_attn_W_x"].T, "wdt": a["L1_attn_W_dt"].T, "wout": a["L1_attn_W_out"].T,
        "taps": a["L1_attn_conv_w"], "alog": a["L1_attn_A_log"], "bout": a["L1_attn_b_out"],
        "cols": np.concatenate([col(n) for n in ("gamma", "beta", "b_in", "conv_b", "b_dt", "D_param")], 1),
    })
    qs, ks = a["L1_ffn_q_scale"], a["L1_ffn_k_scale"]
    turned = lambda v: np.concatenate([v[:, DH // 2:], v[:, :DH // 2]], 1)
    b1 = np.zeros((L, P, 6), np.float32)
    for j, (o, w) in enumerate(FCH):
        b1[:, :w, j] = a["L1_ffn_b1"][:, FI + o:FI + o + w]
        b1[:, :w, 3 + j] = a["L1_ffn_b1"][:, o:o + w]
    host.update({
        "lwqkv": a["L1_ffn_Wqkv"], "lwo": a["L1_ffn_Wo"], "lw1": a["L1_ffn_W1"], "lw2": a["L1_ffn_W2"], "lb2": a["L1_ffn_b2"],
        "qks": np.concatenate([qs, turned(qs), ks, turned(ks)], 1),
        "cols1": np.concatenate([a["L1_ffn_ln_g"][:, :, None], a["L1_ffn_ln_b"][:, :, None], b1], 2),
    })
    nc = bacc.Bacc("TRN2", target_bir_lowering=False, num_devices=1)
    arrays, aps = {}, {}
    for name, v in host.items():
        v = np.ascontiguousarray(v)
        arrays[name + "_dram"] = v
        aps[name] = nc.dram_tensor(name + "_dram", v.shape, mybir.dt.from_np(v.dtype), kind="ExternalInput").ap()
    out = nc.dram_tensor("out_dram", (1, T, P), F32, kind="ExternalOutput").ap()
    build(nc, aps, out[0])
    return run_bass_kernel_spmd(nc, [arrays], core_ids=[0]).results[0]["out_dram"]
```

```python
from contextlib import ExitStack, contextmanager

import numpy as np

import concourse.bass as bass
from concourse import mybir

F32 = mybir.dt.float32
BF16 = mybir.dt.bfloat16
ALU = mybir.AluOpType
ACT = mybir.ActivationFunctionType
X_AXIS = mybir.AxisListType.X
ds = bass.ds

P = 128
T = 2048
NT = T // P
EPS = 1e-5
H0 = 16
DV0 = 8
VW = DV0 + 1
KB = 1024
NE = 8
ED = 256
ET = ED // P
NS = 16
KC = 15
R = 8
RX = R + 2 * NS
L = 6
H = 16
DH = 64
INNER = H * DH
WIN = 32
FI = 341
FCH = [(0, 128), (128, 128), (256, FI - 256)]
KW = WIN + P
PERM = [0, 2, 1, 3]


class Counter:

    def __init__(self, nc, eng, name, step=1):
        self.eng, self.name, self.step = eng, name, step
        self.sem = nc.alloc_semaphore("s_" + name)
        self.base, self.k, self.seen, self.alone, self.spare = 0, 0, {}, False, None

    def tick(self, ins):
        ins.then_inc(self.sem, self.step)
        self.k += self.step
        return self.now()

    def now(self):
        return (self, self.k)

    def wait(self, *events):
        for ev in events:
            if ev is None:
                continue
            c, k = ev
            if k > self.seen.get(c.name, -1 << 40):
                self.eng.wait_ge(c.sem, c.base + k)
                self.seen[c.name] = k
                if self.alone and not isinstance(c.base, int):
                    self.settle()

    def settle(self):
        self.eng.sem_inc(self.spare, 1)


class Program:
    def __init__(self, nc):
        self.nc = nc
        self.pe = Counter(nc, nc.tensor, "pe")
        self.dve = Counter(nc, nc.vector, "dve")
        self.act = Counter(nc, nc.scalar, "act")
        self.pool = Counter(nc, nc.gpsimd, "pool")
        self.sp = Counter(nc, nc.sync, "sp")
        self.engines = [self.pe, self.dve, self.act, self.pool, self.sp]
        self.counters = list(self.engines)
        self.sp.alone = self.pool.alone = True
        for e in self.engines:
            e.spare = nc.alloc_semaphore("spare_" + e.name)

    def dma(self, name):
        c = Counter(self.nc, self.nc.sync, name, 16)
        self.counters.append(c)
        return c

    def forget(self):
        for c in self.counters:
            c.seen = {}

    @contextmanager
    def loop(self, n, **per):
        kept = [(c.base, c.k) for c in self.counters]
        for e in self.engines:
            if not isinstance(e.base, int):
                e.settle()
        with self.nc.Fori(0, n) as i:
            for c in self.counters:
                gain = per.get(c.name, 0) * c.step
                c.base = c.base + c.k + i * gain if gain else c.base + c.k
                c.k = 0
            self.forget()
            self.meet()
            yield i
            gained = {c.name: c.k // c.step for c in self.counters if c.k}
            assert gained == {a: b for a, b in per.items() if b}, f"the loop's counts are {gained}"
        for c, (base, k) in zip(self.counters, kept):
            c.base, c.k = base, k + n * per.get(c.name, 0) * c.step
        self.forget()

    def pipeline(self, n, body, state, lead=1):
        def moved(by):
            return {a: e and (e[0], e[1] + by[e[0].name]) for a, e in state.items()}

        for i in range(lead):
            start = {c.name: c.k for c in self.counters}
            body(i, state, True)
        ends = {c.name: c.k for c in self.counters}
        gain = {a: ends[a] - start.get(a, 0) for a in ends}
        first = moved({a: -v for a, v in ends.items()})
        state.update(first)
        kept = [(c.base, c.k) for c in self.counters]
        for e in self.engines:
            if not isinstance(e.base, int):
                e.settle()
        with self.nc.Fori(lead, n - 1) as i:
            for c in self.counters:
                g = gain[c.name]
                c.base = c.base + (c.k - lead * g) + i * g if g else c.base + c.k
                c.k = 0
            self.forget()
            body(i, state, True)
            assert {c.name: c.k for c in self.counters} == gain
            state.update(moved({a: -v for a, v in gain.items()}))
            assert state == first, "the turns differ"
        for c, (base, k) in zip(self.counters, kept):
            c.base, c.k = base, k + (n - 1 - lead) * gain[c.name]
        state.update(moved({c.name: c.k for c in self.counters}))
        self.forget()
        body(n - 1, state, False)

    def meet(self):
        for e in self.engines:
            e.seen = {}
            for c in self.engines:
                if c.k > 0 or not isinstance(c.base, int) or c.base > 0:
                    e.wait(c.now())


def bcast(ap, at, n):
    shape = list(ap.shape)
    return ap.unsqueeze(at).broadcast_to(shape[:at] + [n] + shape[at:])


def layer_norm(p, src, dst, st, after, scratch):
    dve, act = p.dve, p.act
    V, A = p.nc.vector, p.nc.scalar
    dve.wait(*after)
    e = dve.tick(V.tensor_reduce(st[:, 0, :], src, X_AXIS, ALU.add))
    dve.wait(e)
    e = dve.tick(V.tensor_scalar(st[:, 1, :], st[:, 0, :], -1.0 / P, None, ALU.mult))
    dve.wait(e)
    e = dve.tick(V.tensor_tensor(dst, src, bcast(st[:, 1, :], 2, P), ALU.add))
    act.wait(e)
    e = act.tick(A.activation(scratch, dst, ACT.Square))
    dve.wait(e)
    e = dve.tick(V.tensor_reduce(st[:, 2, :], scratch, X_AXIS, ALU.add))
    dve.wait(e)
    e = dve.tick(V.tensor_scalar(st[:, 3, :], st[:, 2, :], 1.0 / P, EPS, ALU.mult, ALU.add))
    act.wait(e)
    e = act.tick(A.activation(st[:, 0, :], st[:, 3, :], ACT.Sqrt))
    dve.wait(e)
    e = dve.tick(V.reciprocal(st[:, 1, :], st[:, 0, :]))
    dve.wait(e)
    return dve.tick(V.tensor_tensor(dst, dst, bcast(st[:, 1, :], 2, P), ALU.mult))


def build(nc, d, out):
    p = Program(nc)
    pe, dve, act, pool, sp = p.engines
    TE, V, A, G, S = nc.tensor, nc.vector, nc.scalar, nc.gpsimd, nc.sync
    ctx = ExitStack()
    with ctx:
        def sb(name, shape, dt=F32, c=ctx):
            return c.enter_context(nc.sbuf_tensor(name, shape, dt))

        ps = ctx.enter_context(nc.psum_tensor("ps", [P, 8, 512], F32))

        def load(dst, src, name, after=()):
            c = p.dma(name)
            sp.wait(*after)
            return c.tick(S.dma_start(dst, src))

        ident = sb("ident", [P, P])
        identb = sb("identb", [P, P], BF16)
        acc = sb("acc", [P, NT, P])
        xn = sb("xn", [P, NT, P])
        xs = sb("xs", [P, NT + 2, P])
        st = sb("st", [P, 4, NT])

        x0 = xs[:, 1:NT + 1, :]
        x_in = load(x0, d["x"].rearrange("(t p) d -> p t d", p=P), "x")
        id_in = load(ident[:], d["ident"], "ident")
        dve.wait(id_in)
        idb_in = dve.tick(V.tensor_copy(identb[:], ident[:]))
        pool.tick(G.memset(xs[:, 0, :], 0.0))
        pool.tick(G.memset(xs[:, NT + 1, :], 0.0))
        outs = p.dma("out")

        def transpose_tiles(src, dst, after, scale=None, bias=None, banks=(0, 1)):
            free, last = [None, None], None
            for q in range(NT // 4):
                bank = ps[:, banks[q % 2], :]
                pe.wait(id_in, *after, free[q % 2])
                for c in range(4):
                    mm = TE.transpose(bank[:, c * P:(c + 1) * P], src[:, 4 * q + c, :], ident[:])
                done = pe.tick(mm)
                to = dst[:, q * 512:(q + 1) * 512]
                if scale is None and q % 2:
                    dve.wait(done)
                    free[1] = dve.tick(V.tensor_copy(to, bank))
                else:
                    act.wait(done)
                    if scale is None:
                        ins = A.activation(to, bank, ACT.Copy)
                    else:
                        ins = A.activation(to, bank, ACT.Identity, bias=bias, scale=scale)
                    free[q % 2] = act.tick(ins)
            return free

        with ExitStack() as c0:
            xnT = sb("xnT", [P, T], c=c0)
            valL = sb("values", [P, NT, H0, VW], c=c0)
            wv = sb("wv", [P, P], c=c0)
            bv = sb("bv", [P, P], c=c0)
            wp = sb("wp", [P, P], c=c0)
            bp = sb("bp", [P, P], c=c0)
            causal = sb("causal", [P, P], BF16, c=c0)
            nmaxL = sb("nmaxL", [P, H0, 24], c=c0)
            oL = sb("oL", [P, H0, 24, VW], c=c0)
            wv_in = load(wv[:], d["wv"], "wv")
            bv_in = load(bv[:], d["bv"].partition_broadcast(P), "bv")
            causal32 = sb("causal32", [P, P], c=c0)
            e = load(causal32[:], d["causal"], "causal")
            dve.wait(e)
            causal_in = dve.tick(V.tensor_copy(causal[:], causal32[:]))
            wp_in = load(wp[:], d["wp"], "wp")
            bp_in = load(bp[:], d["bp"].partition_broadcast(P), "bp")
            with ExitStack() as cm:
                wg = sb("wg", [P, NE], c=cm)
                we = sb("we", [P, NE * P], c=cm)
                lower = sb("lower", [P, NE, NE], c=cm)
                wg_in = load(wg[:], d["wg"], "wg")
                we_in = load(we[:].rearrange("p (e m) -> p e m", e=NE), d["we"].rearrange("e d m -> d e m"), "we")
                lower_in = load(lower[:], d["lower"].partition_broadcast(P), "lower")
                gate = sb("gate", [P, NT, NE], c=cm)
                g1 = sb("g1", [P, NT], c=cm)
                g2 = sb("g2", [P, NT, NE], c=cm)
                cmp1 = sb("cmp1", [P, NT, NE, NE], c=cm)
                cmp2 = sb("cmp2", [P, NT, NE, NE], c=cm)
                xe = sb("xe", [P, 2, NE, P], c=cm)

                e = layer_norm(p, x0, xn[:], st[:], [x_in], acc[:])
                xnT_ready = transpose_tiles(xn, xnT, [e])
                ones_set = pool.tick(G.memset(valL[:, :, :, DV0], 1.0))

                free = [None, None]
                for q in range(4):
                    bank = ps[:, 2 + q % 2, :]
                    pe.wait(wv_in, *xnT_ready, free[q % 2])
                    for c in range(4):
                        t = 4 * q + c
                        mm = TE.matmul(bank[:, c * P:(c + 1) * P], xnT[:, t * P:(t + 1) * P], wv[:], start=True, stop=True)
                    done = pe.tick(mm)
                    dve.wait(done, bv_in)
                    for c in range(4):
                        t = 4 * q + c
                        ins = V.tensor_tensor(valL[:, t, :, 0:DV0], bank[:, c * P:(c + 1) * P].rearrange("p (h v) -> p h v", h=H0),
                                              bv[:].rearrange("p (h v) -> p h v", h=H0), ALU.add)
                    free[q % 2] = dve.tick(ins)

                glog = ps[:, 4, 0:NT * NE].rearrange("p (t e) -> p t e", e=NE)
                pe.wait(wg_in)
                for t in range(NT):
                    mm = TE.matmul(glog[:, t, :], xnT[:, t * P:(t + 1) * P], wg[:], start=True, stop=True)
                done = pe.tick(mm)
                dve.wait(done)
                e = dve.tick(V.tensor_reduce(g1[:], glog, X_AXIS, ALU.max))
                dve.wait(e)
                e = dve.tick(V.tensor_tensor(g2[:], glog, bcast(g1[:], 2, NE), ALU.subtract))
                act.wait(e)
                e = act.tick(A.activation(g2[:], g2[:], ACT.Exp))
                dve.wait(e)
                e = dve.tick(V.tensor_reduce(g1[:], g2[:], X_AXIS, ALU.add))
                dve.wait(e)
                e = dve.tick(V.reciprocal(g1[:], g1[:]))
                dve.wait(e)
                e = dve.tick(V.tensor_tensor(gate[:], g2[:], bcast(g1[:], 2, NE), ALU.mult))
                mine, other = bcast(gate[:], 3, NE), bcast(gate[:], 2, NE)
                dve.wait(e, lower_in)
                V.tensor_tensor(cmp1[:], other, mine, ALU.is_gt)
                e = dve.tick(V.tensor_tensor(cmp2[:], other, mine, ALU.is_equal))
                dve.wait(e)
                e = dve.tick(V.tensor_tensor(cmp2[:], cmp2[:], bcast(lower[:], 1, NT), ALU.mult))
                dve.wait(e)
                e = dve.tick(V.tensor_tensor(cmp1[:], cmp1[:], cmp2[:], ALU.add))
                dve.wait(e)
                e = dve.tick(V.tensor_reduce(g2[:], cmp1[:], X_AXIS, ALU.add))
                dve.wait(e)
                e = dve.tick(V.tensor_scalar(g2[:], g2[:], 1.5, None, ALU.is_lt))
                dve.wait(e)
                e = dve.tick(V.tensor_tensor(gate[:], gate[:], g2[:], ALU.mult))
                dve.wait(e)
                e = dve.tick(V.tensor_reduce(g1[:], gate[:], X_AXIS, ALU.add))
                dve.wait(e)
                e = dve.tick(V.tensor_scalar(g1[:], g1[:], 1e-9, None, ALU.add))
                dve.wait(e)
                e = dve.tick(V.reciprocal(g1[:], g1[:]))
                dve.wait(e)
                gate_ready = dve.tick(V.tensor_tensor(gate[:], gate[:], bcast(g1[:], 2, NE), ALU.mult))
                free, pend = [None, None], [None, None]
                for t in range(NT):
                    b = t % 2
                    bank = ps[:, 2 * b:2 * b + 2, :]
                    pe.wait(we_in, free[b], dve.now())
                    for g in range(2):
                        mm = TE.matmul(bank[:, g, :], xnT[:, t * P:(t + 1) * P], we[:, g * 512:(g + 1) * 512], start=True, stop=True)
                    done = pe.tick(mm)
                    dve.wait(done, gate_ready, pend[b])
                    for g in range(2):
                        ins = V.tensor_tensor(xe[:, b, 4 * g:4 * g + 4, :], bank[:, g, :].rearrange("p (e m) -> p e m", e=4),
                                              bcast(gate[:, t, 4 * g:4 * g + 4], 2, P), ALU.mult)
                    free[b] = dve.tick(ins)
                    dve.wait(free[b])
                    e = dve.tick(V.tensor_reduce(acc[:, t, :], xe[:, b, :, :].rearrange("p e m -> p m e"), X_AXIS, ALU.add))
                    pool.wait(e)
                    pend[b] = pool.tick(G.tensor_tensor(acc[:, t, :], acc[:, t, :], x0[:, t, :], ALU.add))
                p.meet()

            with ExitStack() as ca:
                wh = sb("wh", [P, 2, 2 * P], c=ca)
                bh = sb("bh", [P, 2, 2], c=ca)
                bqs = sb("bqs", [P, 2], c=ca)
                kq = sb("kq", [P, 2, 2, T], c=ca)
                prob = sb("prob", [P, 2, KB], c=ca)
                probT = sb("probT", [P, 2, 2, 512], c=ca)
                nmx = sb("nmx", [P, 2, 24], c=ca)
                vb = sb("vb", [P, 2, NT, 32], c=ca)
                oT = sb("ot", [P, 2, P], c=ca)
                oh = sb("oh", [P, 2, 24, VW], c=ca)
                pick = sb("pick", [P, VW], c=ca)
                pick_in = load(pick[:], d["pick"], "pick")
                vb_zero = pool.tick(G.memset(vb[:], 0.0))
                w_in = [p.dma(f"wh{b}") for b in range(2)]
                units = [(g, 0, (g + 1) * P) for g in range(NT // 2)]
                for g in range(NT // 2, NT):
                    units += [(g, 0, KB), (g, KB, (g + 1) * P - KB)]

                NU = len(units)
                st0 = dict.fromkeys([n + str(b) + str(r) for n in ("turned", "probT") for b in range(2) for r in range(2)] +
                                    [n + str(b) for n in ("s", "prob", "pt", "kept", "w", "bias", "kq", "e", "vb", "vb_used", "x", "xs", "ot", "ot_used", "oh") for b in range(2)])

                def fetch(ev, b, head):
                    sp.wait(ev["kq%d" % b], ev["bias%d" % b])
                    w_in[b].tick(S.dma_start(wh[:, b, :], d["wkq"][head, :, :].rearrange("a d e -> d (a e)")))
                    ev["w%d" % b] = w_in[b].tick(S.dma_start(bh[:, b, :], d["bkq"][head, :, :].rearrange("a d e -> d (a e)")))

                def project(ev, b, n):
                    w, ch = n % 2, n // 2
                    if n == 0:
                        dve.wait(ev["w%d" % b])
                        ev["bias%d" % b] = dve.tick(V.tensor_scalar(bqs[:, b:b + 1], bh[:, b, 1:2], P ** -0.5, None, ALU.mult))
                    pe.wait(ev["w%d" % b], ev["pt1"])
                    done = pe.tick(TE.matmul(ps[:, 5, :], wh[:, b, w * P:(w + 1) * P], xnT[:, ch * 512:(ch + 1) * 512], start=True, stop=True))
                    to = kq[:, b, w, ch * 512:(ch + 1) * 512]
                    dve.wait(done, ev["bias%d" % b])
                    if w:
                        ins = V.tensor_scalar(to, ps[:, 5, :], P ** -0.5, bqs[:, b:b + 1], ALU.mult, ALU.add)
                    else:
                        ins = V.tensor_scalar(to, ps[:, 5, :], bh[:, b, 0:1], None, ALU.add)
                    ev["pt1"] = ev["kq%d" % b] = dve.tick(ins)

                def scores(ev, b, u):
                    g, k0, nk = units[u]
                    s = u % 2
                    pe.wait(ev["s%d" % s], ev["kq%d" % b])
                    diag = k0 + nk == (g + 1) * P
                    for o in range(0, nk, 512):
                        w = min(512, nk - o)
                        mm = TE.matmul(ps[:, 2 * s + o // 512, 0:w], kq[:, b, 1, g * P:(g + 1) * P], kq[:, b, 0, k0 + o:k0 + o + w],
                                       start=True, stop=not (o + w == nk and diag), skip_group_check=True)
                    if diag:
                        j, o = (nk - P) // 512, (nk - P) % 512
                        mm = TE.matmul(ps[:, 2 * s + j, o:o + P], identb[:], causal[:], start=False, stop=True, skip_group_check=True)
                    done = pe.tick(mm)
                    sc = ps[:, 2 * s:2 * s + 2, :].rearrange("p a b -> p (a b)")[:, 0:nk]
                    dve.wait(done, ev["kept%d" % b])
                    e = dve.tick(V.tensor_reduce(nmx[:, b, u:u + 1], sc, X_AXIS, ALU.max, negate=True))
                    act.wait(e, ev["prob%d" % s])
                    ev["s%d" % s] = ev["e%d" % s] = act.tick(A.activation(prob[:, s, 0:nk], sc, ACT.Exp, bias=nmx[:, b, u:u + 1]))

                def turn_probs(ev, b, u, r):
                    g, k0, nk = units[u]
                    s, m = u % 2, min(4, nk // P - 4 * r)
                    pe.wait(ev["e%d" % s], ev["pt%d" % r])
                    for c in range(m):
                        mm = TE.transpose(ps[:, 4 + r, c * P:(c + 1) * P], prob[:, s, (4 * r + c) * P:(4 * r + c + 1) * P], ident[:])
                    done = ev["prob%d" % s] = pe.tick(mm)
                    eng = (act, dve)[r]
                    eng.wait(done, ev[f"probT{s}{r}"])
                    if r:
                        ins = V.tensor_copy(probT[:, s, r, 0:m * P], ps[:, 4 + r, 0:m * P])
                    else:
                        ins = A.activation(probT[:, s, r, 0:m * P], ps[:, 4 + r, 0:m * P], ACT.Copy)
                    ev["pt%d" % r] = ev[f"turned{s}{r}"] = eng.tick(ins)

                def take_values(ev, b, head):
                    pool.wait(ev["vb_used%d" % b])
                    ev["vb%d" % b] = pool.tick(G.tensor_copy(vb[:, b, :, 0:VW], valL[:, :, head, :].rearrange("p t h v -> p t (h v)")))

                def values(ev, b, u):
                    g, k0, nk = units[u]
                    s, n = u % 2, nk // P
                    pe.wait(ev["vb%d" % b], ev["x%d" % s])
                    for j in range(n):
                        r, c = j // 4, j % 4
                        if c == 0:
                            pe.wait(ev[f"turned{s}{r}"])
                        mm = TE.matmul(ps[32 * c:32 * c + 32, 6 + s, 0:P], vb[:, b, k0 // P + j, :], probT[:, s, r, c * P:(c + 1) * P],
                                       start=r == 0, stop=j + 4 >= n, skip_group_check=True)
                        if c == 3 or j == n - 1:
                            done = ev[f"probT{s}{r}"] = pe.tick(mm)
                    ev["vb_used%d" % b] = done
                    rows = 32 * min(4, n)
                    act.wait(done, ev["ot_used%d" % s])
                    ev["ot%d" % s] = act.tick(A.activation(oT[0:rows, s, :], ps[0:rows, 6 + s, 0:P], ACT.Copy))

                def gather(ev, b, u):
                    s, rows = u % 2, 32 * min(4, units[u][2] // P)
                    pe.wait(ev["ot%d" % s])
                    done = ev["ot_used%d" % s] = pe.tick(TE.matmul(ps[:, 6 + s, P:P + VW], oT[0:rows, s, :], pick[0:rows, :],
                                                                   start=True, stop=True, skip_group_check=True))
                    dve.wait(done, ev["oh%d" % b])
                    ev["x%d" % s] = dve.tick(V.tensor_copy(oh[:, b, u, :], ps[:, 6 + s, P:P + VW]))

                def close(ev, b, head):
                    gather(ev, b, NU - 1)
                    dve.wait(dve.now())
                    ev["oh%d" % b] = dve.tick(V.tensor_copy(oL[:, head, :, :].rearrange("p h u v -> p (h u) v"), oh[:, b, :, :]))
                    ev["kept%d" % b] = dve.tick(V.tensor_copy(nmaxL[:, head, :], nmx[:, b, :]))

                def two_heads(i, ev, more):
                    for b in range(2):
                        ahead = more or b == 0
                        none = isinstance(i, int) and i == 0 and b == 0
                        if ahead:
                            fetch(ev, 1 - b, ds(2 * i + b + 1, 1))
                        for u in range(NU):
                            for r in range(-(-units[u][2] // 512)):
                                turn_probs(ev, b, u, r)
                            if u + 2 < NU:
                                scores(ev, b, u + 2)
                            elif ahead:
                                scores(ev, 1 - b, u + 2 - NU)
                            if u >= 2:
                                gather(ev, b, u - 2)
                            elif not none and u == 1:
                                close(ev, 1 - b, ds(2 * i + b - 1, 1))
                            elif not none:
                                gather(ev, 1 - b, NU - 2)
                                values(ev, 1 - b, NU - 1)
                            if u:
                                values(ev, b, u - 1)
                            if u == 2 and ahead:
                                take_values(ev, 1 - b, ds(2 * i + b + 1, 1))
                            if ahead and u >= 6 and u % 2 == 0 and (u - 6) // 2 < 8:
                                project(ev, 1 - b, (u - 6) // 2)

                pool.wait(vb_zero)
                pe.wait(pick_in)
                fetch(st0, 0, ds(0, 1))
                take_values(st0, 0, ds(0, 1))
                for n in range(8):
                    project(st0, 0, n)
                for u in range(2):
                    scores(st0, 0, u)
                p.pipeline(H0 // 2, two_heads, st0, lead=2)
                gather(st0, 1, NU - 2)
                values(st0, 1, NU - 1)
                close(st0, 1, ds(H0 - 1, 1))
                p.meet()

            with ExitStack() as cj:
                sa = sb("sa", [P, NT, H0, DV0], c=cj)
                saT = sb("saT", [P, T], c=cj)
                HN = NT // 2
                wgt = sb("wgt", [P, 2, H0, HN], c=cj)
                mn = sb("mn", [P, H0, HN], c=cj)
                o2 = sb("o2", [P, 2, H0, HN, VW], c=cj)
                rec = sb("rec", [P, H0, HN], c=cj)
                nm = [nmaxL[:, :, HN + j::2] for j in range(2)]
                ov = [oL[:, :, HN + j::2, :] for j in range(2)]
                e = dve.tick(V.tensor_tensor(mn[:], nm[0], nm[1], ALU.min))
                dve.wait(e)
                for j in range(2):
                    e = dve.tick(V.tensor_tensor(wgt[:, j], mn[:], nm[j], ALU.subtract))
                act.wait(e)
                e = act.tick(A.activation(wgt[:], wgt[:], ACT.Exp))
                dve.wait(e)
                for j in range(2):
                    e = dve.tick(V.tensor_tensor(o2[:, j], ov[j], bcast(wgt[:, j], 3, VW), ALU.mult))
                dve.wait(e)
                e = dve.tick(V.tensor_tensor(o2[:, 0], o2[:, 0], o2[:, 1], ALU.add))
                dve.wait(e)
                for half, o in ((0, oL[:, :, 0:HN, :]), (1, o2[:, 0])):
                    e = dve.tick(V.reciprocal(rec[:], o[:, :, :, DV0]))
                    dve.wait(e)
                    e = dve.tick(V.tensor_tensor(sa[:, half * HN:(half + 1) * HN, :, :].rearrange("p g h v -> p h g v"), o[:, :, :, 0:DV0],
                                                 bcast(rec[:], 3, DV0), ALU.mult))
                    dve.wait(e)
                saT_ready = transpose_tiles(sa[:].rearrange("p t h v -> p t (h v)"), saT, [e])
                pe.wait(*saT_ready, wp_in)
                for t in range(NT):
                    mm = TE.matmul(ps[:, 2 + t // 4, (t % 4) * P:(t % 4 + 1) * P], saT[:, t * P:(t + 1) * P], wp[:], start=True, stop=True, skip_group_check=True)
                done = pe.tick(mm)
                dve.wait(done, bp_in, pool.now())
                e = dve.tick(V.tensor_tensor(acc[:].rearrange("p (q c) d -> p q (c d)", q=4), acc[:].rearrange("p (q c) d -> p q (c d)", q=4), ps[:, 2:6, :], ALU.add))
                dve.wait(e)
                e = dve.tick(V.tensor_tensor(acc[:], acc[:], bcast(bp[:], 1, NT), ALU.add))
                e = layer_norm(p, acc[:], xn[:], st[:], [e], saT[:].rearrange("p (t d) -> p t d", d=P))
                p.meet()

        mamba(p, d, sb, ps, load, acc, xn, st, ident, transpose_tiles)
        transformer(p, d, sb, ps, load, acc, xn, xs, ident, identb)

        S.dma_start(out.rearrange("(t p) d -> p t d", p=P), acc[:]).then_inc(outs.sem, 16)
        S.wait_ge(outs.sem, 16)


def mamba(p, d, sb, ps, load, acc, xn, st, ident, transpose_tiles):
    pe, dve, act, pool, sp = p.engines
    TE, V, A, G, S = p.nc.tensor, p.nc.vector, p.nc.scalar, p.nc.gpsimd, p.nc.sync
    PAD = KC - 1
    with ExitStack() as c:
        u = sb("mu", [P, ET, T], c=c)
        z = sb("mz", [P, ET, T], c=c)
        y = sb("my", [P, ET, T], c=c)
        xd = sb("xd", [RX, T], c=c)
        win = sb("win", [P, 4 * P], c=c)
        wx = sb("wx", [P, ET, RX], c=c)
        wdt = sb("wdt", [R, ET * P], c=c)
        wout = sb("wout", [P, ET, P], c=c)
        taps = sb("taps", [P, ET, KC], c=c)
        alog = sb("alog", [P, ET, NS], c=c)
        cols = sb("cols", [P, 12], c=c)
        bout = sb("bout", [P, P], c=c)
        gam, bet, bin_, cb, bdt, dpar = (cols[:, a:b] for a, b in ((0, 1), (1, 2), (2, 6), (6, 8), (8, 10), (10, 12)))
        win_in = load(win[:], d["win"], "win")
        cols_in = load(cols[:], d["cols"], "cols")
        taps_in = load(taps[:], d["taps"].rearrange("(a p) k -> p a k", p=P), "taps")
        wx_in = load(wx[:], d["wx"].rearrange("(a p) r -> p a r", p=P), "wx")
        wdt_in = load(wdt[:], d["wdt"], "wdt")
        alog_in = load(alog[:], d["alog"].rearrange("(a p) n -> p a n", p=P), "alog")
        wout_in = load(wout[:], d["wout"].rearrange("(a p) n -> p a n", p=P), "wout")
        bout_in = load(bout[:], d["bout"].partition_broadcast(P), "bout")
        act.wait(alog_in)
        a_exp = act.tick(A.activation(alog[:], alog[:], ACT.Exp))
        pool.wait(a_exp)
        neg_a = pool.tick(G.tensor_scalar(alog[:], alog[:], -1.0, None, ALU.mult))
        with ExitStack() as cx:
            xT = sb("mxT", [P, T], c=cx)
            xp = sb("mxp", [P, ET, PAD + T], c=cx)
            hat = y[:, 0, :].rearrange("p (t d) -> p t d", d=P)
            e = layer_norm(p, xn[:], hat, st[:], [], y[:, 1, :].rearrange("p (t d) -> p t d", d=P))
            act.wait(cols_in)
            xT_ready = transpose_tiles(hat, xT, [e], scale=gam, bias=bet)
            padded = dve.tick(V.memset(xp[:, :, 0:PAD], 0.0))
            diag = sb("diag", [P, KC, P], c=cx)
            pool.wait(taps_in)
            for k in range(KC):
                diag_ready = pool.tick(G.tensor_scalar(diag[:, k, :], ident[:], taps[:, 1, k:k + 1], None, ALU.mult))
            pool.wait(bout_in)
            e = pool.tick(G.tensor_tensor(acc[:], acc[:], xn[:], ALU.add))
            pool.wait(e)
            pool.tick(G.tensor_tensor(acc[:], acc[:], bcast(bout[:], 1, NT), ALU.add))
            free = [None] * 4
            n = 0

            def project_in(m):
                nonlocal n
                for q in range(4):
                    bank = ps[:, 4 + n % 4, :]
                    pe.wait(free[n % 4])
                    done = pe.tick(TE.matmul(bank, win[:, m * P:(m + 1) * P], xT[:, q * 512:(q + 1) * 512], start=True, stop=True))
                    act.wait(done)
                    if m >= 2:
                        ins = A.activation(z[:, m - 2, q * 512:(q + 1) * 512], bank, ACT.Silu, bias=bin_[:, m:m + 1])
                    else:
                        ins = A.activation(xp[:, m, PAD + q * 512:PAD + (q + 1) * 512], bank, ACT.Identity, bias=bin_[:, m:m + 1])
                    free[n % 4] = act.tick(ins)
                    n += 1
                return free[(n - 1) % 4]

            pe.wait(win_in, *xT_ready)
            in_ready = [project_in(0), project_in(1)]
            pe.wait(in_ready[1], padded, diag_ready)
            conv_done = []
            for q in range(1, 4):
                for k in range(KC):
                    mm = TE.matmul(ps[:, q, :], diag[:, k, :], xp[:, 1, q * 512 + k:q * 512 + k + 512], start=k == 0, stop=k == KC - 1)
                conv_done.append(pe.tick(mm))
            parts = [(0, 0, 1024), (0, 1024, 1024), (1, 0, 512)]
            done = [None] * 3
            dve.wait(in_ready[0], padded, taps_in)
            for k in range(KC):
                for i, (a, o, w) in enumerate(parts):
                    if k == 0:
                        dve.wait(in_ready[a])
                        done[i] = dve.tick(V.tensor_scalar(u[:, a, o:o + w], xp[:, a, o:o + w], taps[:, a, 0:1], cb[:, a:a + 1], ALU.mult, ALU.add))
                    else:
                        dve.wait(done[i])
                        done[i] = dve.tick(V.scalar_tensor_tensor(u[:, a, o:o + w], xp[:, a, o + k:o + k + w], taps[:, a, k:k + 1], u[:, a, o:o + w],
                                                                  ALU.mult, ALU.add))
            project_in(2)
            project_in(3)
            for q in range(1, 4):
                act.wait(conv_done[q - 1])
                act.tick(A.activation(u[:, 1, q * 512:(q + 1) * 512], ps[:, q, :], ACT.Silu, bias=cb[:, 1:2]))
            for i in (0, 2, 1):
                a, o, w = parts[i]
                act.wait(done[i])
                act.tick(A.activation(u[:, a, o:o + w], u[:, a, o:o + w], ACT.Silu))
            p.meet()
        pe.wait(wx_in)
        for q in range(4):
            for a in range(ET):
                mm = TE.matmul(ps[0:RX, q, :], wx[:, a, :], u[:, a, q * 512:(q + 1) * 512], start=a == 0, stop=a == ET - 1)
            done = pe.tick(mm)
            eng = (act, dve)[q % 2]
            eng.wait(done)
            to = xd[:, q * 512:(q + 1) * 512]
            eng.tick(V.tensor_copy(to, ps[0:RX, q, :]) if q % 2 else A.activation(to, ps[0:RX, q, :], ACT.Copy))
        for a in range(ET):
            pool.tick(G.tensor_scalar(y[:, a, :], u[:, a, :], dpar[:, a:a + 1], None, ALU.mult))
        delta = sb("delta", [P, ET, T], c=c)
        du = sb("du", [P, ET, T], c=c)
        dec = sb("dec", [P, ET, T], c=c)
        inp = sb("inp", [P, ET, T], c=c)
        parts3 = sb("parts3", [RX, 3, T], BF16, c=c)
        pe.wait(wdt_in, act.now(), dve.now())
        for a in range(ET):
            for q in range(4):
                mm = TE.matmul(ps[:, 4 * (1 - a) + q, :], wdt[:, a * P:(a + 1) * P], xd[0:R, q * 512:(q + 1) * 512], start=True, stop=True)
            done = pe.tick(mm)
            v = ps[:, 4 * (1 - a):4 * (1 - a) + 4, :].rearrange("p a b -> p (a b)")
            act.wait(done)
            e = act.tick(A.activation(dec[:, a, :], v, ACT.Abs, bias=bdt[:, a:a + 1]))
            dve.wait(e)
            dve.tick(V.tensor_scalar(delta[:, a, :], v, bdt[:, a:a + 1], 0.0, ALU.add, ALU.max))
        rest = inp[0:RX, 0, :]
        dve.wait(act.now())
        e = dve.tick(V.tensor_copy(parts3[:, 0, :], xd[:]))
        dve.wait(e)
        e = dve.tick(V.tensor_tensor(rest, xd[:], parts3[:, 0, :], ALU.subtract))
        dve.wait(e)
        e = dve.tick(V.tensor_copy(parts3[:, 1, :], rest))
        dve.wait(e)
        e = dve.tick(V.tensor_tensor(rest, rest, parts3[:, 1, :], ALU.subtract))
        dve.wait(e)
        e = dve.tick(V.tensor_copy(parts3[:, 2, :], rest))
        bc = p.nc.dram_tensor("bc_scratch", [2 * NS, 3, T], BF16).ap()
        bc_saved = load(bc, parts3[R:RX, :, :], "bc_save", [e])
        act.wait(act.now())
        e = act.tick(A.activation(dec[:], dec[:], ACT.Exp, scale=-1.0))
        act.wait(e)
        for a in range(ET):
            e = act.tick(A.activation(dec[:, a, :], dec[:, a, :], ACT.Ln, bias=1.0))
            dve.wait(e)
            e = dve.tick(V.tensor_tensor(delta[:, a, :], delta[:, a, :], dec[:, a, :], ALU.add))
            dve.wait(e)
            dve.tick(V.tensor_tensor(du[:, a, :], delta[:, a, :], u[:, a, :], ALU.mult))
        rows = sb("rows", [3, 2, T], BF16, c=c)
        ones = sb("ones", [3, P], BF16, c=c)
        ac = sb("ac", [P, ET], c=c)
        pool.tick(G.memset(ones[:], 1.0))
        bc_in = p.dma("bc")
        flat_b, flat_c = (ps[:, 4 * w:4 * w + 4, :].rearrange("p a b -> p (a b)") for w in range(2))
        st0 = dict.fromkeys(["rows", "ac", "b", "c", "c_used", "rows_used"] + [k + str(a) for k in ("inp", "dec", "y") for a in range(ET)])

        def fetch_rows(ev, n):
            sp.wait(ev["rows_used"])
            for w in range(2):
                ev["rows"] = bc_in.tick(S.dma_start(rows[:, w, :], bc[ds(w * NS + n, 1), :, :].rearrange("a c t -> c (a t)")))

        def spread(ev, w):
            pe.wait(ev["rows"], ev["inp1"] if w == 0 else ev["c_used"])
            for q in range(4):
                mm = TE.matmul(ps[:, 4 * w + q, :], ones[:], rows[:, w, q * 512:(q + 1) * 512], start=True, stop=True)
            ev["bc"[w]] = ev["rows_used"] = pe.tick(mm)

        def decay(ev, a):
            act.wait(ev["ac"], ev[f"y{a}"])
            ev[f"dec{a}"] = act.tick(A.activation(dec[:, a, :], delta[:, a, :], ACT.Exp, scale=ac[:, a:a + 1]))

        def rates(ev, n):
            dve.wait(ev["dec1"])
            ev["ac"] = dve.tick(V.tensor_copy(ac[:], alog[:, :, ds(n, 1)]))

        def state(n, ev, more):
            if more:
                fetch_rows(ev, n + 1)
            for a in range(ET):
                dve.wait(ev["b"], ev[f"y{a}"])
                ev[f"inp{a}"] = e = dve.tick(V.tensor_tensor(inp[:, a, :], du[:, a, :], flat_b, ALU.mult))
                dve.wait(e, ev[f"dec{a}"])
                e = dve.tick(V.tensor_tensor_scan(inp[:, a, :], dec[:, a, :], inp[:, a, :], 0.0, ALU.mult, ALU.add))
                dve.wait(e, ev["c"])
                ev["c_used"] = e = dve.tick(V.tensor_tensor(dec[:, a, :], inp[:, a, :], flat_c, ALU.mult))
                pool.wait(e, ev[f"y{a}"])
                ev[f"y{a}"] = pool.tick(G.tensor_tensor(y[:, a, :], y[:, a, :], dec[:, a, :], ALU.add))
                if more:
                    if a == 0:
                        rates(ev, n + 1)
                    decay(ev, a)
                    if a:
                        spread(ev, 0)
            if more:
                spread(ev, 1)

        sp.wait(bc_saved)
        p.meet()
        fetch_rows(st0, 0)
        rates(st0, 0)
        for a in range(ET):
            decay(st0, a)
        for w in range(2):
            spread(st0, w)
        p.pipeline(NS, state, st0, lead=1)
        for a in range(ET):
            dve.wait(st0[f"y{a}"])
            e = dve.tick(V.tensor_tensor(y[:, a, :], y[:, a, :], z[:, a, :], ALU.mult))
        pe.wait(e, wout_in)
        for t in range(NT):
            for a in range(ET):
                mm = TE.matmul(ps[:, t // 4, (t % 4) * P:(t % 4 + 1) * P], y[:, a, t * P:(t + 1) * P], wout[:, a, :],
                               start=a == 0, stop=a == ET - 1, skip_group_check=True)
        done = pe.tick(mm)
        flat = acc[:].rearrange("p (q c) d -> p q (c d)", q=4)
        dve.wait(done)
        dve.tick(V.tensor_tensor(flat, flat, ps[:, 0:4, :], ALU.add))
        p.meet()


def transformer(p, d, sb, ps, load, acc, xn, xs, ident, identb):
    pe, dve, act, pool, sp = p.engines
    TE, V, A, G, S = p.nc.tensor, p.nc.vector, p.nc.scalar, p.nc.gpsimd, p.nc.sync
    c = ExitStack()
    with c:
        ys = sb("ys", [P, NT + 1, P], c=c)
        wqkv = sb("wqkv", [P, 3 * INNER], c=c)
        wo = sb("wo", [P, INNER // P, P], c=c)
        w1 = sb("w1", [P, 2 * FI], c=c)
        w2 = sb("w2", [P, 3, P], c=c)
        colA = sb("colA", [P, 2 + 6], c=c)
        b2 = sb("b2", [P, P], c=c)
        qks = sb("qks", [P, 4, DH], c=c)
        rotary = sb("rotary", [P, 4, DH], c=c)
        tab = sb("tab", [P, 4, DH], c=c)
        turn = sb("turn", [P, P], c=c)
        band = sb("band", [P, 2, 2 * KW], BF16, c=c)
        band32 = sb("band32", [P, 2, 2 * KW], c=c)
        xc = sb("xc", [P, 2, P], c=c)
        xcT = sb("xcT", [P, 2, P], c=c)
        xf = sb("xf", [P, 2, P], c=c)
        xfT = sb("xfT", [P, 2 * P], c=c)
        half = sb("half", [P, 1], c=c)
        uc = sb("uc", [P, 2, 512], c=c)
        sq = sb("sq", [P, 2, 512], c=c)
        ra = sb("ra", [P, 2, 4, 512], c=c)
        rb = sb("rb", [P, 2, 512], c=c)
        ss = sb("ss", [P, 2, 4, 8], c=c)
        rn = sb("rn", [P, 2, 4, 8], c=c)
        qT = sb("qT", [P, 2, 8, P], c=c)
        kT = sb("kT", [P, 2, 8, KW], c=c)
        vs = sb("vs", [P, 2, H, DH + 1], c=c)
        vh = sb("vh", [WIN, 2, H, DH + 1], c=c)
        pr = sb("pr", [P, 2, 4, KW], c=c)
        prT = sb("prT", [P, 2, 512], c=c)
        phT = sb("phT", [WIN, 2, P], c=c)
        nmx = sb("nmxl", [P, 2, 4], c=c)
        rec = sb("recl", [P, 2, 4], c=c)
        on = sb("on", [P, 2, INNER], c=c)
        oT = sb("oT", [P, INNER], c=c)
        hv = sb("hv", [P, 3, 2 * P], c=c)
        bnst = sb("bnst", [P, 2, 6], c=c)
        mv = sb("mv", [P, 2, 2], c=c)
        rs = sb("rs", [P, 2], c=c)

        turn_in = load(turn[:], d["turn"], "turn")
        rotary_in = load(rotary[:], d["rotary"], "rotary")
        band_in = load(band32[:], d["band"], "band")
        wA, wO, wS = p.dma("wA"), p.dma("wO"), p.dma("wS")
        wB = p.dma("wB")
        xc_in = [p.dma("xc0"), p.dma("xc1")]
        xf_in = p.dma("xf")
        vh_in = [p.dma("vh0"), p.dma("vh1")]

        def shifted(c, to, src, t0, n):
            c.tick(S.dma_start(to[:, :, 0:DH], src[:, ds(t0 + 1, n), 0:DH]))
            c.tick(S.dma_start(to[1:P, :, DH:P], src[0:P - 1, ds(t0 + 1, n), DH:P]))
            return c.tick(S.dma_start(to[0:1, :, DH:P], src[P - 1:P, ds(t0, n), DH:P]))

        def new_events():
            return dict.fromkeys(["bank4", "bank5", "bank6", "bank7", "y", "x", "hv", "wqk", "wv", "wo", "tab", "wB", "xf", "xf_used", "rs", "xfT", "xfT_used", "hv_used"] + [n + str(r) for n in (
                "halo",
                "s", "exp", "xc", "xcT", "xc_used", "xcT_used", "uc", "uc_sq", "sq", "rb", "q_rows", "k_rows", "ra_used",
                "qT", "kT", "v", "v_used", "vh", "vh_used", "prob_used", "prT", "prT_used", "phT", "on", "on_used", "oT_used") for r in range(2)])

        ring = [0]

        def t_bank(ev):
            r = ring[0] = (ring[0] + 1) % 4
            pe.wait(ev[f"bank{4 + r}"])
            return f"bank{4 + r}", ps[:, 4 + r, :]

        def fetch_tile(ev, b, t):
            sp.wait(ev[f"xc_used{b}"], ev[f"xc{b}"])
            ev[f"xc{b}"] = shifted(xc_in[b], xc[:, b:b + 1, :], xs, t, 1)

        def prepare(ev, b):
            k, bank = t_bank(ev)
            pe.wait(ev[f"xc{b}"])
            done = ev[f"xc_used{b}"] = pe.tick(TE.transpose(bank[:, 0:P], xc[:, b, :], ident[:]))
            act.wait(done, ev[f"xcT_used{b}"])
            ev[k] = ev[f"xcT{b}"] = act.tick(A.activation(xcT[:, b, :], bank[:, 0:P], ACT.Copy))

        def project_v(ev, b, w):
            k, bank = t_bank(ev)
            done = ev[f"xcT_used{b}"] = pe.tick(TE.matmul(bank, xcT[:, b, :], wqkv[:, (4 + w) * 512:(5 + w) * 512], start=True, stop=True))
            act.wait(done, ev[f"v_used{b}"], ev[f"vh{1 - b}"])
            ev[k] = ev[f"v{b}"] = act.tick(A.activation(vs[:, b, w * 8:(w + 1) * 8, 0:DH], bank.rearrange("p (h d) -> p h d", d=DH), ACT.Copy))

        def project_qk(ev, b, w):
            r = w % 2
            k, bank = t_bank(ev)
            pe.wait(ev[f"xcT{b}"])
            done = pe.tick(TE.matmul(bank, xcT[:, b, :], wqkv[:, w * 512:(w + 1) * 512], start=True, stop=True))
            act.wait(done, ev[f"uc{r}"], ev[f"uc_sq{r}"])
            out = ev[k] = act.tick(A.activation(uc[:, r, :], bank, ACT.Copy))
            act.wait(out, ev[f"sq{r}"])
            squared = ev[f"uc_sq{r}"] = act.tick(A.activation(sq[:, r, :], uc[:, r, :], ACT.Square))
            heads, out_a, out_b = (x.rearrange("p (h d) -> p h d", d=DH) for x in (uc[:, r, :], ra[:, b, w, :], rb[:, r, :]))
            cos, sin = tab[:, w // 2 * 2, :], tab[:, w // 2 * 2 + 1, :]
            dve.wait(out, ev[f"ra_used{b}"], ev[f"rb{r}"])
            V.tensor_tensor(out_a, heads, bcast(cos, 1, 8), ALU.mult)
            V.tensor_tensor(out_b[:, :, 0:32], heads[:, :, 32:64], bcast(sin[:, 0:32], 1, 8), ALU.mult)
            turned = ev[f"uc{r}"] = dve.tick(V.tensor_tensor(out_b[:, :, 32:64], heads[:, :, 0:32], bcast(sin[:, 32:64], 1, 8), ALU.mult))
            dve.wait(squared)
            summed = ev[f"sq{r}"] = dve.tick(V.tensor_reduce(ss[:, b, w, :], sq[:, r, :].rearrange("p (h d) -> p h d", d=DH), X_AXIS, ALU.add))
            pool.wait(turned)
            ev[f"rb{r}"] = pool.tick(G.tensor_tensor(ra[:, b, w, :], ra[:, b, w, :], rb[:, r, :], ALU.add))
            pool.wait(summed)
            e = pool.tick(G.tensor_scalar(rn[:, b, w, :], ss[:, b, w, :], 1e-24, None, ALU.max))
            pool.wait(e)
            e = pool.tick(G.tensor_tensor(rn[:, b, w, :], rn[:, b, w, :], half[:].broadcast_to([P, 8]), ALU.pow))
            pool.wait(e, ev[f"rb{r}"])
            ev[("q_rows", "k_rows")[w // 2] + str(b)] = pool.tick(G.tensor_tensor(out_a, out_a, bcast(rn[:, b, w, :], 2, DH), ALU.mult))

        def turn_rows(ev, b, w):
            k, bank = t_bank(ev)
            pe.wait(ev[("q_rows", "k_rows")[w // 2] + str(b)])
            for j in range(4):
                mm = TE.transpose(bank[:, j * P:(j + 1) * P], ra[:, b, w, j * P:(j + 1) * P], ident[:])
            done = ev[f"ra_used{b}"] = pe.tick(mm)
            to = qT[:, b, 4 * w:4 * w + 4, :] if w < 2 else kT[:, b, 4 * w - 8:4 * w - 4, WIN:KW]
            act.wait(done)
            ev[k] = ev[("qT", "kT")[w // 2] + str(b)] = act.tick(A.activation(to, bank.rearrange("p (j n) -> p j n", n=P), ACT.Copy))

        def keys_before(ev, b):
            k, bank = t_bank(ev)
            pe.wait(ev[f"kT{1 - b}"])
            done = pe.tick(TE.matmul(bank[:, 0:8 * WIN], turn[:], kT[:, 1 - b, :, P:KW], start=True, stop=True))
            dve.wait(done)
            ev[k] = ev[f"halo{b}"] = dve.tick(V.tensor_copy(kT[:, b, :, 0:WIN], bank[:, 0:8 * WIN].rearrange("p (j n) -> p j n", n=WIN)))

        def values_before(ev, b):
            sp.wait(ev[f"v{1 - b}"], ev[f"vh_used{b}"])
            ev[f"vh{b}"] = vh_in[b].tick(S.dma_start(vh[:, b, :, :], vs[P - WIN:P, 1 - b, :, :]))

        def scores(ev, b, g, first):
            r = g % 2
            pe.wait(ev[f"s{r}"], ev[f"qT{b}"], ev[f"kT{b}"], ev[f"halo{b}"])
            for o in range(2):
                TE.matmul(ps[:, 2 * r + o, 0:2 * KW], identb[:], band[:, 0 if first else 1, :], start=True, stop=False, skip_group_check=True)
            for pair in range(2):
                for o in range(2):
                    j = 2 * g + pair
                    mm = TE.matmul(ps[:, 2 * r + o, pair * KW:(pair + 1) * KW], qT[o * DH:(o + 1) * DH, b, j, :], kT[o * DH:(o + 1) * DH, b, j, :],
                                   start=False, stop=pair == 1, skip_group_check=True)
            done = pe.tick(mm)
            sc = ps[:, 2 * r:2 * r + 2, 0:2 * KW].rearrange("p o (a n) -> p o a n", a=2)
            dve.wait(done, ev[f"exp{r}"])
            e = dve.tick(V.tensor_reduce(nmx[:, r, :].rearrange("p (o a) -> p o a", o=2), sc, X_AXIS, ALU.max, negate=True))
            act.wait(e, ev[f"prob_used{r}"], ev[f"phT{r}"])
            for j in range(4):
                ins = A.activation(pr[:, r, j, :], sc[:, j // 2, j % 2, :], ACT.Exp, bias=nmx[:, r, j:j + 1])
            ev[f"s{r}"] = ev[f"exp{r}"] = act.tick(ins)

        def turn_probs(ev, b, g):
            r = g % 2
            k, bank = t_bank(ev)
            pe.wait(ev[f"exp{r}"])
            for j in range(4):
                mm = TE.transpose(bank[:, j * P:(j + 1) * P], pr[:, r, j, WIN:KW], ident[:])
            done = ev[f"prob_used{r}"] = pe.tick(mm)
            dve.wait(done, ev[f"prT_used{r}"])
            ev[k] = ev[f"prT{r}"] = dve.tick(V.tensor_copy(prT[:, r, :], bank))
            ev[f"phT{r}"] = dve.tick(V.transpose(phT[:, r, :].rearrange("p (j n) -> p j n", j=4), pr[0:WIN, r, :, 0:WIN]))

        def values(ev, b, g):
            r = g % 2
            k, bank = t_bank(ev)
            pe.wait(ev[f"prT{r}"], ev[f"phT{r}"], ev[f"v{b}"], ev[f"vh{b}"])
            o_bank = bank[:, 0:4 * (DH + 1)]
            for j in range(4):
                TE.matmul(o_bank[:, j * (DH + 1):(j + 1) * (DH + 1)], prT[:, r, j * P:(j + 1) * P], vs[:, b, 4 * g + PERM[j], :],
                          start=j == 0, stop=False, skip_group_check=True)
            for j in range(4):
                mm = TE.matmul(o_bank[0:WIN, j * (DH + 1):(j + 1) * (DH + 1)], phT[:, r, j * WIN:(j + 1) * WIN], vh[:, b, 4 * g + PERM[j], :],
                               start=False, stop=j == 3, skip_group_check=True)
            done = ev[f"prT_used{r}"] = ev[f"v_used{b}"] = ev[f"vh_used{b}"] = pe.tick(mm)
            o4 = o_bank.rearrange("p (j d) -> p j d", j=4)
            dve.wait(done, ev[f"on_used{b}"])
            e = dve.tick(V.reciprocal(rec[:, r, :], o4[:, :, DH]))
            dve.wait(e)
            to = on[:, b, 4 * g * DH:4 * (g + 1) * DH].rearrange("p (a o d) -> p o a d", a=2, o=2)
            ev[k] = ev[f"on{b}"] = dve.tick(V.tensor_tensor(to, o4[:, :, 0:DH].rearrange("p (o a) d -> p o a d", o=2),
                                                            bcast(rec[:, r, :].rearrange("p (o a) -> p o a", o=2), 3, DH), ALU.mult))

        def turn_out(ev, b, w):
            k, bank = t_bank(ev)
            pe.wait(ev[f"on{b}"])
            for j in range(4):
                mm = TE.transpose(bank[:, j * P:(j + 1) * P], on[:, b, (4 * w + j) * P:(4 * w + j + 1) * P], ident[:])
            done = ev[f"on_used{b}"] = pe.tick(mm)
            act.wait(done, ev["oT_used0"])
            ev[k] = ev["oT_used1"] = act.tick(A.activation(oT[:, w * 512:(w + 1) * 512], bank, ACT.Copy))

        def finish(ev, t):
            k, bank = t_bank(ev)
            pe.wait(ev["oT_used1"], ev["wo"])
            for j in range(8):
                mm = TE.matmul(bank[:, 0:P], oT[:, j * P:(j + 1) * P], wo[:, j, :], start=j == 0, stop=j == 7)
            done = ev["oT_used0"] = pe.tick(mm)
            dve.wait(done)
            ev[k] = ev["y"] = dve.tick(V.tensor_tensor(ys[:, ds(t + 1, 1), :], xs[:, ds(t + 1, 1), :], bank[:, 0:P].unsqueeze(1), ALU.add))

        def load_qk(ev):
            sp.wait(pe.now(), dve.now())
            ev["wqk"] = wA.tick(S.dma_start(wqkv[:, 0:2 * INNER], d["lwqkv"][ds(now["next"], 1), :, 0:2 * INNER].rearrange("a p n -> p (a n)")))
            got = wS.tick(S.dma_start(qks[:].rearrange("p a b -> p (a b)"), d["qks"][ds(now["next"], 1)].rearrange("a n -> (a n)").partition_broadcast(P)))
            dve.wait(got)
            ev["tab"] = dve.tick(V.tensor_tensor(tab[:], rotary[:], qks[:], ALU.mult))

        def load_v(ev):
            sp.wait(pe.now())
            ev["wv"] = wA.tick(S.dma_start(wqkv[:, 2 * INNER:], d["lwqkv"][ds(now["next"], 1), :, 2 * INNER:].rearrange("a p n -> p (a n)")))

        def load_o(ev):
            sp.wait(pe.now())
            ev["wo"] = wO.tick(S.dma_start(wo[:], d["lwo"][ds(now["this"], 1)].rearrange("a (c p) n -> p (a c) n", p=P)))

        def load_forward(ev):
            sp.wait(pe.now(), act.now(), dve.now())
            wB.tick(S.dma_start(w1[:], d["lw1"][ds(now["this"], 1)].rearrange("a p n -> p (a n)")))
            for j, (o, w) in enumerate(FCH):
                wB.tick(S.dma_start(w2[0:w, j, :], d["lw2"][ds(now["this"], 1), o:o + w, :].rearrange("a p n -> p (a n)")))
            wB.tick(S.dma_start(colA[:], d["cols1"][ds(now["this"], 1)].rearrange("a p n -> p (a n)")))
            ev["wB"] = wB.tick(S.dma_start(b2[:], d["lb2"][ds(now["this"], 1)].rearrange("a n -> (a n)").partition_broadcast(P)))

        def start(ev, step):
            if step == 0:
                sp.wait(ev["x"])
                for b in range(2):
                    fetch_tile(ev, b, b)
                for b in range(2):
                    prepare(ev, b)
                fetch_tile(ev, 0, 2)
                values_before(ev, 0)
                pe.wait(ev["wqk"])
                dve.wait(ev["tab"])
                ev["tab"] = None
            if step < 2:
                for w in range(2):
                    project_qk(ev, 0, 2 * step + w)
            elif step == 2:
                project_qk(ev, 1, 0)
                pe.wait(ev["wv"])
                for w in range(2):
                    project_v(ev, 0, w)
            elif step == 3:
                for w in range(1, 4):
                    project_qk(ev, 1, w)
            elif step == 4:
                for w in range(4):
                    turn_rows(ev, 0, w)
            elif step == 5:
                keys_before(ev, 0)
            else:
                for g in range(2):
                    scores(ev, 0, g, True)
                pe.wait(ev["xc0"], ev["vh0"])

        def fetch_two(ev, i):
            sp.wait(ev["y"], ev["xf_used"])
            ev["xf"] = shifted(xf_in, xf[:], ys, 2 * i, 2)

        def measure(ev):
            dve.wait(ev["xf"])
            for t in range(2):
                e = dve.tick(V.bn_stats(bnst[:, t, :], xf[:, t, :]))
            dve.wait(e)
            dve.settle()
            for t in range(2):
                e = dve.tick(V.bn_aggr(mv[:, t, :], bnst[:, t, :]))
            pool.wait(e)
            e = pool.tick(G.tensor_scalar(rs[:], mv[:, :, 1], EPS, None, ALU.add))
            pool.wait(e)
            ev["rs"] = pool.tick(G.tensor_tensor(rs[:], rs[:], half[:].broadcast_to([P, 2]), ALU.pow))

        def normalise(ev):
            dve.wait(ev["rs"])
            for t in range(2):
                ev["xf"] = dve.tick(V.tensor_scalar(xf[:, t, :], xf[:, t, :], mv[:, t, 0:1], rs[:, t:t + 1], ALU.subtract, ALU.mult))

        def turn_normal(ev):
            k, bank = t_bank(ev)
            pe.wait(ev["xf"])
            for t in range(2):
                mm = TE.transpose(bank[:, t * P:(t + 1) * P], xf[:, t, :], ident[:])
            ev["xf_used"] = e = pe.tick(mm)
            act.wait(e, ev["xfT_used"], ev["wB"])
            ev[k] = ev["xfT"] = act.tick(A.activation(xfT[:], bank[:, 0:2 * P], ACT.Identity, bias=colA[:, 1:2], scale=colA[:, 0:1]))

        def feed_forward(ev):
            up = []
            for j, (o, w) in enumerate(FCH):
                k, bank = t_bank(ev)
                pe.wait(ev["xfT"], ev["wB"])
                TE.matmul(bank[0:w, 0:2 * P], w1[:, FI + o:FI + o + w], xfT[:], start=True, stop=True, skip_group_check=True)
                up.append((k, bank, pe.tick(TE.matmul(bank[0:w, 2 * P:4 * P], w1[:, o:o + w], xfT[:], start=True, stop=True, skip_group_check=True))))
            ev["xfT_used"] = up[-1][2]
            gated = []
            for (k, bank, e), (j, (o, w)) in zip(up, enumerate(FCH)):
                act.wait(e, ev["hv_used"])
                gated.append(act.tick(A.activation(hv[0:w, j, :], bank[0:w, 0:2 * P], ACT.Gelu, bias=colA[0:w, 2 + j:3 + j])))
            for (k, bank, e), (j, (o, w)), g in zip(up, enumerate(FCH), gated):
                dve.wait(g, ev["wB"])
                ev[k] = ev["hv"] = dve.tick(V.scalar_tensor_tensor(hv[0:w, j, :], bank[0:w, 2 * P:4 * P], colA[0:w, 5 + j:6 + j], hv[0:w, j, :], ALU.add, ALU.mult))

        def down(ev, i):
            k, bank = t_bank(ev)
            pe.wait(ev["hv"])
            for t in range(2):
                for j, (o, w) in enumerate(FCH):
                    mm = TE.matmul(bank[:, t * P:(t + 1) * P], hv[0:w, j, t * P:(t + 1) * P], w2[0:w, j, :], start=j == 0, stop=j == 2,
                                   skip_group_check=True)
            ev["hv_used"] = e = pe.tick(mm)
            to = xs[:, ds(2 * i + 1, 2), :]
            dve.wait(e, ev["xc0"], ev["xc1"])
            e = ev[k] = dve.tick(V.tensor_tensor(to, ys[:, ds(2 * i + 1, 2), :], bank[:, 0:2 * P].rearrange("p (t d) -> p t d", d=P), ALU.add))
            dve.wait(e)
            ev["x"] = dve.tick(V.tensor_tensor(to, to, bcast(b2[:], 1, 2), ALU.add))

        def two_tiles(i, ev, more):
            first = isinstance(i, int) and i == 0
            none = first and now["first"]
            pair = NT // 2 - 1 if first else i - 1
            if not more:
                load_qk(ev)
            for b in range(2):
                last = not more and b == 1
                for g in range(4):
                    turn_probs(ev, b, g)
                    if not (none and b == 0):
                        if g == 0:
                            for w in range(2):
                                turn_out(ev, 1 - b, w)
                        if g == 1:
                            finish(ev, NT - 1 if first and b == 0 else 2 * i + b - 1)
                            if first and b == 0:
                                load_o(ev)
                    if not none:
                        if (b, g) == (0, 1):
                            fetch_two(ev, pair)
                        if (b, g) == (0, 2):
                            measure(ev)
                        if (b, g) == (0, 3):
                            normalise(ev)
                        if (b, g) == (1, 0):
                            turn_normal(ev)
                        if (b, g) == (1, 1):
                            feed_forward(ev)
                        if (b, g) == (1, 3):
                            down(ev, pair)
                            if first:
                                load_forward(ev)
                    if g == 0 and more:
                        prepare(ev, b)
                        fetch_tile(ev, 1 - b, 2 * i + b + 3)
                    if g == 0 and not last:
                        values_before(ev, 1 - b)
                    if g < 2 and not last:
                        project_v(ev, 1 - b, g)
                    if g == 2 and not last:
                        keys_before(ev, 1 - b)
                    if more:
                        project_qk(ev, b, g)
                    elif b == 1:
                        start(ev, g)
                    elif g == 1:
                        load_v(ev)
                    if not last and g < 2:
                        turn_rows(ev, 1 - b, g)
                        turn_rows(ev, 1 - b, 2 + g)
                    if g < 2:
                        scores(ev, b, g + 2, first and b == 0)
                    elif not last:
                        scores(ev, 1 - b, g - 2, False)
                    values(ev, b, g)
            ring[0] = 0

        def layer(l, first, ev):
            now.update(this=l, next=(l + 1) % L, first=first)
            ring[0] = 0
            if first:
                for step in range(7):
                    start(ev, step)
            p.pipeline(NT // 2, two_tiles, ev, lead=2)
            for step in range(4, 7):
                start(ev, step)

        now = dict(this=0, next=0)
        ev = new_events()
        dve.wait(rotary_in)
        for weights in (load_qk, load_v, load_o, load_forward):
            weights(ev)
        dve.wait(band_in)
        dve.tick(V.tensor_copy(band[:], band32[:]))
        pool.tick(G.memset(ys[:, 0, :], 0.0))
        pool.tick(G.memset(half[:], -0.5))
        pool.tick(G.memset(vh[:], 0.0))
        dve.tick(V.memset(vs[:], 1.0))
        pool.tick(G.memset(kT[:], 0.0))
        pool.tick(G.memset(xc[:], 0.0))
        pool.tick(G.memset(xf[:], 0.0))
        dve.tick(V.tensor_copy(xs[:, 1:NT + 1, :], xn[:]))
        pe.wait(turn_in, band_in)
        p.meet()

        layer(0, True, ev)
        with p.loop(L - 1, **LAYER) as l:
            layer(l + 1, False, new_events())
        p.meet()
        ev = new_events()
        for w in range(2):
            turn_out(ev, 1, w)
        finish(ev, NT - 1)
        fetch_two(ev, NT // 2 - 1)
        measure(ev)
        normalise(ev)
        turn_normal(ev)
        feed_forward(ev)
        down(ev, NT // 2 - 1)
        sp.wait(xc_in[0].now(), xc_in[1].now())
        p.meet()
        dve.tick(V.tensor_tensor(acc[:], acc[:], xs[:, 1:NT + 1, :], ALU.add))
        p.meet()


LAYER = dict(pe=472, dve=569, act=368, pool=272, wA=2, wO=1, wS=1, wB=6, xc0=27, xc1=24, xf=24, vh0=8, vh1=8)


def constants():
    c = {"ident": np.eye(P, dtype=np.float32), }
    q, k = np.arange(P)[:, None], np.arange(P)[None, :]
    c["causal"] = np.where(k > q, -1e30, 0.0).astype(np.float32)
    c["lower"] = (np.arange(NE)[None, :] < np.arange(NE)[:, None]).astype(np.float32)
    half = np.arange(0, DH, 2, dtype=np.float64)
    freq = np.tile(1.0 / 10000.0 ** (half / DH), 2)
    base = np.tile((half + 0.4 * DH) / (1.4 * DH), 2)
    pos = np.arange(P, dtype=np.float64)[:, None] - P // 2
    scale = base[None, :] ** (pos / (WIN // 2))
    sign = np.where(np.arange(DH) < DH // 2, -1.0, 1.0)
    cos, sin = np.cos(pos * freq), np.sin(pos * freq) * sign
    c["rotary"] = np.stack([8 * cos * scale, 8 * sin * scale, cos / scale, sin / scale], 1).astype(np.float32)
    phi = -P * freq
    turn = np.zeros((2 * DH, 2 * DH))
    fac = base ** (P / (WIN // 2))
    for h in range(2):
        for f in range(DH):
            o = h * DH
            turn[o + f, o + f] = np.cos(phi[f]) * fac[f]
            turn[o + (f + DH // 2) % DH, o + f] = sign[f] * np.sin(phi[f]) * fac[f]
    c["pick"] = np.tile(np.eye(32, VW, dtype=np.float32), (4, 1))
    c["turn"] = turn.astype(np.float32)
    j = np.arange(KW)[None, :] - WIN
    keep = (j <= q) & (j >= q - WIN)
    rows = [np.where(keep & (j >= 0), 0.0, -1e30), np.where(keep, 0.0, -1e30)]
    c["band"] = np.stack([np.tile(r, (1, 2)) for r in rows], 1).astype(np.float32)
    return c


def kernel(**inputs):
    import concourse.bacc as bacc
    from concourse.bass_utils import run_bass_kernel_spmd

    a = {k: np.asarray(v) for k, v in inputs.items()}
    wkqv, bkqv = a["L0_attn_Wkqv"], a["L0_attn_bkqv"]
    host = constants()
    host.update({
        "x": a["L0_attn_x"][0],
        "wkq": wkqv[:, :, :2 * P], "bkq": bkqv[:, :2 * P].reshape(H0, 2, P).transpose(0, 2, 1),
        "wv": wkqv[:, :, 2 * P:].transpose(1, 0, 2).reshape(P, P), "bv": bkqv[:, 2 * P:].reshape(P),
        "wp": a["L0_attn_Wp"], "bp": a["L0_attn_bp"], "wg": a["L0_ffn_Wg"], "we": a["L0_ffn_We"],
    })
    col = lambda n: a["L1_attn_" + n].reshape(-1, P).T
    host.update({
        "win": a["L1_attn_W_in"].T, "wx": a["L1_attn_W_x"].T, "wdt": a["L1_attn_W_dt"].T, "wout": a["L1_attn_W_out"].T,
        "taps": a["L1_attn_conv_w"], "alog": a["L1_attn_A_log"], "bout": a["L1_attn_b_out"],
        "cols": np.concatenate([col(n) for n in ("gamma", "beta", "b_in", "conv_b", "b_dt", "D_param")], 1),
    })
    qs, ks = a["L1_ffn_q_scale"], a["L1_ffn_k_scale"]
    turned = lambda v: np.concatenate([v[:, DH // 2:], v[:, :DH // 2]], 1)
    b1 = np.zeros((L, P, 6), np.float32)
    for j, (o, w) in enumerate(FCH):
        b1[:, :w, j] = a["L1_ffn_b1"][:, FI + o:FI + o + w]
        b1[:, :w, 3 + j] = a["L1_ffn_b1"][:, o:o + w]
    host.update({
        "lwqkv": a["L1_ffn_Wqkv"], "lwo": a["L1_ffn_Wo"], "lw1": a["L1_ffn_W1"], "lw2": a["L1_ffn_W2"], "lb2": a["L1_ffn_b2"],
        "qks": np.concatenate([qs, turned(qs), ks, turned(ks)], 1),
        "cols1": np.concatenate([a["L1_ffn_ln_g"][:, :, None], a["L1_ffn_ln_b"][:, :, None], b1], 2),
    })
    nc = bacc.Bacc("TRN2", target_bir_lowering=False, num_devices=1)
    arrays, aps = {}, {}
    for name, v in host.items():
        v = np.ascontiguousarray(v)
        arrays[name + "_dram"] = v
        aps[name] = nc.dram_tensor(name + "_dram", v.shape, mybir.dt.from_np(v.dtype), kind="ExternalInput").ap()
    out = nc.dram_tensor("out_dram", (1, T, P), F32, kind="ExternalOutput").ap()
    build(nc, aps, out[0])
    return run_bass_kernel_spmd(nc, [arrays], core_ids=[0]).results[0]["out_dram"]
```
